# Optimizing a Trainium2 kernel written in Bass

```python
import numpy as np
import jax
import jax.numpy as jnp

def _softmax(x, axis=-1):
    return jax.nn.softmax(x, axis=axis)

def _gelu(x):
    return jax.nn.gelu(x, approximate=True)

def _silu(x):
    return jax.nn.silu(x)

def _sigmoid(x):
    return jax.nn.sigmoid(x)

def _layernorm(x, axis=-1, eps=1e-05):
    m = jnp.mean(x, axis=axis, keepdims=True)
    v = jnp.var(x, axis=axis, keepdims=True)
    return (x - m) / jnp.sqrt(v + eps)

def _scatter_add(tgt, idx, src, axis=0):
    return tgt.at[idx].add(src)

def _segment_sum(src, seg, n):
    return jax.ops.segment_sum(src, seg, n)
kernel_name = 'mk_lm_tower_d1_tok_ids768_r4_75cf07'

def setup_inputs(seed: int=0):
    np.random.seed(seed)
    _w = jnp.asarray

    def _rec_inputs():
        import jax
        import jax.numpy as jnp
        _rk = jax.random.key(seed)
        x = jax.random.randint(jax.random.fold_in(_rk, 1), (4, 512), 0, 128, jnp.int32)
        return x
    x = _rec_inputs()

    def _L0_tok_setup():
        import jax, jax.numpy as jnp
        import numpy as np
        D_MODEL = 192
        MAX_ROWS = 100
        MAX_COLS = 200
        NEWLINE_ID = 7
        ROW_DIM = D_MODEL // 2
        COL_DIM = D_MODEL - ROW_DIM

        def _compute_2d_positions(token_ids):
            B, S = token_ids.shape
            is_newline = (token_ids == NEWLINE_ID).astype(token_ids.dtype)
            rows_unshifted = jnp.cumsum(is_newline, axis=1)
            rows = jnp.concatenate([jnp.zeros((B, 1), dtype=token_ids.dtype), rows_unshifted[:, :-1]], axis=1)
            pos = jnp.broadcast_to(jnp.arange(S, dtype=token_ids.dtype)[None, :], (B, S))
            newline_pos = jnp.where(is_newline.astype(bool), pos, jnp.array(-1, dtype=token_ids.dtype))
            shifted = jnp.concatenate([jnp.full((B, 1), -1, dtype=token_ids.dtype), newline_pos[:, :-1]], axis=1)
            last_newline_before = jax.lax.cummax(shifted, axis=1)
            cols = pos - last_newline_before - 1
            return (rows, cols)
        key = jax.random.key(seed)
        k1, k2, k3 = jax.random.split(key, 3)
        token_ids = jax.random.randint(k1, (32, 2048), 0, 128, dtype=jnp.int64 if jax.config.jax_enable_x64 else jnp.int32)
        row_emb_W = 0.02 * jax.random.normal(k2, (MAX_ROWS, ROW_DIM), dtype=jnp.float32)
        col_emb_W = 0.02 * jax.random.normal(k3, (MAX_COLS, COL_DIM), dtype=jnp.float32)
        return {'token_ids': token_ids, 'row_emb_W': row_emb_W, 'col_emb_W': col_emb_W}
    _L0_tok_all = _L0_tok_setup()
    _L0_tok_in = {k: v for k, v in _L0_tok_all.items() if k in ('row_emb_W', 'col_emb_W')}
    del _L0_tok_all

    def _L0_attn_setup():
        import jax, jax.numpy as jnp
        import numpy as np
        B_, L_, D_ = (4, 512, 192)
        D_INNER = 2 * D_
        HEADDIM = 2 * D_
        NHEADS = D_INNER // HEADDIM
        D_STATE = 128
        D_CONV = 4
        CONV_DIM = D_INNER + 2 * D_STATE
        D_IN_PROJ = 2 * D_INNER + 2 * D_STATE + NHEADS
        D_FF = 4 * D_
        EPS = 1e-05

        def _rmsnorm(x, w):
            return x * jax.lax.rsqrt(jnp.mean(x * x, -1, keepdims=True) + EPS) * w

        def _causal_dwconv(xBC, w, b):
            xc = xBC.transpose(0, 2, 1)
            y = jax.lax.conv_general_dilated(xc, w[:, None, :], window_strides=(1,), padding=[(D_CONV - 1, 0)], feature_group_count=CONV_DIM)
            return (y + b[None, :, None]).transpose(0, 2, 1)

        def _ssd_scan(xh, dt, A, Bm, Cm):
            dA = jnp.exp(dt * A)
            dBx = jnp.einsum('blhp,bln,blh->blhpn', xh, Bm, dt)

            def step(h, inp):
                dA_t, dBx_t, C_t = inp
                h = h * dA_t[:, :, None, None] + dBx_t
                y = jnp.einsum('bhpn,bn->bhp', h, C_t)
                return (h, y)
            h0 = jnp.zeros((xh.shape[0], NHEADS, HEADDIM, D_STATE), xh.dtype)
            _, ys = jax.lax.scan(step, h0, (dA.transpose(1, 0, 2), dBx.transpose(1, 0, 2, 3, 4), Cm.transpose(1, 0, 2)))
            return ys.transpose(1, 0, 2, 3)

        def _mamba2(u, in_proj_W, conv_w, conv_b, dt_bias, A_log, D, ssm_norm_w, out_proj_W):
            zxbcdt = u @ in_proj_W
            z = zxbcdt[..., :D_INNER]
            xBC = zxbcdt[..., D_INNER:D_INNER + CONV_DIM]
            dt = jax.nn.softplus(zxbcdt[..., -NHEADS:] + dt_bias)
            xBC = jax.nn.silu(_causal_dwconv(xBC, conv_w, conv_b))
            xs = xBC[..., :D_INNER]
            Bm = xBC[..., D_INNER:D_INNER + D_STATE]
            Cm = xBC[..., D_INNER + D_STATE:]
            A = -jnp.exp(A_log)
            xh = xs.reshape(xs.shape[0], xs.shape[1], NHEADS, HEADDIM)
            y = _ssd_scan(xh, dt, A, Bm, Cm) + xh * D[None, None, :, None]
            y = y.reshape(y.shape[0], y.shape[1], D_INNER)
            y = _rmsnorm(y * jax.nn.silu(z), ssm_norm_w)
            return y @ out_proj_W
        key = jax.random.key(seed)
        ks = jax.random.split(key, 8)
        s = 0.02
        return {'x': jax.random.normal(ks[0], (B_, L_, D_), jnp.float32), 'norm1_w': jnp.ones((D_,), jnp.float32), 'in_proj_W': jax.random.normal(ks[1], (D_, D_IN_PROJ), jnp.float32) * s, 'conv_w': jax.random.normal(ks[2], (CONV_DIM, D_CONV), jnp.float32) * 0.1, 'conv_b': jnp.zeros((CONV_DIM,), jnp.float32), 'dt_bias': jax.random.normal(ks[3], (NHEADS,), jnp.float32) * 0.1, 'A_log': jnp.zeros((NHEADS,), jnp.float32), 'D': jnp.ones((NHEADS,), jnp.float32), 'ssm_norm_w': jnp.ones((D_INNER,), jnp.float32), 'out_proj_W': jax.random.normal(ks[4], (D_INNER, D_), jnp.float32) * s, 'norm2_w': jnp.ones((D_,), jnp.float32), 'mlp_W1': jax.random.normal(ks[5], (D_, D_FF), jnp.float32) * s, 'mlp_W2': jax.random.normal(ks[6], (D_FF, D_), jnp.float32) * s}
    _L0_attn_all = _L0_attn_setup()
    _L0_attn_in = {k: v for k, v in _L0_attn_all.items() if k in ('norm1_w', 'in_proj_W', 'conv_w', 'conv_b', 'dt_bias', 'A_log', 'D', 'ssm_norm_w', 'out_proj_W', 'norm2_w', 'mlp_W1', 'mlp_W2')}
    del _L0_attn_all

    def _L0_ffn_setup():
        import jax, jax.numpy as jnp
        import numpy as np
        B, T, E = (2, 256, 192)
        H = 768
        N_EXP = 4
        key = jax.random.key(seed)
        ks = jax.random.split(key, 8)
        s_e = 1.0 / np.sqrt(E)
        s_h = 1.0 / np.sqrt(H)
        return {'x': jax.random.normal(ks[0], (B, T, E), dtype=jnp.float32), 'Wg': jax.random.uniform(ks[1], (E, N_EXP), minval=-s_e, maxval=s_e, dtype=jnp.float32), 'bg': jax.random.uniform(ks[2], (N_EXP,), minval=-s_e, maxval=s_e, dtype=jnp.float32), 'W1': jax.random.uniform(ks[3], (N_EXP, E, H), minval=-s_e, maxval=s_e, dtype=jnp.float32), 'b1': jax.random.uniform(ks[4], (N_EXP, H), minval=-s_e, maxval=s_e, dtype=jnp.float32), 'W2': jax.random.uniform(ks[5], (N_EXP, H, E), minval=-s_h, maxval=s_h, dtype=jnp.float32), 'b2': jax.random.uniform(ks[6], (N_EXP, E), minval=-s_h, maxval=s_h, dtype=jnp.float32)}
    _L0_ffn_all = _L0_ffn_setup()
    _L0_ffn_in = {k: v for k, v in _L0_ffn_all.items() if k in ('Wg', 'bg', 'W1', 'b1', 'W2', 'b2')}
    del _L0_ffn_all
    return {'x': x, 'L0_tok_row_emb_W': _L0_tok_in['row_emb_W'], 'L0_tok_col_emb_W': _L0_tok_in['col_emb_W'], 'L0_attn_norm1_w': _L0_attn_in['norm1_w'], 'L0_attn_in_proj_W': _L0_attn_in['in_proj_W'], 'L0_attn_conv_w': _L0_attn_in['conv_w'], 'L0_attn_conv_b': _L0_attn_in['conv_b'], 'L0_attn_dt_bias': _L0_attn_in['dt_bias'], 'L0_attn_A_log': _L0_attn_in['A_log'], 'L0_attn_D': _L0_attn_in['D'], 'L0_attn_ssm_norm_w': _L0_attn_in['ssm_norm_w'], 'L0_attn_out_proj_W': _L0_attn_in['out_proj_W'], 'L0_attn_norm2_w': _L0_attn_in['norm2_w'], 'L0_attn_mlp_W1': _L0_attn_in['mlp_W1'], 'L0_attn_mlp_W2': _L0_attn_in['mlp_W2'], 'L0_ffn_Wg': _L0_ffn_in['Wg'], 'L0_ffn_bg': _L0_ffn_in['bg'], 'L0_ffn_W1': _L0_ffn_in['W1'], 'L0_ffn_b1': _L0_ffn_in['b1'], 'L0_ffn_W2': _L0_ffn_in['W2'], 'L0_ffn_b2': _L0_ffn_in['b2']}

def reference(x, L0_tok_row_emb_W, L0_tok_col_emb_W, L0_attn_norm1_w, L0_attn_in_proj_W, L0_attn_conv_w, L0_attn_conv_b, L0_attn_dt_bias, L0_attn_A_log, L0_attn_D, L0_attn_ssm_norm_w, L0_attn_out_proj_W, L0_attn_norm2_w, L0_attn_mlp_W1, L0_attn_mlp_W2, L0_ffn_Wg, L0_ffn_bg, L0_ffn_W1, L0_ffn_b1, L0_ffn_W2, L0_ffn_b2):
    import jax
    import jax.numpy as jnp

    def _L0_tok_ref(token_ids, row_emb_W, col_emb_W):
        import jax, jax.numpy as jnp
        import numpy as np
        D_MODEL = 192
        MAX_ROWS = 100
        MAX_COLS = 200
        NEWLINE_ID = 7
        ROW_DIM = D_MODEL // 2
        COL_DIM = D_MODEL - ROW_DIM

        def _compute_2d_positions(token_ids):
            B, S = token_ids.shape
            is_newline = (token_ids == NEWLINE_ID).astype(token_ids.dtype)
            rows_unshifted = jnp.cumsum(is_newline, axis=1)
            rows = jnp.concatenate([jnp.zeros((B, 1), dtype=token_ids.dtype), rows_unshifted[:, :-1]], axis=1)
            pos = jnp.broadcast_to(jnp.arange(S, dtype=token_ids.dtype)[None, :], (B, S))
            newline_pos = jnp.where(is_newline.astype(bool), pos, jnp.array(-1, dtype=token_ids.dtype))
            shifted = jnp.concatenate([jnp.full((B, 1), -1, dtype=token_ids.dtype), newline_pos[:, :-1]], axis=1)
            last_newline_before = jax.lax.cummax(shifted, axis=1)
            cols = pos - last_newline_before - 1
            return (rows, cols)
        rows, cols = _compute_2d_positions(token_ids)
        rows = jnp.clip(rows, 0, MAX_ROWS - 1)
        cols = jnp.clip(cols, 0, MAX_COLS - 1)
        row_emb = row_emb_W[rows]
        col_emb = col_emb_W[cols]
        return jnp.concatenate([row_emb, col_emb], axis=-1)

    def _L0_attn_ref(x, norm1_w, in_proj_W, conv_w, conv_b, dt_bias, A_log, D, ssm_norm_w, out_proj_W, norm2_w, mlp_W1, mlp_W2):
        import jax, jax.numpy as jnp
        import numpy as np
        B_, L_, D_ = (4, 512, 192)
        D_INNER = 2 * D_
        HEADDIM = 2 * D_
        NHEADS = D_INNER // HEADDIM
        D_STATE = 128
        D_CONV = 4
        CONV_DIM = D_INNER + 2 * D_STATE
        D_IN_PROJ = 2 * D_INNER + 2 * D_STATE + NHEADS
        D_FF = 4 * D_
        EPS = 1e-05

        def _rmsnorm(x, w):
            return x * jax.lax.rsqrt(jnp.mean(x * x, -1, keepdims=True) + EPS) * w

        def _causal_dwconv(xBC, w, b):
            xc = xBC.transpose(0, 2, 1)
            y = jax.lax.conv_general_dilated(xc, w[:, None, :], window_strides=(1,), padding=[(D_CONV - 1, 0)], feature_group_count=CONV_DIM)
            return (y + b[None, :, None]).transpose(0, 2, 1)

        def _ssd_scan(xh, dt, A, Bm, Cm):
            dA = jnp.exp(dt * A)
            dBx = jnp.einsum('blhp,bln,blh->blhpn', xh, Bm, dt)

            def step(h, inp):
                dA_t, dBx_t, C_t = inp
                h = h * dA_t[:, :, None, None] + dBx_t
                y = jnp.einsum('bhpn,bn->bhp', h, C_t)
                return (h, y)
            h0 = jnp.zeros((xh.shape[0], NHEADS, HEADDIM, D_STATE), xh.dtype)
            _, ys = jax.lax.scan(step, h0, (dA.transpose(1, 0, 2), dBx.transpose(1, 0, 2, 3, 4), Cm.transpose(1, 0, 2)))
            return ys.transpose(1, 0, 2, 3)

        def _mamba2(u, in_proj_W, conv_w, conv_b, dt_bias, A_log, D, ssm_norm_w, out_proj_W):
            zxbcdt = u @ in_proj_W
            z = zxbcdt[..., :D_INNER]
            xBC = zxbcdt[..., D_INNER:D_INNER + CONV_DIM]
            dt = jax.nn.softplus(zxbcdt[..., -NHEADS:] + dt_bias)
            xBC = jax.nn.silu(_causal_dwconv(xBC, conv_w, conv_b))
            xs = xBC[..., :D_INNER]
            Bm = xBC[..., D_INNER:D_INNER + D_STATE]
            Cm = xBC[..., D_INNER + D_STATE:]
            A = -jnp.exp(A_log)
            xh = xs.reshape(xs.shape[0], xs.shape[1], NHEADS, HEADDIM)
            y = _ssd_scan(xh, dt, A, Bm, Cm) + xh * D[None, None, :, None]
            y = y.reshape(y.shape[0], y.shape[1], D_INNER)
            y = _rmsnorm(y * jax.nn.silu(z), ssm_norm_w)
            return y @ out_proj_W
        res = x + _mamba2(_rmsnorm(x, norm1_w), in_proj_W, conv_w, conv_b, dt_bias, A_log, D, ssm_norm_w, out_proj_W)
        h = _rmsnorm(res, norm2_w)
        return jax.nn.gelu(h @ mlp_W1, approximate=False) @ mlp_W2

    def _L0_ffn_ref(x, Wg, bg, W1, b1, W2, b2):
        import jax, jax.numpy as jnp
        import numpy as np
        B, T, E = (2, 256, 192)
        H = 768
        N_EXP = 4
        gate_logits = jnp.einsum('bte,en->btn', x, Wg) + bg
        top = jnp.argmax(gate_logits, axis=-1)
        h = jax.nn.gelu(jnp.einsum('bte,neh->nbth', x, W1) + b1[:, None, None, :], approximate=False)
        y = jnp.einsum('nbth,nhe->nbte', h, W2) + b2[:, None, None, :]
        onehot = jax.nn.one_hot(top, N_EXP, dtype=x.dtype)
        out = jnp.einsum('nbte,btn->bte', y, onehot)
        return out
    h = _L0_tok_ref(x, L0_tok_row_emb_W, L0_tok_col_emb_W)
    h = h + _L0_attn_ref(_layernorm(h, axis=-1), L0_attn_norm1_w, L0_attn_in_proj_W, L0_attn_conv_w, L0_attn_conv_b, L0_attn_dt_bias, L0_attn_A_log, L0_attn_D, L0_attn_ssm_norm_w, L0_attn_out_proj_W, L0_attn_norm2_w, L0_attn_mlp_W1, L0_attn_mlp_W2)
    h = h + _L0_ffn_ref(_layernorm(h, axis=-1), L0_ffn_Wg, L0_ffn_bg, L0_ffn_W1, L0_ffn_b1, L0_ffn_W2, L0_ffn_b2)
    return h

_drawn_inputs = setup_inputs


def setup_inputs(seed=0):
    import zlib

    import numpy as np

    out = dict(_drawn_inputs(seed))
    spreads = {'L0_attn_norm1_w': (1.0, 0.2),
     'L0_attn_conv_b': (0.0, 0.1),
     'L0_attn_ssm_norm_w': (1.0, 0.2),
     'L0_attn_norm2_w': (1.0, 0.2)}
    factors = {}
    for name, (base, spread) in spreads.items():
        noise = np.random.default_rng([zlib.crc32(name.encode()), seed]).standard_normal(out[name].shape)
        drawn = base * np.exp(spread * noise) if base else spread * noise
        out[name] = jnp.asarray(drawn.astype(out[name].dtype))
    for name, factor in factors.items():
        out[name] = (out[name] * factor).astype(out[name].dtype)
    return out
```

```python
from contextlib import ExitStack

import concourse.bass as bass
from concourse import mybir

F32 = mybir.dt.float32
BF16 = mybir.dt.bfloat16
I32 = mybir.dt.int32
ALU = mybir.AluOpType
ACT = mybir.ActivationFunctionType
AX = mybir.AxisListType

P = 128
NB, S = 4, 512
TB = S // P
NT = NB * TB
D = 192
DH = D // 2
KA, KB = 128, 64
NROW, NCOL = 100, 200
NEWLINE = 7
DI = 2 * D
NS = 128
CT_X = DI // P
NCT = CT_X + 2
TAPS = 4
DF = 4 * D
HT = DF // P
NE = 4
EPS = 1e-5
SLOTS = NT + NE - 1
ROW = 2 * D + 4
NOBODY = 8192.0
Z0, XBC0, DT0 = 0, DI, 2 * DI + 2 * NS


def build(nc, a, out):
    with ExitStack() as ctx:
        def sb(name, shape, dt=F32):
            return ctx.enter_context(nc.sbuf_tensor(name, shape, dt))

        def sem(name):
            return ctx.enter_context(nc.semaphore(name))

        sorted_rows = nc.dram_tensor("sorted_rows", [SLOTS * P, ROW], F32, kind="Internal").ap()
        ps = ctx.enter_context(nc.psum_tensor("ps", [P, 8, 512], F32))

        ident = sb("ident", [P, P])
        upto = sb("upto", [P, NB, P])
        before = sb("before", [P, P])
        after = sb("after", [P, P])
        ones = sb("ones", [P, P])
        pick = sb("pick", [NB, NB, P], BF16)
        part_i = sb("part_i", [P, 2], I32)
        part = sb("part", [P, 2])
        count_i = sb("count_i", [P, S], I32)
        count = sb("count", [P, S])
        zeros = sb("zeros", [NB, S])
        mhalf = sb("mhalf", [P, NT])
        d_diag = sb("d_diag", [P, NB, P])
        tok_i = sb("tok_i", [NB, S], I32)
        rowW = sb("rowW", [NROW, DH])
        colW = sb("colW", [P, 2, DH])
        winA = sb("winA", [KA, DT0 + 1])
        winB = sb("winB", [KB, DT0 + 1])
        n1A = sb("n1A", [KA, 1])
        n1B = sb("n1B", [KB, 1])
        convw = sb("convw", [P, NCT, TAPS])
        convb = sb("convb", [P, NCT])
        scal = sb("scal", [P, 4])
        wout = sb("wout", [P, CT_X, D])
        ssmn = sb("ssmn", [P, CT_X])
        m1A = sb("m1A", [KA, DF])
        m1B = sb("m1B", [KB, DF])
        n2A = sb("n2A", [KA, 1])
        n2B = sb("n2B", [KB, 1])
        m2 = sb("m2", [P, HT, D])
        wgA = sb("wgA", [KA, NE])
        wgB = sb("wgB", [KB, NE])
        bg = sb("bg", [P, NE])
        e2b = sb("e2b", [1, NE * D])
        newl = sb("newl", [NB, 2, S])
        scanned = sb("scanned", [NB, 2, S + 1])
        rc = sb("rc", [NB, 2, S], BF16)
        h0 = sb("h0", [P, NT, D])
        x1 = sb("x1", [P, NT, D])
        stats = sb("stats", [P, TB, 6])
        mv = sb("mv", [P, NT, 2])
        var2 = sb("var2", [P, NB, 2, TB])
        rstd2 = sb("rstd2", [P, NB, 2, TB])
        u = sb("u", [P, 2, TB, D])
        uAB = sb("uAB", [P, 4, S])
        uA = uAB[:, 0:2, :]
        uB = uAB[0:KB, 2:4, :]
        acc = sb("acc", [P, 3, S])
        xch = sb("xch", [P, 2, CT_X, S])
        BC = sb("BC", [P, NE * HT * D])
        BT = BC[:, 0:NT * P]
        CT = BC[:, NT * P:2 * NT * P]
        xB = sb("xB", [P, NT, S])
        zs = sb("zs", [P, NT, DI])
        onehot = xB[:].rearrange("p t s -> p (t s)")[:, 0:6 * S].rearrange("p (a b s) -> p a b s", a=2, b=3)
        e2 = BC
        zsf = zs[:].rearrange("p t d -> p (t d)")
        e1A = zsf[:, 0:NE * DF]
        e1B = zsf[0:KB + 1, NE * DF:2 * NE * DF]
        dtr = sb("dtr", [P, NT])
        dtx = sb("dtx", [P, NT])
        dta = sb("dta", [P, NT])
        dte = sb("dte", [P, NT])
        dtl = sb("dtl", [P, NT])
        dt = sb("dt", [P, NT])
        decay = sb("decay", [P, NT])
        ssq = sb("ssq", [P, NT])
        ssq_e = sb("ssq_e", [P, NT])
        rr = sb("rr", [P, NT])
        Av = acc[:, 0, :].rearrange("p (b t) -> p b t", b=NB)
        E1 = acc[:, 1, :].rearrange("p (b t) -> p b t", b=NB)
        E2 = acc[:, 2, :].rearrange("p (b t) -> p b t", b=NB)
        LM = xch[:, 0, 0, :].rearrange("p (b t) -> p b t", b=NB)
        CE = xch[:, 0, 1, :].rearrange("p (b t) -> p b t", b=NB)
        MT = xch[:, 0, 2, :].rearrange("p (b t) -> p b t", b=NB)
        Bw = xch[:, 1, 0, :].rearrange("p (b t) -> p b t", b=NB)
        MT0 = xch[:, 1, 1, :].rearrange("p (b t) -> p b t", b=NB)
        junk = xch[:, 1, 2, :]
        wB = sb("wB", [P, NB])
        state = uAB[:].rearrange("p a s -> p (a s)")[:, 0:NB * DI].rearrange("p (b c) -> p b c", b=NB)
        gT = acc[:].rearrange("p a s -> p (a s)")[:, 0:2 * DI].rearrange("p (a c t) -> p a c t", a=2, c=CT_X)
        res = sb("res", [P, 2, TB, D])
        resn = u
        rA, rB = uA, uB
        hT = xch[:].rearrange("p a c s -> p (a c) s")
        ssq2 = sb("ssq2", [P, NT])
        ssq2e = sb("ssq2e", [P, NT])
        rn = sb("rn", [P, NT])
        mv2 = sb("mv2", [P, NT, 2])
        var_e = sb("var_e", [P, NT])
        r2 = sb("r2", [P, NT])
        row = xB[:].rearrange("p t s -> p (t s)")[:, 0:NT * ROW].rearrange("p (t r) -> p t r", r=ROW)
        logit = sb("logit", [P, NT, NE])
        top = sb("top", [P, NT])
        F = sb("F", [P, NT, NE])
        free = sb("free", [P, NT])
        tmp16 = sb("tmp16", [P, NT])
        rank = sb("rank", [P, NT, NE])
        tot = sb("tot", [P, NE, NT + 1])
        zer64 = sb("zer64", [P, NT])
        ntile = sb("ntile", [P, NE, NT])
        need = sb("need", [P, NE])
        base = sb("base", [P, NE + 1])
        pos = sb("pos", [P, NT])
        posi = sb("posi", [P, NT], I32)
        eidf = sb("eidf", [P, 3, 20])
        eid = sb("eid", [P, 20], I32)
        h0f = h0[:].rearrange("p t d -> p (t d)")
        slot_x = sb("slot_x", [P, 2, D])
        slot_h = sb("slot_h", [P, 2, ROW - D])
        ids = sb("ids", [P, 2], I32)
        xTA = sb("xTA", [KA, 2, P])
        xTB = sb("xTB", [KB + 1, 2, P])
        hid = h0f[:, 0:2 * DF].rearrange("p (a d) -> p a d", a=2)
        hidT = h0f[:, 2 * DF:3 * DF]
        yo = sb("yo", [P, 2, D])
        empty = sb("empty", [P, ROW])
        junk2 = sb("junk2", [P, D])
        starts = sb("starts", [P, NT])
        slotno = sb("slotno", [P, 20])

        names = """ld_x ld_tab ld_in ld_conv ld_scal ld_out ld_mlp ld_gate ld_e b1_row consts pool_seq dve_seq act_seq
            folded_in folded_out folded_mlp filled tokpos_ready idx_bc_ready onehot_ready h0_ready
            h0_copied var_ready rstd_ready u_ready uT_psum uT_copied xbc_psum tap_ready conv_done silu_done
            z_psum z_copied xtok_psum xtok_copied dt_abs dt_exp dt_done av_ready seg_psum g_psum e_ready ce_ready
            mt_ready bw_ready y_psum st_psum st_done gated ssq_done ssqe_ready rr_ready gT_psum gT_copied
            out_psum res_ready ssq2_done ssq2e_ready rn_ready resn_ready rT_psum rT_copied w1_psum gelu_done
            w2_psum h1_done var2_ready r2_ready x2_ready x2T_psum x2T_copied gate_psum logit_ready f_ready
            rank_psum pos_ready eid_ready scattered loaded_even loaded_odd h1_even h1_odd stored_even stored_odd ids_ready xT_psum xT_copied hid_psum hid_ready
            hidT_psum hidT_copied y2_psum yo_ready ddiag_ready""".split()
        s = {n: sem(n) for n in names}
        slot_loaded = (s["loaded_even"], s["loaded_odd"])
        h1_loaded = (s["h1_even"], s["h1_odd"])
        stored = (s["stored_even"], s["stored_odd"])
        block = ctx.enter_context(nc.Block())

        def bc_rows(ap1, n):
            return ap1.rearrange("(o n) -> o n", o=1).to_broadcast([P, n])

        @block.sync
        def _(sp):
            sp.dma_start(tok_i[:], a["x"]).then_inc(s["ld_x"], 16)
            sp.dma_start(rowW[:], a["L0_tok_row_emb_W"]).then_inc(s["ld_tab"], 16)
            sp.dma_start(colW[:, 0, :], a["L0_tok_col_emb_W"][0:P, :]).then_inc(s["ld_tab"], 16)
            sp.dma_start(colW[0:NCOL - P, 1, :], a["L0_tok_col_emb_W"][P:NCOL, :]).then_inc(s["ld_tab"], 16)
            for dst, k0, k1, src in ((winA, 0, KA, "L0_attn_in_proj_W"), (winB, KA, D, "L0_attn_in_proj_W")):
                sp.dma_start(dst[:], a[src][k0:k1, :]).then_inc(s["ld_in"], 16)
            n1 = a["L0_attn_norm1_w"].rearrange("(p o) -> p o", o=1)
            sp.dma_start(n1A[:], n1[0:KA, :]).then_inc(s["ld_in"], 16)
            sp.dma_start(n1B[:], n1[KA:D, :]).then_inc(s["ld_in"], 16)
            sp.dma_start(convw[:], a["L0_attn_conv_w"].rearrange("(c p) k -> p c k", p=P)).then_inc(s["ld_conv"], 16)
            sp.dma_start(convb[:], a["L0_attn_conv_b"].rearrange("(c p) -> p c", p=P),
                         allow_slow_non_contiguous=True).then_inc(s["ld_conv"], 16)
            for i, n in enumerate(("L0_attn_dt_bias", "L0_attn_A_log", "L0_attn_D")):
                sp.dma_start(scal[:, i:i + 1], bc_rows(a[n], 1)).then_inc(s["ld_scal"], 16)
            sp.dma_start(wout[:], a["L0_attn_out_proj_W"].rearrange("(c p) d -> p c d", p=P)).then_inc(s["ld_out"], 16)
            sp.dma_start(ssmn[:], a["L0_attn_ssm_norm_w"].rearrange("(c p) -> p c", p=P),
                         allow_slow_non_contiguous=True).then_inc(s["ld_out"], 16)
            sp.dma_start(m1A[:], a["L0_attn_mlp_W1"][0:KA, :]).then_inc(s["ld_mlp"], 16)
            sp.dma_start(m1B[:], a["L0_attn_mlp_W1"][KA:D, :]).then_inc(s["ld_mlp"], 16)
            n2 = a["L0_attn_norm2_w"].rearrange("(p o) -> p o", o=1)
            sp.dma_start(n2A[:], n2[0:KA, :]).then_inc(s["ld_mlp"], 16)
            sp.dma_start(n2B[:], n2[KA:D, :]).then_inc(s["ld_mlp"], 16)
            sp.dma_start(m2[:], a["L0_attn_mlp_W2"].rearrange("(c p) d -> p c d", p=P)).then_inc(s["ld_mlp"], 16)
            sp.dma_start(wgA[:], a["L0_ffn_Wg"][0:KA, :]).then_inc(s["ld_gate"], 16)
            sp.dma_start(wgB[:], a["L0_ffn_Wg"][KA:D, :]).then_inc(s["ld_gate"], 16)
            sp.dma_start(bg[:], bc_rows(a["L0_ffn_bg"], NE)).then_inc(s["ld_gate"], 16)
            sp.dma_start(e2b[:], a["L0_ffn_b2"].rearrange("(o e) h -> o (e h)", o=1)).then_inc(s["ld_e"], 16)
            sp.wait_ge(s["consts"], 1)
            for j in range(SLOTS):
                sp.dma_start(sorted_rows[j * P:(j + 1) * P, :], empty[:]).then_inc(s["filled"], 16)
            sp.wait_ge(s["ce_ready"], TB)
            sp.wait_ge(s["g_psum"], TB)
            for e in range(NE):
                sp.dma_start(e2[:, e * HT * D:(e + 1) * HT * D].rearrange("p (c d) -> p c d", c=HT),
                             a["L0_ffn_W2"][e].rearrange("(c p) d -> p c d", p=P)).then_inc(s["ld_e"], 16)
            sp.wait_ge(s["gT_psum"], NT)
            sp.wait_ge(s["ssq_done"], NT)
            for e in range(NE):
                w = slice(e * DF, (e + 1) * DF)
                sp.dma_start(e1A[:, w], a["L0_ffn_W1"][e, 0:KA, :]).then_inc(s["ld_e"], 16)
                sp.dma_start(e1B[0:KB, w], a["L0_ffn_W1"][e, KA:D, :]).then_inc(s["ld_e"], 16)
            sp.dma_start(e1B[KB:KB + 1, :], a["L0_ffn_b1"].rearrange("(o e) h -> o (e h)", o=1)).then_inc(s["ld_e"], 16)
            sp.wait_ge(s["scattered"], 16 * NT)

            def load_x2(h, par, early=False):
                if not early:
                    sp.wait_ge(s["xT_psum"], h * 2 + par - 1)
                sp.dma_start(slot_x[:, par, :], sorted_rows[bass.ds((h * 2 + par) * P, P), 0:D]
                             ).then_inc(slot_loaded[par], 16)

            def load_h1(h, par, early=False):
                if not early:
                    sp.wait_ge(s["yo_ready"], h * 2 + par - 1)
                    sp.wait_ge(s["ids_ready"], h * 2 + par - 1)
                sp.dma_start(slot_h[:, par, :], sorted_rows[bass.ds((h * 2 + par) * P, P), D:ROW]
                             ).then_inc(h1_loaded[par], 16)

            for par in range(2):
                load_x2(0, par, True)
                load_h1(0, par, True)
            with sp.Fori(1, (SLOTS - 1) // 2) as i:
                for par in range(2):
                    load_x2(i, par)
                    load_h1(i, par)
            load_x2((SLOTS - 1) // 2, 0)
            load_h1((SLOTS - 1) // 2, 0)

        @block.gpsimd
        def _(pool):
            g = nc.gpsimd
            n = [0]

            def link(ins):
                n[0] += 1
                ins.then_inc(s["pool_seq"], 1)
                pool.wait_ge(s["pool_seq"], n[0])

            g.memset(ones[:], 1.0)
            g.memset(zeros[:], 0.0)
            g.memset(zer64[:], 0.0)
            g.memset(pick[:], 1.0)
            g.memset(empty[:], 0.0)
            g.memset(upto[:], 1.0)
            g.iota(part_i[:], [[P, 2]], base=0, channel_multiplier=1)
            link(g.iota(count_i[:], [[1, S]], base=1, channel_multiplier=0))
            g.tensor_copy(part[:], part_i[:])
            link(g.tensor_copy(count[:], count_i[:]))
            g.tensor_scalar(slotno[:], count[:, 0:20], -1.0, None, ALU.add)
            g.tensor_scalar(starts[:], count[:, 0:NT], float(P), -float(P), ALU.mult, ALU.add)
            g.affine_select(out=pick[:], in_=pick[:], compare_op=ALU.is_equal, fill=0.0, base=0,
                            pattern=[[-1, NB], [0, P]], channel_multiplier=1)
            g.affine_select(out=ident[:], in_=ones[:], compare_op=ALU.is_equal, fill=0.0, base=0,
                            pattern=[[-1, P]], channel_multiplier=1)
            g.affine_select(out=before[:], in_=ones[:], compare_op=ALU.is_ge, fill=0.0, base=-1,
                            pattern=[[1, P]], channel_multiplier=-1)
            g.affine_select(out=after[:], in_=ones[:], compare_op=ALU.is_ge, fill=0.0, base=-1,
                            pattern=[[-1, P]], channel_multiplier=1)
            link(g.affine_select(out=upto[:], in_=upto[:], compare_op=ALU.is_ge, fill=0.0, base=0,
                                 pattern=[[0, NB], [1, P]], channel_multiplier=-1))
            link(g.memset(empty[:, 2 * D:2 * D + 1], NOBODY))
            g.memset(mhalf[:], -0.5).then_inc(s["consts"], 1)
            pool.wait_ge(s["ld_in"], 64)
            g.tensor_scalar(winA[:], winA[:], n1A[:, 0:1], None, ALU.mult)
            g.tensor_scalar(winB[:], winB[:], n1B[:, 0:1], None, ALU.mult).then_inc(s["folded_in"], 1)
            for b in range(NB):
                pool.wait_ge(s["var_ready"], b + 1)
                g.tensor_tensor(rstd2[:, b], var2[:, b], mhalf[:, 0:2 * TB].rearrange("p (a t) -> p a t", a=2),
                                ALU.pow).then_inc(s["rstd_ready"], 1)
            pool.wait_ge(s["ld_out"], 32)
            for c in range(CT_X):
                last = g.tensor_scalar(wout[:, c, :], wout[:, c, :], ssmn[:, c:c + 1], None, ALU.mult)
            last.then_inc(s["folded_out"], 1)
            pool.wait_ge(s["ld_mlp"], 80)
            g.tensor_scalar(m1A[:], m1A[:], n2A[:, 0:1], None, ALU.mult)
            g.tensor_scalar(m1B[:], m1B[:], n2B[:, 0:1], None, ALU.mult).then_inc(s["folded_mlp"], 1)
            pool.wait_ge(s["ld_scal"], 48)
            for b in range(NB):
                last = g.tensor_scalar(d_diag[:, b, :], ident[:], scal[:, 2:3], None, ALU.mult)
            last.then_inc(s["ddiag_ready"], 1)
            pool.wait_ge(s["ssqe_ready"], 1)
            g.tensor_tensor(rr[:], ssq_e[:], mhalf[:], ALU.pow).then_inc(s["rr_ready"], 1)

            def pow_res(b):
                pool.wait_ge(s["ssq2e_ready"], b + 1)
                g.tensor_tensor(rn[:, b * TB:(b + 1) * TB], ssq2e[:, b * TB:(b + 1) * TB], mhalf[:, 0:TB],
                                ALU.pow).then_inc(s["rn_ready"], 1)

            pow_res(0)
            for b in range(NB):
                if b + 1 < NB:
                    pow_res(b + 1)
                pool.wait_ge(s["var2_ready"], b + 1)
                g.tensor_tensor(r2[:, b * TB:(b + 1) * TB], var_e[:, b * TB:(b + 1) * TB], mhalf[:, 0:TB],
                                ALU.pow).then_inc(s["r2_ready"], 1)
            pool.wait_ge(s["pos_ready"], 1)
            pool.wait_ge(s["x2_ready"], NB)
            pool.wait_ge(s["filled"], 16 * SLOTS)
            for m in range(NT):
                g.indirect_dma_start(out=sorted_rows, out_offset=bass.IndirectOffsetOnAxis(posi[:, m:m + 1], 0),
                                     in_=row[:, m, :], in_offset=None).then_inc(s["scattered"], 16)

            last_token = pool.to_reg(NB * S - 1)

            def store_slot(j, par):
                pool.wait_ge(s["yo_ready"], j + 1)
                pool.wait_ge(s["ids_ready"], j + 1)
                g.indirect_dma_start(out=out, out_offset=bass.IndirectOffsetOnAxis(ids[:, par:par + 1], 0),
                                     in_=yo[:, par, :], in_offset=None, bounds_check=last_token,
                                     oob_is_err=False).then_inc(stored[par], 16)

            for j in range(SLOTS):
                store_slot(j, j % 2)
            pool.wait_ge(stored[0], 16 * ((SLOTS + 1) // 2))
            pool.wait_ge(stored[1], 16 * (SLOTS // 2))

        @block.scalar
        def _(act):
            A = nc.scalar
            act.wait_ge(s["ld_conv"], 32)
            for n in range(2 * NB):
                act.wait_ge(s["h0_ready"], n + 1)
                A.copy(h0[:, 2 * n:2 * n + 2, :], ps[:, 4 + n % 2, 0:2 * D].rearrange("p (a d) -> p a d", a=2)
                       ).then_inc(s["h0_copied"], 1)

            def tap(n):
                act.wait_ge(s["xbc_psum"], n + 1)
                if n >= 3:
                    act.wait_ge(s["silu_done"], n - 2)
                A.activation(acc[:, n % 3, :], ps[:, n % 3, :], ACT.Identity, bias=convb[:, n % NCT:n % NCT + 1],
                             scale=convw[:, n % NCT, TAPS - 1:TAPS]).then_inc(s["tap_ready"], 1)

            def silu(n):
                b, c = divmod(n, NCT)
                act.wait_ge(s["conv_done"], n + 1)
                if c == 0 and b >= 2:
                    act.wait_ge(s["xtok_psum"], (b - 1) * TB)
                dst = xch[:, b % 2, c, :] if c < CT_X else (BT, CT)[c - CT_X][:, b * S:(b + 1) * S]
                A.activation(dst, acc[:, n % 3, :], ACT.Silu).then_inc(s["silu_done"], 1)

            def xtok(b):
                for m in range(b * TB, (b + 1) * TB):
                    act.wait_ge(s["xtok_psum"], m + 1)
                    A.copy(xB[:, m, :], ps[:, 5, :]).then_inc(s["xtok_copied"], 1)

            for b in range(NB):
                act.wait_ge(s["uT_psum"], b + 1)
                if b >= 2:
                    act.wait_ge(s["z_psum"], (b - 1) * TB)
                A.copy(uA[:, b % 2, :], ps[:, 6, :])
                A.copy(uB[:, b % 2, :], ps[0:KB, 7, :]).then_inc(s["uT_copied"], 1)
                tap(b * NCT)
                for c in range(1, NCT):
                    tap(b * NCT + c)
                    silu(b * NCT + c - 1)
                for m in range(b * TB, (b + 1) * TB):
                    act.wait_ge(s["z_psum"], m + 1)
                    A.activation(zs[:, m, :], ps[:, 3 + m % 2, 0:DI], ACT.Silu)
                    A.copy(dtr[:, m:m + 1], ps[:, 3 + m % 2, DI:DI + 1]).then_inc(s["z_copied"], 1)
                silu(b * NCT + NCT - 1)
                if b:
                    xtok(b - 1)
            xtok(NB - 1)
            act.wait_ge(s["dt_abs"], 1)
            A.activation(dte[:], dta[:], ACT.Exp, scale=-1.0).then_inc(s["act_seq"], 1)
            A.activation(scal[:, 3:4], scal[:, 1:2], ACT.Exp).then_inc(s["act_seq"], 1)
            act.wait_ge(s["act_seq"], 2)
            A.activation(dtl[:], dte[:], ACT.Ln, bias=1.0).then_inc(s["dt_exp"], 1)

            def square(c, b):
                k = c * NB + b
                m = b * TB + c
                act.wait_ge(s["gated"], k + 1)
                if k:
                    act.wait_ge(s["ssq_done"], k)
                A.activation(junk[:, 0:DI], zs[:, m, :], ACT.Square, accum_out=ssq[:, m:m + 1]
                             ).then_inc(s["ssq_done"], 1)

            for c in range(TB):
                act.wait_ge(s["seg_psum"], c + 1)
                if c:
                    act.wait_ge(s["ce_ready"], c)
                    act.wait_ge(s["bw_ready"], c)
                    act.wait_ge(s["st_done"], NB * c)
                A.activation(E1, ps[:, 0, :].rearrange("p (b t) -> p b t", b=NB), ACT.Exp)
                A.activation(E2, ps[:, 1, :].rearrange("p (b t) -> p b t", b=NB), ACT.Exp).then_inc(s["e_ready"], 1)
                for b in range(NB):
                    square(c, b)

            def out_stage(b):
                for m in range(b * TB, (b + 1) * TB):
                    act.wait_ge(s["gT_psum"], m + 1)
                    if m >= 2:
                        act.wait_ge(s["out_psum"], m - 1)
                    A.copy(gT[:, m % 2], ps[:, 0, 0:DI].rearrange("p (c t) -> p c t", c=CT_X)
                           ).then_inc(s["gT_copied"], 1)
                for m in range(b * TB, (b + 1) * TB):
                    act.wait_ge(s["res_ready"], m + 1)
                    if m:
                        act.wait_ge(s["ssq2_done"], m)
                    A.activation(junk2[:], res[:, b % 2, m % TB, :],
                                 ACT.Square, accum_out=ssq2[:, m:m + 1]).then_inc(s["ssq2_done"], 1)

            def copy_T(sem_in, n, sem_out):
                act.wait_ge(s[sem_in], n)
                A.copy(rA[:, 0 if sem_in == "rT_psum" else 1, :], ps[:, 2, :])
                A.copy(rB[:, 0 if sem_in == "rT_psum" else 1, :], ps[0:KB, 3, :]).then_inc(s[sem_out], 1)

            out_stage(0)
            for b in range(NB):
                if b + 1 < NB:
                    out_stage(b + 1)
                if b:
                    act.wait_ge(s["w1_psum"], b * HT)
                copy_T("rT_psum", b + 1, "rT_copied")
                for n in range(b * HT, (b + 1) * HT):
                    act.wait_ge(s["w1_psum"], n + 1)
                    if b and n % HT == 0:
                        act.wait_ge(s["w2_psum"], b * TB)
                    A.activation(hT[:, n % HT, :], ps[:, 4 + n % 2, :], ACT.Gelu).then_inc(s["gelu_done"], 1)
                if b:
                    if b >= 2:
                        act.wait_ge(s["gate_psum"], b - 1)
                    copy_T("x2T_psum", b, "x2T_copied")
            act.wait_ge(s["gate_psum"], NB - 1)
            copy_T("x2T_psum", NB, "x2T_copied")

            def turn(j, par):
                act.wait_ge(s["xT_psum"], j + 1)
                A.copy(xTA[:, par, :], ps[:, 0, 0:P])
                A.copy(xTB[0:KB, par, :], ps[0:KB, 0, P:2 * P]).then_inc(s["xT_copied"], 1)

            def gelu(j, par):
                act.wait_ge(s["hid_psum"], j + 1)
                A.activation(hid[:, par, :], ps[:, 1 + 2 * par:3 + 2 * par, :].rearrange("p a s -> p (a s)")[:, 0:DF],
                             ACT.Gelu).then_inc(s["hid_ready"], 1)

            turn(0, 0)
            turn(1, 1)
            with act.Fori(0, (SLOTS - 3) // 2) as i:
                for par in range(2):
                    gelu(i * 2 + par, par)
                    turn(i * 2 + par + 2, par)
            gelu(SLOTS - 3, 0)
            turn(SLOTS - 1, 0)
            gelu(SLOTS - 2, 1)
            gelu(SLOTS - 1, 0)

        @block.vector
        def _(dve):
            V = nc.vector
            n = [0]

            def link(ins):
                n[0] += 1
                ins.then_inc(s["dve_seq"], 1)
                dve.wait_ge(s["dve_seq"], n[0])

            dve.wait_ge(s["ld_x"], 16)
            dve.wait_ge(s["consts"], 1)
            V.memset(xTB[KB:KB + 1, :, :], 1.0)
            V.memset(scanned[:, :, 0:1], 0.0)
            link(V.tensor_copy(newl[:, 1, :], tok_i[:]))
            link(V.tensor_scalar(newl[:, 0, :], newl[:, 1, :], float(NEWLINE), None, ALU.is_equal))
            link(V.tensor_tensor(newl[:, 1, :], newl[:, 0, :], count[0:NB, :], ALU.mult))
            V.tensor_tensor_scan(scanned[:, 0, 1:S + 1], newl[:, 0, :], zeros[:], 0.0, ALU.add, ALU.add)
            link(V.tensor_tensor_scan(scanned[:, 1, 1:S + 1], newl[:, 1, :], zeros[:], 0.0, ALU.max, ALU.max))
            V.tensor_scalar(rc[:, 0, :], scanned[:, 0, 0:S], float(NROW - 1), None, ALU.min)
            link(V.scalar_tensor_tensor(newl[:, 0, :], count[0:NB, :], 1.0, scanned[:, 1, 0:S],
                                        ALU.subtract, ALU.subtract))
            V.tensor_scalar(rc[:, 1, :], newl[:, 0, :], float(NCOL - 1), None, ALU.min).then_inc(s["tokpos_ready"], 1)

            def one_hot(b):
                q = b % 2
                dve.wait_ge(s["idx_bc_ready"], b + 1)
                if b >= 2:
                    dve.wait_ge(s["h0_ready"], 2 * (b - 1))
                V.tensor_scalar(onehot[:, q, 0, :], ps[:, 2 * q, :], part[:, 0:1], None, ALU.is_equal)
                V.tensor_scalar(onehot[:, q, 1, :], ps[:, 2 * q + 1, :], part[:, 0:1], None, ALU.is_equal)
                V.tensor_scalar(onehot[:, q, 2, :], ps[:, 2 * q + 1, :], part[:, 1:2], None, ALU.is_equal
                                ).then_inc(s["onehot_ready"], 1)

            def norm_stats(src, b, dst):
                for t in range(TB):
                    last = V.bn_stats(stats[:, t, :], src[:, b * TB + t, :])
                link(last)
                for t in range(TB):
                    last = V.bn_aggr(dst[:, b * TB + t, :], stats[:, t, :])
                link(last)

            def first_norm(b):
                dve.wait_ge(s["h0_copied"], 2 * b + 2)
                norm_stats(h0, b, mv)
                v = mv[:, b * TB:(b + 1) * TB, 1]
                V.tensor_scalar(var2[:, b, 0, :], v, EPS, None, ALU.add)
                V.tensor_scalar(var2[:, b, 1, :], v, 1.0 + EPS, EPS * EPS, ALU.mult, ALU.add
                                ).then_inc(s["var_ready"], 1)
                dve.wait_ge(s["rstd_ready"], b + 1)
                if b >= 2:
                    dve.wait_ge(s["uT_psum"], b - 1)
                for t in range(TB):
                    m = b * TB + t
                    V.tensor_scalar(u[:, b % 2, t, :], h0[:, m, :], mv[:, m, 0:1], rstd2[:, b, 1, t:t + 1],
                                    ALU.subtract, ALU.mult)
                    last = V.tensor_scalar(x1[:, m, :], h0[:, m, :], mv[:, m, 0:1], rstd2[:, b, 0, t:t + 1],
                                           ALU.subtract, ALU.mult)
                last.then_inc(s["u_ready"], 1)

            def conv(n):
                dve.wait_ge(s["tap_ready"], n + 1)
                for k in range(TAPS - 2, -1, -1):
                    d = TAPS - 1 - k
                    ins = V.scalar_tensor_tensor(acc[:, n % 3, d:S], ps[:, n % 3, 0:S - d],
                                                 convw[:, n % NCT, k:k + 1], acc[:, n % 3, d:S], ALU.mult, ALU.add)
                    if k:
                        link(ins)
                ins.then_inc(s["conv_done"], 1)

            for b in range(NB):
                one_hot(b)
            first_norm(0)
            first_norm(1)
            for b in range(NB):
                for c in range(NCT):
                    conv(b * NCT + c)
                if b + 2 < NB:
                    first_norm(b + 2)
            dve.wait_ge(s["z_copied"], NT)
            dve.wait_ge(s["ld_scal"], 48)
            link(V.tensor_scalar(dtx[:], dtr[:], scal[:, 0:1], None, ALU.add))
            link(V.tensor_scalar(dta[:], dtx[:], -1.0, None, ALU.mult))
            V.tensor_tensor(dta[:], dta[:], dtx[:], ALU.max).then_inc(s["dt_abs"], 1)
            dve.wait_ge(s["dt_exp"], 1)
            link(V.scalar_tensor_tensor(dt[:], dtx[:], 0.0, dtl[:], ALU.max, ALU.add))
            link(V.tensor_scalar(decay[:], dt[:], scal[:, 3:4], -1.0, ALU.mult, ALU.mult))

            dtg = dt[:].rearrange("p (b c) -> p b c", b=NB)
            CTg = CT.rearrange("p (b c t) -> p b c t", b=NB, c=TB)
            dve.wait_ge(s["silu_done"], NB * NCT)
            dve.wait_ge(s["xtok_psum"], NT)
            dve.wait_ge(s["ddiag_ready"], 1)

            def segments(c):
                if c:
                    dve.wait_ge(s["seg_psum"], c)
                for b in range(NB):
                    m = b * TB + c
                    last = V.tensor_scalar(Av[:, b, :], upto[:, 0, :], decay[:, m:m + 1], None, ALU.mult)
                last.then_inc(s["av_ready"], 1)

            segments(0)
            for c in range(TB):
                dve.wait_ge(s["e_ready"], c + 1)
                V.tensor_tensor(LM, E1, upto[:], ALU.mult)
                link(V.tensor_tensor(wB[:], E1[:, :, P - 1], dtg[:, :, c], ALU.mult))
                if c:
                    dve.wait_ge(s["y_psum"], c * NB)
                V.tensor_tensor(CE, CTg[:, :, c, :], E2, ALU.mult).then_inc(s["ce_ready"], 1)
                dve.wait_ge(s["g_psum"], c + 1)
                for b in range(NB):
                    m = b * TB + c
                    last = V.scalar_tensor_tensor(MT0[:, b, :], ps[:, 2, b * P:(b + 1) * P], dt[:, m:m + 1],
                                                  LM[:, b, :], ALU.mult, ALU.mult)
                link(last)
                V.tensor_tensor(MT, MT0, d_diag[:], ALU.add).then_inc(s["mt_ready"], 1)
                if c and c < TB - 1:
                    dve.wait_ge(s["st_psum"], c * NB)
                if c < TB - 1:
                    for b in range(NB):
                        last = V.tensor_scalar(Bw[:, b, :], xB[:, b * TB + c, DI:S], wB[:, b:b + 1], None, ALU.mult)
                    last.then_inc(s["bw_ready"], 1)
                    segments(c + 1)
                for b in range(NB):
                    m = b * TB + c
                    k = c * NB + b
                    dve.wait_ge(s["y_psum"], k + 1)
                    V.tensor_tensor(zs[:, m, :], ps[:, 3 + b % 2, 0:DI], zs[:, m, :], ALU.mult
                                    ).then_inc(s["gated"], 1)
                    if c == TB - 1:
                        continue
                    dve.wait_ge(s["st_psum"], k + 1)
                    if c == 0:
                        V.tensor_copy(state[:, b, :], ps[:, 5 + b % 2, 0:DI]).then_inc(s["st_done"], 1)
                    else:
                        V.scalar_tensor_tensor(state[:, b, :], state[:, b, :], E2[:, b, P - 1:P],
                                               ps[:, 5 + b % 2, 0:DI], ALU.mult, ALU.add).then_inc(s["st_done"], 1)
            dve.wait_ge(s["ssq_done"], NT)
            V.tensor_scalar(ssq_e[:], ssq[:], 1.0 / DI, EPS, ALU.mult, ALU.add).then_inc(s["ssqe_ready"], 1)
            dve.wait_ge(s["rr_ready"], 1)

            def residual(b):
                for m in range(b * TB, (b + 1) * TB):
                    dve.wait_ge(s["out_psum"], m + 1)
                    V.scalar_tensor_tensor(res[:, b % 2, m % TB, :], ps[:, 1, 0:D], rr[:, m:m + 1], x1[:, m, :],
                                           ALU.mult, ALU.add).then_inc(s["res_ready"], 1)
                dve.wait_ge(s["ssq2_done"], (b + 1) * TB)
                q = slice(b * TB, (b + 1) * TB)
                V.tensor_scalar(ssq2e[:, q], ssq2[:, q], 1.0 / D, EPS, ALU.mult, ALU.add
                                ).then_inc(s["ssq2e_ready"], 1)

            def res_scaled(b):
                dve.wait_ge(s["rn_ready"], b + 1)
                for m in range(b * TB, (b + 1) * TB):
                    last = V.tensor_scalar(resn[:, b % 2, m % TB, :], res[:, b % 2, m % TB, :], rn[:, m:m + 1], None,
                                           ALU.mult)
                last.then_inc(s["resn_ready"], 1)

            def second_norm(b):
                q = slice(b * TB, (b + 1) * TB)
                for m in range(b * TB, (b + 1) * TB):
                    dve.wait_ge(s["w2_psum"], m + 1)
                    last = V.tensor_tensor(row[:, m, D:2 * D], ps[:, 6 + m % 2, 0:D], h0[:, m, :], ALU.add)
                    last.then_inc(s["h1_done"], 1)
                dve.wait_ge(s["h1_done"], (b + 1) * TB)
                norm_stats(row[:, :, D:2 * D], b, mv2)
                V.tensor_scalar(var_e[:, q], mv2[:, q, 1], EPS, None, ALU.add).then_inc(s["var2_ready"], 1)
                dve.wait_ge(s["r2_ready"], b + 1)
                for m in range(b * TB, (b + 1) * TB):
                    V.memset(row[:, m, 2 * D + 1:ROW], 0.0)
                    V.tensor_scalar(row[:, m, 2 * D:2 * D + 1], part[:, 0:1], float(m * P), None, ALU.add)
                    last = V.tensor_scalar(row[:, m, 0:D], row[:, m, D:2 * D], mv2[:, m, 0:1], r2[:, m:m + 1],
                                           ALU.subtract, ALU.mult)
                last.then_inc(s["x2_ready"], 1)

            def logits(b):
                dve.wait_ge(s["gate_psum"], b + 1)
                for t in range(TB):
                    last = V.tensor_tensor(logit[:, b * TB + t, :], ps[:, 1, 256 + NE * t:256 + NE * (t + 1)], bg[:],
                                           ALU.add)
                last.then_inc(s["logit_ready"], 1)

            dve.wait_ge(s["ld_gate"], 48)
            residual(0)
            for b in range(NB):
                if b + 1 < NB:
                    residual(b + 1)
                res_scaled(b)
                if b:
                    logits(b - 1)
                second_norm(b)
            logits(NB - 1)
            dve.wait_ge(s["logit_ready"], NB)
            link(V.tensor_reduce(top[:], logit[:], AX.X, ALU.max))
            for e in range(NE):
                link(V.tensor_tensor(tmp16[:], logit[:, :, e], top[:], ALU.is_equal))
                if e == 0:
                    V.tensor_copy(F[:, :, e], tmp16[:])
                    link(V.tensor_scalar(free[:], tmp16[:], -1.0, 1.0, ALU.mult, ALU.add))
                else:
                    link(V.tensor_tensor(F[:, :, e], tmp16[:], free[:], ALU.mult))
                    link(V.tensor_tensor(free[:], free[:], F[:, :, e], ALU.subtract))
            V.memset(tot[:, :, 0:1], 0.0).then_inc(s["f_ready"], 1)
            dve.wait_ge(s["rank_psum"], 1)
            V.tensor_copy(rank[:], ps[:, 0, 0:NT * NE].rearrange("p (t e) -> p t e", e=NE))
            for e in range(NE):
                last = V.tensor_tensor_scan(tot[:, e, 1:NT + 1],
                                            ps[:, 1, 0:NT * NE].rearrange("p (t e) -> p t e", e=NE)[:, :, e],
                                            zer64[:], 0.0, ALU.add, ALU.add)
            link(last)
            for e in range(NE):
                last = V.tensor_scalar(ntile[:, e, :], starts[:], tot[:, e, NT:NT + 1], None, ALU.is_lt)
            link(last)
            V.memset(base[:, 0:1], 0.0)
            link(V.tensor_reduce(need[:], ntile[:], AX.X, ALU.add))
            for e in range(NE):
                link(V.tensor_tensor(base[:, e + 1:e + 2], base[:, e:e + 1], need[:, e:e + 1], ALU.add))
            for e in range(NE):
                link(V.scalar_tensor_tensor(tmp16[:], rank[:, :, e], 1.0, tot[:, e, 0:NT], ALU.mult, ALU.add))
                link(V.scalar_tensor_tensor(free[:], base[:, e:e + 1].to_broadcast([P, NT]), float(P), tmp16[:],
                                            ALU.mult, ALU.add))
                if e == 0:
                    link(V.tensor_tensor(pos[:], free[:], F[:, :, e], ALU.mult))
                else:
                    link(V.tensor_tensor(free[:], free[:], F[:, :, e], ALU.mult))
                    link(V.tensor_tensor(pos[:], pos[:], free[:], ALU.add))
            V.tensor_copy(posi[:], pos[:]).then_inc(s["pos_ready"], 1)
            for e in range(1, NE):
                last = V.tensor_scalar(eidf[:, e - 1, :], slotno[:], base[:, e:e + 1], None, ALU.is_ge)
            link(last)
            link(V.tensor_tensor(eidf[:, 0, :], eidf[:, 0, :], eidf[:, 1, :], ALU.add))
            link(V.tensor_tensor(eidf[:, 0, :], eidf[:, 0, :], eidf[:, 2, :], ALU.add))
            V.tensor_copy(eid[:], eidf[:, 0, :]).then_inc(s["eid_ready"], 1)

            def numbers(h, par, first=False):
                dve.wait_ge(h1_loaded[par], (h + 1) * 16)
                if not first:
                    dve.wait_ge(stored[par], h * 16)
                V.tensor_copy(ids[:, par:par + 1], slot_h[:, par, D:D + 1]).then_inc(s["ids_ready"], 1)

            def turn_hidden(j):
                dve.wait_ge(s["hidT_psum"], j + 1)
                V.tensor_copy(hidT[:], ps[:, 5:7, :].rearrange("p a s -> p (a s)")[:, 0:DF]
                              ).then_inc(s["hidT_copied"], 1)

            def add_h1(j, par):
                dve.wait_ge(s["y2_psum"], j + 1)
                V.tensor_tensor(yo[:, par, :], ps[:, 7, 0:D], slot_h[:, par, 0:D], ALU.add
                                ).then_inc(s["yo_ready"], 1)

            numbers(0, 0, True)
            turn_hidden(0)
            add_h1(0, 0)
            numbers(0, 1, True)
            turn_hidden(1)
            add_h1(1, 1)
            with dve.Fori(1, (SLOTS - 1) // 2) as i:
                for par in range(2):
                    numbers(i, par)
                    turn_hidden(i * 2 + par)
                    add_h1(i * 2 + par, par)
            numbers((SLOTS - 1) // 2, 0)
            turn_hidden(SLOTS - 1)
            add_h1(SLOTS - 1, 0)

        @block.tensor
        def _(pe):
            T = nc.tensor

            def mm(o, l, r, start=True, stop=True):
                return T.matmul(o, l, r, start=start, stop=stop)

            pe.wait_ge(s["consts"], 1)
            pe.wait_ge(s["tokpos_ready"], 1)
            pe.wait_ge(s["ld_tab"], 48)
            for b in range(NB):
                q = b % 2
                if b >= 2:
                    pe.wait_ge(s["onehot_ready"], b - 1)
                mm(ps[:, 2 * q, :], pick[:, b, :], rc[:, 0, :])
                mm(ps[:, 2 * q + 1, :], pick[:, b, :], rc[:, 1, :]).then_inc(s["idx_bc_ready"], 1)
                pe.wait_ge(s["onehot_ready"], b + 1)
                for p in range(2):
                    n = 2 * b + p
                    if n >= 2:
                        pe.wait_ge(s["h0_copied"], n - 1)
                    for t in range(2):
                        w = slice((2 * p + t) * P, (2 * p + t + 1) * P)
                        o = ps[:, 4 + n % 2, t * D:(t + 1) * D]
                        mm(o[:, 0:DH], onehot[0:NROW, q, 0, w], rowW[:])
                        mm(o[:, DH:D], onehot[:, q, 1, w], colW[:, 0, :], stop=False)
                        last = mm(o[:, DH:D], onehot[0:NCOL - P, q, 2, w], colW[0:NCOL - P, 1, :], start=False)
                    last.then_inc(s["h0_ready"], 1)

            def turn_tiles(src, bankA, bankB):
                for t in range(TB):
                    T.transpose(ps[:, bankA, t * P:(t + 1) * P], src(t)[:, 0:KA], ident[:])
                    last = T.transpose(ps[0:KB, bankB, t * P:(t + 1) * P], src(t)[:, KA:D], ident[:])
                return last

            def xtok(b):
                pe.wait_ge(s["silu_done"], b * NCT + CT_X + 1)
                for t in range(TB):
                    m = b * TB + t
                    if m:
                        pe.wait_ge(s["xtok_copied"], m)
                    for c in range(CT_X):
                        T.transpose(ps[:, 5, c * P:(c + 1) * P], xch[:, b % 2, c, t * P:(t + 1) * P], ident[:])
                    T.transpose(ps[:, 5, DI:S], BT[:, m * P:(m + 1) * P], ident[:]).then_inc(s["xtok_psum"], 1)

            pe.wait_ge(s["folded_in"], 1)
            for b in range(NB):
                q = b % 2
                pe.wait_ge(s["u_ready"], b + 1)
                if b:
                    pe.wait_ge(s["uT_copied"], b)
                turn_tiles(lambda t: u[:, q, t, :], 6, 7).then_inc(s["uT_psum"], 1)
                pe.wait_ge(s["uT_copied"], b + 1)
                for c in range(NCT):
                    n = b * NCT + c
                    if n >= 3:
                        pe.wait_ge(s["conv_done"], n - 2)
                    w = slice(XBC0 + c * P, XBC0 + (c + 1) * P)
                    mm(ps[:, n % 3, :], winA[:, w], uA[:, q, :], stop=False)
                    mm(ps[:, n % 3, :], winB[:, w], uB[:, q, :], start=False).then_inc(s["xbc_psum"], 1)
                if b == 0:
                    pe.wait_ge(s["h0_copied"], 2 * NB)
                for t in range(TB):
                    m = b * TB + t
                    if m >= 2:
                        pe.wait_ge(s["z_copied"], m - 1)
                    bank = 3 + m % 2
                    w = slice(t * P, (t + 1) * P)
                    mm(ps[:, bank, 0:DI], uA[:, q, w], winA[:, Z0:Z0 + DI], stop=False)
                    mm(ps[:, bank, 0:DI], uB[:, q, w], winB[:, Z0:Z0 + DI], start=False)
                    mm(ps[:, bank, DI:DI + 1], uA[:, q, w], winA[:, DT0:DT0 + 1], stop=False)
                    mm(ps[:, bank, DI:DI + 1], uB[:, q, w], winB[:, DT0:DT0 + 1], start=False
                       ).then_inc(s["z_psum"], 1)
                if b:
                    xtok(b - 1)
            xtok(NB - 1)
            pe.wait_ge(s["xtok_copied"], NT)
            pe.wait_ge(s["z_copied"], NT)

            def seg(c):
                pe.wait_ge(s["av_ready"], c + 1)
                if c:
                    pe.wait_ge(s["e_ready"], c)
                mm(ps[:, 0, :], after[:], Av)
                mm(ps[:, 1, :], ones[:], Av).then_inc(s["seg_psum"], 1)

            def bc(c):
                if c:
                    pe.wait_ge(s["mt_ready"], c)
                for b in range(NB):
                    w = slice((b * TB + c) * P, (b * TB + c + 1) * P)
                    last = mm(ps[:, 2, b * P:(b + 1) * P], BT[:, w], CT[:, w])
                last.then_inc(s["g_psum"], 1)

            pe.wait_ge(s["silu_done"], NB * NCT)
            pe.wait_ge(s["conv_done"], NB * NCT)
            bc(0)
            seg(0)
            for c in range(TB):
                pe.wait_ge(s["mt_ready"], c + 1)
                pe.wait_ge(s["ce_ready"], c + 1)
                if c < TB - 1:
                    bc(c + 1)
                    seg(c + 1)
                    pe.wait_ge(s["bw_ready"], c + 1)
                if c:
                    pe.wait_ge(s["st_done"], NB * c)
                for b in range(NB):
                    m = b * TB + c
                    k = c * NB + b
                    if k >= 2:
                        pe.wait_ge(s["gated"], k - 1)
                    last = mm(ps[:, 3 + b % 2, 0:DI], MT[:, b, :], xB[:, m, 0:DI], stop=(c == 0))
                    if c:
                        last = mm(ps[:, 3 + b % 2, 0:DI], CE[:, b, :], state[:, b, :], start=False)
                    last.then_inc(s["y_psum"], 1)
                    if c < TB - 1:
                        if k >= 2:
                            pe.wait_ge(s["st_done"], k - 1)
                        mm(ps[:, 5 + b % 2, 0:DI], Bw[:, b, :], xB[:, m, 0:DI]).then_inc(s["st_psum"], 1)

            pe.wait_ge(s["folded_out"], 1)
            pe.wait_ge(s["folded_mlp"], 1)
            pe.wait_ge(s["ld_gate"], 48)

            def out_proj(b):
                for m in range(b * TB, (b + 1) * TB):
                    pe.wait_ge(s["gated"], (m % TB) * NB + m // TB + 1)
                    if m:
                        pe.wait_ge(s["gT_copied"], m)
                    for c in range(CT_X):
                        last = T.transpose(ps[:, 0, c * P:(c + 1) * P], zs[:, m, c * P:(c + 1) * P], ident[:])
                    last.then_inc(s["gT_psum"], 1)
                    pe.wait_ge(s["gT_copied"], m + 1)
                    if m:
                        pe.wait_ge(s["res_ready"], m)
                    if b >= 3:
                        pe.wait_ge(s["logit_ready"], b - 2)
                    for c in range(CT_X):
                        last = mm(ps[:, 1, 0:D], gT[:, m % 2, c, :], wout[:, c, :], start=(c == 0), stop=(c == CT_X - 1))
                    last.then_inc(s["out_psum"], 1)

            def mlp(b):
                pe.wait_ge(s["resn_ready"], b + 1)
                if b >= 2:
                    pe.wait_ge(s["x2T_copied"], b - 1)
                turn_tiles(lambda t: resn[:, b % 2, t, :], 2, 3).then_inc(s["rT_psum"], 1)
                pe.wait_ge(s["rT_copied"], b + 1)
                for c in range(HT):
                    n = b * HT + c
                    if n >= 2:
                        pe.wait_ge(s["gelu_done"], n - 1)
                    w = slice(c * P, (c + 1) * P)
                    mm(ps[:, 4 + n % 2, :], m1A[:, w], rA[:, 0, :], stop=False)
                    mm(ps[:, 4 + n % 2, :], m1B[:, w], rB[:, 0, :], start=False).then_inc(s["w1_psum"], 1)

            def mlp_down(b):
                pe.wait_ge(s["gelu_done"], (b + 1) * HT)
                for t in range(TB):
                    m = b * TB + t
                    if m >= 2:
                        pe.wait_ge(s["h1_done"], m - 1)
                    for c in range(HT):
                        last = mm(ps[:, 6 + m % 2, 0:D], hT[:, c, t * P:(t + 1) * P], m2[:, c, :],
                                  start=(c == 0), stop=(c == HT - 1))
                    last.then_inc(s["w2_psum"], 1)

            def gate(b):
                pe.wait_ge(s["x2_ready"], b + 1)
                turn_tiles(lambda t: row[:, b * TB + t, 0:D], 2, 3).then_inc(s["x2T_psum"], 1)
                pe.wait_ge(s["x2T_copied"], b + 1)
                pe.wait_ge(s["res_ready"], min(NT, (b + 3) * TB))
                if b:
                    pe.wait_ge(s["logit_ready"], b)
                for t in range(TB):
                    o = ps[:, 1, 256 + NE * t:256 + NE * (t + 1)]
                    w = slice(t * P, (t + 1) * P)
                    mm(o, rA[:, 1, w], wgA[:], stop=False)
                    last = mm(o, rB[:, 1, w], wgB[:], start=False)
                last.then_inc(s["gate_psum"], 1)

            out_proj(0)
            for b in range(NB):
                if b + 1 < NB:
                    out_proj(b + 1)
                mlp(b)
                if b:
                    gate(b - 1)
                mlp_down(b)
            gate(NB - 1)
            pe.wait_ge(s["f_ready"], 1)
            Ff = F[:].rearrange("p t e -> p (t e)")
            mm(ps[:, 0, 0:NT * NE], before[:], Ff)
            mm(ps[:, 1, 0:NT * NE], ones[:], Ff).then_inc(s["rank_psum"], 1)
            pe.wait_ge(s["eid_ready"], 1)
            pe.wait_ge(s["ld_e"], 16 * (3 * NE + 2))

            def turn(h, par, first=False):
                pe.wait_ge(slot_loaded[par], (h + 1) * 16)
                if not first:
                    pe.wait_ge(s["xT_copied"], h * 2 + par)
                T.transpose(ps[:, 0, 0:P], slot_x[:, par, 0:KA], ident[:])
                T.transpose(ps[0:KB, 0, P:2 * P], slot_x[:, par, KA:D], ident[:]).then_inc(s["xT_psum"], 1)

            def up(j, par, e):
                pe.wait_ge(s["xT_copied"], j + 1)
                for bank, c0, w in ((1 + 2 * par, 0, 512), (2 + 2 * par, 512, DF - 512)):
                    mm(ps[:, bank, 0:w], xTA[:, par, :], e1A[:, bass.ds(e * DF + c0, w)], stop=False)
                    last = mm(ps[:, bank, 0:w], xTB[:, par, :], e1B[:, bass.ds(e * DF + c0, w)], start=False)
                last.then_inc(s["hid_psum"], 1)

            def down(j, par, e, first=False):
                pe.wait_ge(s["hid_ready"], j + 1)
                if not first:
                    pe.wait_ge(s["hidT_copied"], j)
                for c in range(HT):
                    last = T.transpose(ps[:, 5 + c // 4, (c % 4) * P:(c % 4 + 1) * P],
                                       hid[:, par, c * P:(c + 1) * P], ident[:])
                last.then_inc(s["hidT_psum"], 1)
                pe.wait_ge(s["hidT_copied"], j + 1)
                if not first:
                    pe.wait_ge(s["yo_ready"], j)
                for c in range(HT):
                    mm(ps[:, 7, 0:D], hidT[:, c * P:(c + 1) * P], e2[:, bass.ds(e * (HT * D) + c * D, D)],
                       start=(c == 0), stop=False)
                mm(ps[:, 7, 0:D], ones[0:1, :], e2b[:, bass.ds(e * D, D)], start=False).then_inc(s["y2_psum"], 1)

            def expert(j):
                return pe.value_load(eid[0:1, bass.ds(j, 1)], min_val=0, max_val=NE - 1)

            turn(0, 0, True)
            up(0, 0, expert(0))
            turn(0, 1)
            up(1, 1, expert(1))
            turn(1, 0)
            down(0, 0, expert(0), True)
            with pe.Fori(0, (SLOTS - 3) // 2) as i:
                for par in range(2):
                    j = i * 2 + par
                    up(j + 2, par, expert(j + 2))
                    turn(i + 1 + par, 1 - par)
                    down(j + 1, 1 - par, expert(j + 1))
            up(SLOTS - 1, 0, expert(SLOTS - 1))
            down(SLOTS - 2, 1, expert(SLOTS - 2))
            down(SLOTS - 1, 0, expert(SLOTS - 1))


_INS = ["x", "L0_tok_row_emb_W", "L0_tok_col_emb_W", "L0_attn_norm1_w", "L0_attn_in_proj_W", "L0_attn_conv_w",
        "L0_attn_conv_b", "L0_attn_dt_bias", "L0_attn_A_log", "L0_attn_D", "L0_attn_ssm_norm_w",
        "L0_attn_out_proj_W", "L0_attn_norm2_w", "L0_attn_mlp_W1", "L0_attn_mlp_W2", "L0_ffn_Wg", "L0_ffn_bg",
        "L0_ffn_W1", "L0_ffn_b1", "L0_ffn_W2", "L0_ffn_b2"]


def kernel(**inputs):
    import numpy as _np
    import concourse.bacc as _bacc
    from concourse import mybir as _mybir
    from concourse.bass_utils import run_bass_kernel_spmd as _run

    nc = _bacc.Bacc("TRN2", target_bir_lowering=False, num_devices=1)
    arrays, aps = {}, {}
    for name in _INS:
        v = _np.ascontiguousarray(inputs[name])
        arrays[f"in_{name}"] = v
        aps[name] = nc.dram_tensor(f"in_{name}", v.shape, _mybir.dt.from_np(v.dtype), kind="ExternalInput").ap()
    out = nc.dram_tensor("out_h", (NB * S, D), _mybir.dt.from_np(_np.dtype("float32")), kind="ExternalOutput").ap()
    build(nc, aps, out)
    r = _run(nc, [arrays], core_ids=[0])
    return r.results[0]["out_h"].reshape(NB, S, D)
```

```python
from contextlib import ExitStack

import concourse.bass as bass
from concourse import mybir

F32 = mybir.dt.float32
BF16 = mybir.dt.bfloat16
F32R = mybir.dt.float32r
I32 = mybir.dt.int32
ALU = mybir.AluOpType
ACT = mybir.ActivationFunctionType
AX = mybir.AxisListType

P = 128
NB, S = 4, 512
TB = S // P
NT = NB * TB
D = 192
DH = D // 2
KA, KB = 128, 64
NROW, NCOL = 100, 200
NEWLINE = 7
DI = 2 * D
NS = 128
CT_X = DI // P
NCT = CT_X + 2
TAPS = 4
DF = 4 * D
HT = DF // P
NE = 4
EPS = 1e-5
SLOTS = NT + NE - 1
ROW = 2 * D + 4
NOBODY = 8192.0
DT0 = 2 * DI + 2 * NS
DTC, XBC0 = DI, DI + 2
NW = XBC0 + DI + 2 * NS


def build(nc, a, out):
    with ExitStack() as ctx:
        def sb(name, shape, dt=F32):
            return ctx.enter_context(nc.sbuf_tensor(name, shape, dt))

        def sem(name):
            return ctx.enter_context(nc.semaphore(name))

        sorted_rows = nc.dram_tensor("sorted_rows", [SLOTS * P, ROW], F32, kind="Internal").ap()
        ps = ctx.enter_context(nc.psum_tensor("ps", [P, 8, 512], F32))

        ident = sb("ident", [P, P])
        upto = sb("upto", [P, 1, P])
        before = sb("before", [P, P])
        after = sb("after", [P, P])
        ones = sb("ones", [P, P])
        part_i = sb("part_i", [P, 2], I32)
        part = sb("part", [P, 2])
        mhalf = sb("mhalf", [P, NT])
        d_diag = sb("d_diag", [P, 1, P])
        starts = sb("starts", [P, NT])
        slotno = sb("slotno", [P, 20])
        n1A = sb("n1A", [KA, 1])
        n1B = sb("n1B", [P, 1])
        convw = sb("convw", [P, NCT, TAPS])
        convb = sb("convb", [P, NCT])
        scal = sb("scal", [P, 4])
        wout = sb("wout", [P, CT_X, D])
        ssmn = sb("ssmn", [P, CT_X])
        m1r = sb("m1r", [P, 4, DF], F32R)
        stg0 = sb("stg0", [P, 2, DF])
        n2A = sb("n2A", [KA, 1])
        n2B = sb("n2B", [P, 1])
        m2 = sb("m2", [P, HT, D])
        wgA = sb("wgA", [KA, NE])
        wgB = sb("wgB", [KB, NE])
        bg = sb("bg", [P, NE])
        e2b = sb("e2b", [1, NE * D])
        h0 = sb("h0", [P, NT, D])
        stats = sb("stats", [P, TB, 6])
        mv = sb("mv", [P, NT, 2])
        var2 = sb("var2", [P, NB, 2, TB])
        rstd2 = sb("rstd2", [P, NB, 2, TB])
        nmr = sb("nmr", [P, NT])
        u = sb("u", [P, 2, TB, D])
        acc = sb("acc", [P, 3, S])
        xch = sb("xch", [P, 2, CT_X, S])
        BC = sb("BC", [P, NE * HT * D])
        BT = BC[:, 0:NT * P]
        CT = BC[:, NT * P:2 * NT * P]
        e2 = BC
        zs = sb("zs", [P, NT, DI])
        with ExitStack() as first:
            def early(name, shape, dt=F32):
                return first.enter_context(nc.sbuf_tensor(name, shape, dt))
            tok_i = early("tok_i", [NB, S], I32)
            count_i = early("count_i", [P, S], I32)
            count = early("count", [P, S])
            zeros = early("zeros", [NB, S])
            pick = early("pick", [NB, NB, P], BF16)
            newl = early("newl", [NB, 2, S])
            scanned = early("scanned", [NB, 2, S + 1])
            rc = early("rc", [NB, 2, S], BF16)
            bcb = early("bcb", [P, 2, 2, S], BF16)
            onehot = early("onehot", [P, 2, 3, S], BF16)
            tab = early("tab", [P, 3, DH])
            tabs = early("tabs", [P, 3, 3, DH], BF16)
        xB = sb("xB", [P, NT, S])
        with ExitStack() as first:
            winr = first.enter_context(nc.sbuf_tensor("winr", [P, 4, NW], F32R))
            uT = first.enter_context(nc.sbuf_tensor("uT", [P, 2, 3, S], F32R))
            empty = first.enter_context(nc.sbuf_tensor("empty", [P, ROW], F32))
        e1r = sb("e1r", [P, NE, 4, DF], F32R)
        e1f = e1r[:].rearrange("p e k h -> p (e k h)")
        dtr = sb("dtr", [P, NT])
        dtx = sb("dtx", [P, NT])
        dta = sb("dta", [P, NT])
        dte = sb("dte", [P, NT])
        dtl = sb("dtl", [P, NT])
        dt = sb("dt", [P, NT])
        decay = sb("decay", [P, NT])
        ssq = sb("ssq", [P, NT])
        ssq_e = sb("ssq_e", [P, NT])
        rr = sb("rr", [P, NT])
        def slot4(t, i):
            return t[:].rearrange("p a s -> p (a s)")[:, i * S:(i + 1) * S].rearrange("p (b t) -> p b t", b=NB)

        xchf = xch[:].rearrange("p a c s -> p (a c) s")
        uf = u[:].rearrange("p a t d -> p a (t d)")
        Av, E1 = slot4(acc, 0), slot4(acc, 1)
        LM, MT0 = slot4(acc, 2), slot4(uf, 0)
        E2 = (slot4(uf, 1), slot4(uf, 2))
        CE = (slot4(xchf, 0), slot4(xchf, 1))
        MT = (slot4(xchf, 2), slot4(xchf, 3))
        Bw = (slot4(xchf, 4), slot4(xchf, 5))
        junk = sb("junk", [P, DI], BF16)
        b1raw = stg0
        rawA = xchf.rearrange("p c s -> p (c s)")[:, 0:NW]
        rawB = xchf.rearrange("p c s -> p (c s)")[:, NW:2 * NW]
        wB = sb("wB", [P, 2, NB])
        state = sb("state", [P, NB, DI])
        x1 = state[:].rearrange("p b c -> p (b c)").rearrange("p (a t d) -> p a t d", a=2, t=TB)
        xBf = xB[:].rearrange("p t s -> p (t s)")
        res = xBf[:, NT * ROW:NT * ROW + 2 * TB * D].rearrange("p (a t d) -> p a t d", a=2, t=TB)
        resn = u
        with ExitStack() as first:
            stg1 = first.enter_context(nc.sbuf_tensor("stg1", [P, 2, DF], F32))
        stg = (stg0, stg1)
        rT = sb("rT", [P, 3, S], F32R)
        x2T = acc
        hT = xchf
        ssq2 = sb("ssq2", [P, NT])
        ssq2e = sb("ssq2e", [P, NT])
        rn = sb("rn", [P, NT])
        mv2 = sb("mv2", [P, NT, 2])
        var_e = sb("var_e", [P, NT])
        r2 = sb("r2", [P, NT])
        row = xBf[:, 0:NT * ROW].rearrange("p (t r) -> p t r", r=ROW)
        logit = sb("logit", [P, NT, NE])
        top = sb("top", [P, NT])
        F = sb("F", [P, NT, NE])
        free = sb("free", [P, NT])
        tmp16 = sb("tmp16", [P, NT])
        rank = sb("rank", [P, NT, NE])
        tot = sb("tot", [P, NE, NT + 1])
        zer64 = sb("zer64", [P, NT])
        ntile = sb("ntile", [P, NE, NT])
        need = sb("need", [P, NE])
        base = sb("base", [P, NE + 1])
        pos = sb("pos", [P, NT])
        posi = sb("posi", [P, NT], I32)
        eidf = sb("eidf", [P, 3, 20])
        eid = sb("eid", [P, 20], I32)
        h0f = h0[:].rearrange("p t d -> p (t d)")
        accf = acc[:].rearrange("p a s -> p (a s)")
        slot_x = accf[:, 0:2 * D].rearrange("p (a d) -> p a d", a=2)
        slot_h = accf[:, 2 * D:2 * D + 2 * (ROW - D)].rearrange("p (a d) -> p a d", a=2)
        yo = accf[:, 3 * S - 2 * D:3 * S].rearrange("p (a d) -> p a d", a=2)
        ids = sb("ids", [P, 2], I32)
        xTr = rT[:].rearrange("p a s -> p (a s)")[:, 0:8 * P].rearrange("p (a k t) -> p a k t", a=2, k=4)
        hid = h0f[:, 0:2 * DF].rearrange("p (a d) -> p a d", a=2)
        hidT = h0f[:, 2 * DF:4 * DF].rearrange("p (a d) -> p a d", a=2)
        junk2 = junk[:, 0:D]

        names = """ld_x ld_tab ld_in ld_conv ld_scal ld_out ld_m1 ld_e1_odd ld_e1_even ld_b1 ld_mlp ld_gate ld_e2
            consts pool_seq dve_seq act_seq tab_zero win_hi win_split folded_out m1_split e1_split b1_hi b1_lo b1_split
            ddiag_ready filled tokpos_ready tabs_ready idx_bc_ready bcb_ready onehot_ready h0_ready h0_copied
            var_ready rstd_ready u_ready uT_psum uT_copied uT_split xbc_psum tap_ready conv_done silu_done
            z_psum z_copied xtok_psum xtok_copied dt_abs dt_exp dt_done av_ready seg_psum g_psum e_ready ce_ready
            mt_ready bw_ready y_psum st_psum st_done gated ssq_done ssqe_ready rr_ready gT_psum gT_copied
            out_psum x1_ready res_ready ssq2_done ssq2e_ready rn_ready resn_ready rT_psum rT_copied rT_split
            w1_psum gelu_done w2_psum h1_done var2_ready r2_ready x2_ready x2T_psum x2T_copied gate_psum
            logit_ready f_ready rank_psum pos_ready eid_ready scattered loaded_even loaded_odd h1_even h1_odd
            stored_even stored_odd ids_ready xT_psum xT_copied xT_split hid_psum hid_ready hidT_psum hidT_copied
            y2_psum yo_ready""".split()
        s = {n: sem(n) for n in names}
        slot_loaded = (s["loaded_even"], s["loaded_odd"])
        h1_loaded = (s["h1_even"], s["h1_odd"])
        stored = (s["stored_even"], s["stored_odd"])
        block = ctx.enter_context(nc.Block())

        def bc_rows(ap1, n):
            return ap1.rearrange("(o n) -> o n", o=1).to_broadcast([P, n])

        @block.sync
        def _(sp):
            sp.dma_start(tok_i[:], a["x"]).then_inc(s["ld_x"], 16)
            sp.wait_ge(s["tab_zero"], 1)
            sp.dma_start(tab[0:NROW, 0, :], a["L0_tok_row_emb_W"]).then_inc(s["ld_tab"], 16)
            sp.dma_start(tab[:, 1, :], a["L0_tok_col_emb_W"][0:P, :]).then_inc(s["ld_tab"], 16)
            sp.dma_start(tab[0:NCOL - P, 2, :], a["L0_tok_col_emb_W"][P:NCOL, :]).then_inc(s["ld_tab"], 16)
            win = a["L0_attn_in_proj_W"]
            n1 = a["L0_attn_norm1_w"].rearrange("(p o) -> p o", o=1)
            for dst, norm, p0, k0, k1 in ((rawA, n1A, 0, 0, KA), (rawB, n1B, 0, KA, D), (rawB, n1B, KB, KA, D)):
                d = dst[p0:p0 + k1 - k0, :]
                sp.dma_start(d[:, 0:DI], win[k0:k1, 0:DI]).then_inc(s["ld_in"], 16)
                sp.dma_start(d[:, XBC0:NW], win[k0:k1, DI:DT0]).then_inc(s["ld_in"], 16)
                sp.dma_start(d[:, DTC:DTC + 1], win[k0:k1, DT0:DT0 + 1], allow_slow_non_contiguous=True).then_inc(s["ld_in"], 16)
                sp.dma_start(norm[p0:p0 + k1 - k0, :], n1[k0:k1, :]).then_inc(s["ld_in"], 16)
            sp.dma_start(convw[:], a["L0_attn_conv_w"].rearrange("(c p) k -> p c k", p=P)).then_inc(s["ld_conv"], 16)
            sp.dma_start(convb[:], a["L0_attn_conv_b"].rearrange("(c p) -> p c", p=P),
                         allow_slow_non_contiguous=True).then_inc(s["ld_conv"], 16)
            for i, n in enumerate(("L0_attn_dt_bias", "L0_attn_A_log", "L0_attn_D")):
                sp.dma_start(scal[:, i:i + 1], bc_rows(a[n], 1)).then_inc(s["ld_scal"], 16)
            sp.dma_start(wout[:], a["L0_attn_out_proj_W"].rearrange("(c p) d -> p c d", p=P)).then_inc(s["ld_out"], 16)
            sp.dma_start(ssmn[:], a["L0_attn_ssm_norm_w"].rearrange("(c p) -> p c", p=P),
                         allow_slow_non_contiguous=True).then_inc(s["ld_out"], 16)
            n2 = a["L0_attn_norm2_w"].rearrange("(p o) -> p o", o=1)

            def load_split(buf, w, signal):
                sp.dma_start(stg[buf][:, 0, :], w[0:KA, :]).then_inc(signal, 16)
                for p0 in (0, KB):
                    sp.dma_start(stg[buf][p0:p0 + KB, 1, :], w[KA:D, :]).then_inc(signal, 16)

            load_split(0, a["L0_attn_mlp_W1"], s["ld_m1"])
            sp.dma_start(n2A[:], n2[0:KA, :]).then_inc(s["ld_m1"], 16)
            for p0 in (0, KB):
                sp.dma_start(n2B[p0:p0 + KB, :], n2[KA:D, :]).then_inc(s["ld_m1"], 16)
            sp.dma_start(m2[:], a["L0_attn_mlp_W2"].rearrange("(c p) d -> p c d", p=P)).then_inc(s["ld_mlp"], 16)
            sp.dma_start(wgA[:], a["L0_ffn_Wg"][0:KA, :]).then_inc(s["ld_gate"], 16)
            sp.dma_start(wgB[:], a["L0_ffn_Wg"][KA:D, :]).then_inc(s["ld_gate"], 16)
            sp.dma_start(bg[:], bc_rows(a["L0_ffn_bg"], NE)).then_inc(s["ld_gate"], 16)
            sp.dma_start(e2b[:], a["L0_ffn_b2"].rearrange("(o e) h -> o (e h)", o=1)).then_inc(s["ld_e2"], 16)
            sp.wait_ge(s["consts"], 2)
            for j in range(SLOTS):
                sp.dma_start(sorted_rows[j * P:(j + 1) * P, :], empty[:]).then_inc(s["filled"], 16)
            load_split(1, a["L0_ffn_W1"][0], s["ld_e1_odd"])
            b1 = a["L0_ffn_b1"].rearrange("(o e) h -> o e h", o=1)
            sp.wait_ge(s["m1_split"], 1)
            load_split(0, a["L0_ffn_W1"][1], s["ld_e1_even"])
            sp.wait_ge(s["e1_split"], 1)
            load_split(1, a["L0_ffn_W1"][2], s["ld_e1_odd"])
            sp.wait_ge(s["e1_split"], 2)
            load_split(0, a["L0_ffn_W1"][3], s["ld_e1_even"])
            sp.wait_ge(s["ce_ready"], TB)
            sp.wait_ge(s["g_psum"], TB)
            for e in range(NE):
                sp.dma_start(e2[:, e * HT * D:(e + 1) * HT * D].rearrange("p (c d) -> p c d", c=HT),
                             a["L0_ffn_W2"][e].rearrange("(c p) d -> p c d", p=P)).then_inc(s["ld_e2"], 16)
            sp.wait_ge(s["e1_split"], NE)
            for i in range(NE // 2):
                if i:
                    sp.wait_ge(s["b1_split"], i)
                for p0 in range(2):
                    sp.dma_start(b1raw[KB + p0:KB + p0 + 1], b1[:, 2 * i:2 * i + 2]).then_inc(s["ld_b1"], 16)
            sp.wait_ge(s["scattered"], 16 * NT)

            def load_x2(h, par, early=False):
                if not early:
                    sp.wait_ge(s["xT_psum"], h * 2 + par - 1)
                sp.dma_start(slot_x[:, par, :], sorted_rows[bass.ds((h * 2 + par) * P, P), 0:D]
                             ).then_inc(slot_loaded[par], 16)

            def load_h1(h, par, early=False):
                if not early:
                    sp.wait_ge(s["yo_ready"], h * 2 + par - 1)
                    sp.wait_ge(s["ids_ready"], h * 2 + par - 1)
                sp.dma_start(slot_h[:, par, :], sorted_rows[bass.ds((h * 2 + par) * P, P), D:ROW]
                             ).then_inc(h1_loaded[par], 16)

            for par in range(2):
                load_x2(0, par, True)
                load_h1(0, par, True)
            load_x2(1, 0)
            load_x2(1, 1)
            with sp.Fori(1, (SLOTS - 1) // 2 - 1) as i:
                for par in range(2):
                    load_x2(i + 1, par)
                    load_h1(i, par)
            last = (SLOTS - 1) // 2
            load_x2(last, 0)
            load_h1(last - 1, 0)
            load_h1(last - 1, 1)
            load_h1(last, 0)

        @block.gpsimd
        def _(pool):
            g = nc.gpsimd
            n = [0]

            def link(ins):
                n[0] += 1
                ins.then_inc(s["pool_seq"], 1)
                pool.wait_ge(s["pool_seq"], n[0])

            link(g.iota(count_i[:], [[1, S]], base=1, channel_multiplier=0))
            g.memset(pick[:], 1.0)
            g.memset(zeros[:], 0.0)
            g.iota(part_i[:], [[P, 2]], base=0, channel_multiplier=1)
            link(g.tensor_copy(count[:], count_i[:]))
            g.tensor_copy(part[:], part_i[:])
            g.affine_select(out=pick[:], in_=pick[:], compare_op=ALU.is_equal, fill=0.0, base=0,
                            pattern=[[-1, NB], [0, P]], channel_multiplier=1).then_inc(s["consts"], 1)
            g.memset(ones[:], 1.0)
            g.memset(mhalf[:], -0.5)
            g.memset(empty[:], 0.0)
            g.memset(zer64[:], 0.0)
            link(g.memset(upto[:], 1.0))
            g.affine_select(out=ident[:], in_=ones[:], compare_op=ALU.is_equal, fill=0.0, base=0,
                            pattern=[[-1, P]], channel_multiplier=1)
            g.affine_select(out=before[:], in_=ones[:], compare_op=ALU.is_ge, fill=0.0, base=-1,
                            pattern=[[1, P]], channel_multiplier=-1)
            g.affine_select(out=after[:], in_=ones[:], compare_op=ALU.is_ge, fill=0.0, base=-1,
                            pattern=[[-1, P]], channel_multiplier=1)
            g.tensor_scalar(slotno[:], count[:, 0:20], -1.0, None, ALU.add)
            g.tensor_scalar(starts[:], count[:, 0:NT], float(P), -float(P), ALU.mult, ALU.add)
            g.affine_select(out=upto[:], in_=upto[:], compare_op=ALU.is_ge, fill=0.0, base=0,
                            pattern=[[0, 1], [1, P]], channel_multiplier=-1)
            g.memset(empty[:, 2 * D:2 * D + 1], NOBODY).then_inc(s["consts"], 1)
            for b in range(NB):
                pool.wait_ge(s["var_ready"], b + 1)
                g.tensor_tensor(rstd2[:, b], var2[:, b], mhalf[:, 0:2 * TB].rearrange("p (a t) -> p a t", a=2),
                                ALU.pow).then_inc(s["rstd_ready"], 1)
            pool.wait_ge(s["ld_m1"], 6 * 16)
            g.tensor_scalar(stg0[:, 0, :], stg0[:, 0, :], n2A[:, 0:1], None, ALU.mult)
            link(g.tensor_scalar(stg0[:, 1, :], stg0[:, 1, :], n2B[:, 0:1], None, ALU.mult))

            def split(raw, dst):
                g.tensor_copy(dst[:, 0, :], raw[:, 0, :])
                link(g.tensor_copy(dst[:, 2, :], raw[:, 1, :]))
                g.tensor_tensor(dst[:, 1, :], raw[:, 0, :], dst[:, 0, :].bitcast(F32), ALU.subtract)
                return g.tensor_tensor(dst[0:KB, 3, :], raw[0:KB, 1, :], dst[0:KB, 2, :].bitcast(F32), ALU.subtract)

            split(stg0, m1r).then_inc(s["m1_split"], 1)
            pool.wait_ge(s["ld_out"], 32)
            for c in range(CT_X):
                last = g.tensor_scalar(wout[:, c, :], wout[:, c, :], ssmn[:, c:c + 1], None, ALU.mult)
            last.then_inc(s["folded_out"], 1)
            pool.wait_ge(s["ld_scal"], 48)
            g.tensor_scalar(d_diag[:, 0, :], ident[:], scal[:, 2:3], None, ALU.mult).then_inc(s["ddiag_ready"], 1)
            pool.wait_ge(s["filled"], 16 * SLOTS)
            pool.wait_ge(s["xbc_psum"], NB * NCT)
            pool.wait_ge(s["z_psum"], NT)

            def split_expert(e):
                q = (e + 1) % 2
                pool.wait_ge(s[("ld_e1_even", "ld_e1_odd")[q]], 48 * (e // 2 + 1))
                split(stg[q], e1r[:, e]).then_inc(s["e1_split"], 1)

            def pow_gate(c):
                pool.wait_ge(s["ssqe_ready"], c + 1)
                v = lambda t: t[:].rearrange("p (b c) -> p b c", b=NB)[:, :, c]
                g.tensor_tensor(v(rr), v(ssq_e), mhalf[:, 0:NB], ALU.pow).then_inc(s["rr_ready"], 1)

            split_expert(0)
            split_expert(1)
            pow_gate(0)
            split_expert(2)
            pow_gate(1)
            split_expert(3)
            pow_gate(2)
            pow_gate(3)

            def pow_res(b):
                pool.wait_ge(s["ssq2e_ready"], b + 1)
                g.tensor_tensor(rn[:, b * TB:(b + 1) * TB], ssq2e[:, b * TB:(b + 1) * TB], mhalf[:, 0:TB],
                                ALU.pow).then_inc(s["rn_ready"], 1)

            pow_res(0)
            pow_res(1)
            for b in range(NB):
                if b + 2 < NB:
                    pow_res(b + 2)
                pool.wait_ge(s["var2_ready"], b + 1)
                g.tensor_tensor(r2[:, b * TB:(b + 1) * TB], var_e[:, b * TB:(b + 1) * TB], mhalf[:, 0:TB],
                                ALU.pow).then_inc(s["r2_ready"], 1)
            pool.wait_ge(s["pos_ready"], 1)
            pool.wait_ge(s["x2_ready"], NB)
            pool.wait_ge(s["filled"], 16 * SLOTS)
            for m in range(NT):
                g.indirect_dma_start(out=sorted_rows, out_offset=bass.IndirectOffsetOnAxis(posi[:, m:m + 1], 0),
                                     in_=row[:, m, :], in_offset=None).then_inc(s["scattered"], 16)
            last_token = pool.to_reg(NB * S - 1)
            for j in range(SLOTS):
                pool.wait_ge(s["yo_ready"], j + 1)
                pool.wait_ge(s["ids_ready"], j + 1)
                g.indirect_dma_start(out=out, out_offset=bass.IndirectOffsetOnAxis(ids[:, j % 2:j % 2 + 1], 0),
                                     in_=yo[:, j % 2, :], in_offset=None, bounds_check=last_token,
                                     oob_is_err=False).then_inc(stored[j % 2], 16)
            pool.wait_ge(stored[0], 16 * ((SLOTS + 1) // 2))
            pool.wait_ge(stored[1], 16 * (SLOTS // 2))

        @block.scalar
        def _(act):
            A = nc.scalar

            def bc_copy(b):
                act.wait_ge(s["idx_bc_ready"], b + 1)
                if b >= 2:
                    act.wait_ge(s["onehot_ready"], b - 1)
                A.copy(bcb[:, b % 2], ps[:, 2 * (b % 2):2 * (b % 2) + 2, :]).then_inc(s["bcb_ready"], 1)

            def h0_copy(n):
                act.wait_ge(s["h0_ready"], n + 1)
                A.copy(h0[:, 2 * n:2 * n + 2, :], ps[:, 4 + n % 2, 0:2 * D].rearrange("p (a d) -> p a d", a=2)
                       ).then_inc(s["h0_copied"], 1)

            bc_copy(0)
            act.wait_ge(s["ld_in"], 12 * 16)
            act.wait_ge(s["tokpos_ready"], 1)
            A.activation(winr[:, 0, :], rawA, ACT.Identity, scale=n1A[:, 0:1])
            A.activation(winr[:, 2, :], rawB, ACT.Identity, scale=n1B[:, 0:1]).then_inc(s["win_hi"], 1)
            bc_copy(1)
            for b in range(NB):
                h0_copy(2 * b)
                h0_copy(2 * b + 1)
                if b + 2 < NB:
                    bc_copy(b + 2)
            act.wait_ge(s["ld_conv"], 32)

            def tap(n):
                act.wait_ge(s["xbc_psum"], n + 1)
                if n >= 3:
                    act.wait_ge(s["silu_done"], n - 2)
                A.activation(acc[:, n % 3, :], ps[:, n % 3, :], ACT.Identity, bias=convb[:, n % NCT:n % NCT + 1],
                             scale=convw[:, n % NCT, TAPS - 1:TAPS]).then_inc(s["tap_ready"], 1)

            def silu(n):
                b, c = divmod(n, NCT)
                act.wait_ge(s["conv_done"], n + 1)
                if c == 0 and b >= 2:
                    act.wait_ge(s["xtok_psum"], (b - 1) * TB)
                if n == 0:
                    act.wait_ge(s["win_split"], 1)
                dst = xch[:, b % 2, c, :] if c < CT_X else (BT, CT)[c - CT_X][:, b * S:(b + 1) * S]
                A.activation(dst, acc[:, n % 3, :], ACT.Silu).then_inc(s["silu_done"], 1)

            def xtok(b):
                for m in range(b * TB, (b + 1) * TB):
                    act.wait_ge(s["xtok_psum"], m + 1)
                    A.copy(xB[:, m, :], ps[:, 5, :]).then_inc(s["xtok_copied"], 1)

            def u_hi(b):
                act.wait_ge(s["uT_psum"], b + 1)
                if b >= 2:
                    act.wait_ge(s["z_psum"], (b - 1) * TB)
                A.copy(uT[:, b % 2, 0, :], ps[:, 6, :])
                A.copy(uT[0:KB, b % 2, 2, :], ps[0:KB, 7, :]).then_inc(s["uT_copied"], 1)

            u_hi(0)
            for b in range(NB):
                tap(b * NCT)
                for c in range(1, NCT):
                    tap(b * NCT + c)
                    silu(b * NCT + c - 1)
                if b + 1 < NB:
                    u_hi(b + 1)
                for m in range(b * TB, (b + 1) * TB):
                    act.wait_ge(s["z_psum"], m + 1)
                    A.activation(zs[:, m, :], ps[:, 3 + m % 2, 0:DI], ACT.Silu)
                    A.copy(dtr[:, m:m + 1], ps[:, 3 + m % 2, DTC:DTC + 1]).then_inc(s["z_copied"], 1)
                silu(b * NCT + NCT - 1)
                if b:
                    xtok(b - 1)
            act.wait_ge(s["dt_abs"], 1)
            A.activation(dte[:], dta[:], ACT.Exp, scale=-1.0).then_inc(s["act_seq"], 1)
            A.activation(scal[:, 3:4], scal[:, 1:2], ACT.Exp).then_inc(s["act_seq"], 1)
            act.wait_ge(s["act_seq"], 2)
            A.activation(dtl[:], dte[:], ACT.Ln, bias=1.0).then_inc(s["dt_exp"], 1)
            xtok(NB - 1)

            def decays(c):
                act.wait_ge(s["seg_psum"], c + 1)
                if c:
                    act.wait_ge(s["ce_ready"], c)
                if c >= 2:
                    act.wait_ge(s["st_done"], NB * (c - 1))
                A.activation(E1, ps[:, 0, :].rearrange("p (b t) -> p b t", b=NB), ACT.Exp)
                A.activation(E2[c % 2], ps[:, 1, :].rearrange("p (b t) -> p b t", b=NB), ACT.Exp
                             ).then_inc(s["e_ready"], 1)

            def square(k):
                c, b = divmod(k, NB)
                m = b * TB + c
                act.wait_ge(s["gated"], k + 1)
                if k:
                    act.wait_ge(s["ssq_done"], k)
                A.activation(junk[:, 0:DI], zs[:, m, :], ACT.Square, accum_out=ssq[:, m:m + 1]
                             ).then_inc(s["ssq_done"], 1)

            def keep_turned(k):
                c, b = divmod(k, NB)
                act.wait_ge(s["gT_psum"], k + 1)
                act.wait_ge(s["ssq_done"], k + 1)
                A.copy(zs[:, b * TB + c, :], ps[:, 7, 0:DI]).then_inc(s["gT_copied"], 1)

            decays(0)
            for c in range(TB):
                if c + 1 < TB:
                    decays(c + 1)
                for b in range(NB):
                    square(c * NB + b)
                    if c:
                        keep_turned((c - 1) * NB + b)
            for b in range(NB):
                keep_turned((TB - 1) * NB + b)

            def first_norm_again(b):
                act.wait_ge(s["st_done"], NB * (TB - 1))
                act.wait_ge(s["y_psum"], NT)
                if b >= 2:
                    act.wait_ge(s["res_ready"], (b - 1) * TB)
                for t in range(TB):
                    m = b * TB + t
                    last = A.activation(x1[:, b % 2, t, :], h0[:, m, :], ACT.Identity, bias=nmr[:, m:m + 1],
                                        scale=rstd2[:, b, 0, t:t + 1])
                last.then_inc(s["x1_ready"], 1)

            def square_res(b):
                for m in range(b * TB, (b + 1) * TB):
                    act.wait_ge(s["res_ready"], m + 1)
                    if m:
                        act.wait_ge(s["ssq2_done"], m)
                    else:
                        act.wait_ge(s["ssq_done"], NT)
                    A.activation(junk2, res[:, b % 2, m % TB, :], ACT.Square, accum_out=ssq2[:, m:m + 1]
                                 ).then_inc(s["ssq2_done"], 1)

            def r_hi(b):
                act.wait_ge(s["rT_psum"], b + 1)
                if b:
                    act.wait_ge(s["w1_psum"], b * HT)
                else:
                    act.wait_ge(s["e1_split"], NE)
                A.copy(rT[:, 0, :], ps[:, 2, :])
                A.copy(rT[0:KB, 2, :], ps[0:KB, 3, :]).then_inc(s["rT_copied"], 1)

            def x2_turned(b):
                act.wait_ge(s["x2T_psum"], b + 1)
                if b:
                    act.wait_ge(s["gate_psum"], b)
                A.copy(x2T[:, 0, :], ps[:, 2, :])
                A.copy(x2T[0:KB, 1, :], ps[0:KB, 3, :]).then_inc(s["x2T_copied"], 1)

            first_norm_again(0)
            first_norm_again(1)
            square_res(0)
            square_res(1)
            r_hi(0)
            for b in range(NB):
                for n in range(b * HT, (b + 1) * HT):
                    act.wait_ge(s["w1_psum"], n + 1)
                    if b and n % HT == 0:
                        act.wait_ge(s["w2_psum"], b * TB)
                    A.activation(hT[:, n % HT, :], ps[:, 4 + n % 2, :], ACT.Gelu).then_inc(s["gelu_done"], 1)
                if b + 2 < NB:
                    first_norm_again(b + 2)
                    square_res(b + 2)
                if b + 1 < NB:
                    r_hi(b + 1)
                if b:
                    x2_turned(b - 1)
                if b < NE // 2:
                    act.wait_ge(s["ld_b1"], 32 * (b + 1))
                    A.copy(e1r[KB:KB + 2, 2 * b:2 * b + 2, 3, :], b1raw[KB:KB + 2]).then_inc(s["b1_hi"], 1)
                    act.wait_ge(s["b1_lo"], b + 1)
                    A.copy(e1r[KB:KB + 1, 2 * b:2 * b + 2, 3, :], b1raw[KB:KB + 1]).then_inc(s["b1_split"], 1)
            x2_turned(NB - 1)

            def turn(j, par):
                act.wait_ge(s["xT_psum"], j + 1)
                A.copy(xTr[:, par, 0, :], ps[:, 0, 0:P])
                A.copy(xTr[0:KB, par, 2, :], ps[0:KB, 0, P:2 * P])
                A.copy(xTr[0:KB, par, 3, :], ps[0:KB, 0, P:2 * P]).then_inc(s["xT_copied"], 1)

            def gelu(j, par):
                act.wait_ge(s["hid_psum"], j + 1)
                A.activation(hid[:, par, :], ps[:, 1 + 2 * par:3 + 2 * par, :].rearrange("p a s -> p (a s)")[:, 0:DF],
                             ACT.Gelu).then_inc(s["hid_ready"], 1)

            turn(0, 0)
            turn(1, 1)
            gelu(0, 0)
            turn(2, 0)
            gelu(1, 1)
            with act.Fori(0, (SLOTS - 3) // 2) as i:
                for par in range(2):
                    j = i * 2 + par
                    turn(j + 3, 1 - par)
                    act.wait_ge(s["hidT_psum"], j + 1)
                    gelu(j + 2, par)
            gelu(SLOTS - 1, 0)

        @block.vector
        def _(dve):
            V = nc.vector
            n = [0]

            def link(ins):
                n[0] += 1
                ins.then_inc(s["dve_seq"], 1)
                dve.wait_ge(s["dve_seq"], n[0])

            V.memset(tab[:], 0.0).then_inc(s["tab_zero"], 1)
            V.memset(winr[KB:P, 3, :].bitcast(F32), 0.0)
            V.memset(m1r[KB:P, 3, :].bitcast(F32), 0.0)
            V.memset(rawA[:, DTC + 1:DTC + 2], 0.0)
            V.memset(rawB[:, DTC + 1:DTC + 2], 0.0)
            V.memset(scanned[:, :, 0:1], 0.0)
            dve.wait_ge(s["ld_x"], 16)
            dve.wait_ge(s["consts"], 1)
            link(V.tensor_copy(newl[:, 1, :], tok_i[:]))
            link(V.tensor_scalar(newl[:, 0, :], newl[:, 1, :], float(NEWLINE), None, ALU.is_equal))
            link(V.tensor_tensor(newl[:, 1, :], newl[:, 0, :], count[0:NB, :], ALU.mult))
            V.tensor_tensor_scan(scanned[:, 0, 1:S + 1], newl[:, 0, :], zeros[:], 0.0, ALU.add, ALU.add)
            link(V.tensor_tensor_scan(scanned[:, 1, 1:S + 1], newl[:, 1, :], zeros[:], 0.0, ALU.max, ALU.max))
            V.tensor_scalar(rc[:, 0, :], scanned[:, 0, 0:S], float(NROW - 1), None, ALU.min)
            link(V.scalar_tensor_tensor(newl[:, 0, :], count[0:NB, :], 1.0, scanned[:, 1, 0:S],
                                        ALU.subtract, ALU.subtract))
            V.tensor_scalar(rc[:, 1, :], newl[:, 0, :], float(NCOL - 1), None, ALU.min).then_inc(s["tokpos_ready"], 1)
            dve.wait_ge(s["ld_tab"], 48)
            link(V.tensor_copy(tabs[:, 0], tab[:]))
            link(V.tensor_tensor(tab[:], tab[:], tabs[:, 0], ALU.subtract))
            link(V.tensor_copy(tabs[:, 1], tab[:]))
            V.tensor_tensor(tabs[:, 2], tab[:], tabs[:, 1], ALU.subtract).then_inc(s["tabs_ready"], 1)

            def one_hot(b):
                q = b % 2
                dve.wait_ge(s["bcb_ready"], b + 1)
                if b >= 2:
                    dve.wait_ge(s["h0_ready"], 2 * (b - 1))
                V.tensor_scalar(onehot[:, q, 0, :], bcb[:, q, 0, :], part[:, 0:1], None, ALU.is_equal)
                V.tensor_scalar(onehot[:, q, 1, :], bcb[:, q, 1, :], part[:, 0:1], None, ALU.is_equal)
                V.tensor_scalar(onehot[:, q, 2, :], bcb[:, q, 1, :], part[:, 1:2], None, ALU.is_equal
                                ).then_inc(s["onehot_ready"], 1)

            def norm_stats(src, b, dst):
                for t in range(TB):
                    last = V.bn_stats(stats[:, t, :], src[:, b * TB + t, :])
                link(last)
                for t in range(TB):
                    last = V.bn_aggr(dst[:, b * TB + t, :], stats[:, t, :])
                link(last)

            def first_stats(b):
                dve.wait_ge(s["h0_copied"], 2 * b + 2)
                norm_stats(h0, b, mv)
                v = mv[:, b * TB:(b + 1) * TB, 1]
                V.tensor_scalar(var2[:, b, 0, :], v, EPS, None, ALU.add)
                V.tensor_scalar(var2[:, b, 1, :], v, 1.0 + EPS, EPS * EPS, ALU.mult, ALU.add
                                ).then_inc(s["var_ready"], 1)

            def first_norm(b):
                dve.wait_ge(s["rstd_ready"], b + 1)
                V.scalar_tensor_tensor(nmr[:, b * TB:(b + 1) * TB], mv[:, b * TB:(b + 1) * TB, 0], -1.0,
                                       rstd2[:, b, 0, :], ALU.mult, ALU.mult)
                if b >= 2:
                    dve.wait_ge(s["uT_psum"], b - 1)
                for t in range(TB):
                    m = b * TB + t
                    last = V.tensor_scalar(u[:, b % 2, t, :], h0[:, m, :], mv[:, m, 0:1], rstd2[:, b, 1, t:t + 1],
                                           ALU.subtract, ALU.mult)
                last.then_inc(s["u_ready"], 1)

            def u_lo(b):
                q = b % 2
                dve.wait_ge(s["uT_copied"], b + 1)
                V.tensor_tensor(uT[:, q, 1, :], ps[:, 6, :], uT[:, q, 0, :].bitcast(F32), ALU.subtract)
                V.tensor_tensor(uT[KB:P, q, 2, :], ps[0:KB, 7, :], uT[0:KB, q, 2, :].bitcast(F32), ALU.subtract
                                ).then_inc(s["uT_split"], 1)

            def conv(n):
                dve.wait_ge(s["tap_ready"], n + 1)
                for k in range(TAPS - 2, -1, -1):
                    d = TAPS - 1 - k
                    ins = V.scalar_tensor_tensor(acc[:, n % 3, d:S], ps[:, n % 3, 0:S - d],
                                                 convw[:, n % NCT, k:k + 1], acc[:, n % 3, d:S], ALU.mult, ALU.add)
                    if k:
                        link(ins)
                ins.then_inc(s["conv_done"], 1)

            one_hot(0)
            one_hot(1)
            dve.wait_ge(s["win_hi"], 1)
            V.scalar_tensor_tensor(winr[:, 1, :], rawA, n1A[:, 0:1], winr[:, 0, :].bitcast(F32), ALU.mult,
                                   ALU.subtract)
            V.scalar_tensor_tensor(winr[0:KB, 3, :], rawB[0:KB, :], n1B[0:KB, 0:1], winr[0:KB, 2, :].bitcast(F32),
                                   ALU.mult, ALU.subtract).then_inc(s["win_split"], 1)
            first_stats(0)
            one_hot(2)
            one_hot(3)
            first_stats(1)
            first_norm(0)
            first_stats(2)
            first_norm(1)
            u_lo(0)
            first_stats(3)
            for b in range(NB):
                for c in range(NCT):
                    conv(b * NCT + c)
                    if c == 1 and b + 2 < NB:
                        first_norm(b + 2)
                    if c == 3 and b + 1 < NB:
                        u_lo(b + 1)
            dve.wait_ge(s["z_copied"], NT)
            dve.wait_ge(s["ld_scal"], 48)
            link(V.tensor_scalar(dtx[:], dtr[:], scal[:, 0:1], None, ALU.add))
            link(V.tensor_scalar(dta[:], dtx[:], -1.0, None, ALU.mult))
            V.tensor_tensor(dta[:], dta[:], dtx[:], ALU.max).then_inc(s["dt_abs"], 1)
            dve.wait_ge(s["dt_exp"], 1)
            link(V.scalar_tensor_tensor(dt[:], dtx[:], 0.0, dtl[:], ALU.max, ALU.add))
            link(V.tensor_scalar(decay[:], dt[:], scal[:, 3:4], -1.0, ALU.mult, ALU.mult))

            dtg = dt[:].rearrange("p (b c) -> p b c", b=NB)
            CTg = CT.rearrange("p (b c t) -> p b c t", b=NB, c=TB)
            dve.wait_ge(s["silu_done"], NB * NCT)
            dve.wait_ge(s["xtok_psum"], NT)
            dve.wait_ge(s["ddiag_ready"], 1)

            def segments(c):
                if c:
                    dve.wait_ge(s["seg_psum"], c)
                for b in range(NB):
                    m = b * TB + c
                    last = V.tensor_scalar(Av[:, b, :], upto[:, 0, :], decay[:, m:m + 1], None, ALU.mult)
                last.then_inc(s["av_ready"], 1)

            def prepare_decays(c):
                q = c % 2
                dve.wait_ge(s["e_ready"], c + 1)
                V.tensor_tensor(LM, E1, upto[:].to_broadcast([P, NB, P]), ALU.mult)
                link(V.tensor_tensor(wB[:, q, :], E1[:, :, P - 1], dtg[:, :, c], ALU.mult))
                if c >= 2:
                    dve.wait_ge(s["y_psum"], (c - 1) * NB)
                V.tensor_tensor(CE[q], CTg[:, :, c, :], E2[q], ALU.mult).then_inc(s["ce_ready"], 1)

            def prepare_mask(c):
                dve.wait_ge(s["g_psum"], c + 1)
                for b in range(NB):
                    m = b * TB + c
                    last = V.scalar_tensor_tensor(MT0[:, b, :], ps[:, 2, b * P:(b + 1) * P], dt[:, m:m + 1],
                                                  LM[:, b, :], ALU.mult, ALU.mult)
                link(last)
                V.tensor_tensor(MT[c % 2], MT0, d_diag[:].to_broadcast([P, NB, P]), ALU.add).then_inc(s["mt_ready"], 1)

            def prepare_state(c):
                q = c % 2
                if c >= TB - 1:
                    return
                if c >= 2:
                    dve.wait_ge(s["st_psum"], (c - 1) * NB)
                dve.wait_ge(s["xtok_copied"], NT)
                for b in range(NB):
                    last = V.tensor_scalar(Bw[q][:, b, :], xB[:, b * TB + c, DI:S], wB[:, q, b:b + 1], None, ALU.mult)
                last.then_inc(s["bw_ready"], 1)
                segments(c + 1)

            def gate_and_state(c, b):
                m = b * TB + c
                k = c * NB + b
                dve.wait_ge(s["y_psum"], k + 1)
                V.tensor_tensor(zs[:, m, :], ps[:, 3 + b % 2, 0:DI], zs[:, m, :], ALU.mult
                                ).then_inc(s["gated"], 1)
                if c == TB - 1:
                    return
                dve.wait_ge(s["st_psum"], k + 1)
                if c == 0:
                    V.tensor_copy(state[:, b, :], ps[:, 5 + b % 2, 0:DI]).then_inc(s["st_done"], 1)
                else:
                    V.scalar_tensor_tensor(state[:, b, :], state[:, b, :], E2[c % 2][:, b, P - 1:P],
                                           ps[:, 5 + b % 2, 0:DI], ALU.mult, ALU.add).then_inc(s["st_done"], 1)

            def gate_factors(c):
                dve.wait_ge(s["ssq_done"], (c + 1) * NB)
                v = lambda t: t[:].rearrange("p (b c) -> p b c", b=NB)[:, :, c]
                V.tensor_scalar(v(ssq_e), v(ssq), 1.0 / DI, EPS, ALU.mult, ALU.add).then_inc(s["ssqe_ready"], 1)

            segments(0)
            prepare_decays(0)
            prepare_mask(0)
            prepare_state(0)
            for c in range(TB):
                gate_and_state(c, 0)
                if c + 1 < TB:
                    prepare_decays(c + 1)
                gate_and_state(c, 1)
                if c + 1 < TB:
                    prepare_mask(c + 1)
                gate_and_state(c, 2)
                if c + 1 < TB:
                    prepare_state(c + 1)
                if c:
                    gate_factors(c - 1)
                gate_and_state(c, 3)
            gate_factors(TB - 1)
            dve.wait_ge(s["rr_ready"], TB)

            def residual(b):
                dve.wait_ge(s["x1_ready"], b + 1)
                for m in range(b * TB, (b + 1) * TB):
                    dve.wait_ge(s["out_psum"], m + 1)
                    V.scalar_tensor_tensor(res[:, b % 2, m % TB, :], ps[:, m % 2, 0:D], rr[:, m:m + 1],
                                           x1[:, b % 2, m % TB, :], ALU.mult, ALU.add).then_inc(s["res_ready"], 1)

            def res_stats(b):
                dve.wait_ge(s["ssq2_done"], (b + 1) * TB)
                q = slice(b * TB, (b + 1) * TB)
                V.tensor_scalar(ssq2e[:, q], ssq2[:, q], 1.0 / D, EPS, ALU.mult, ALU.add
                                ).then_inc(s["ssq2e_ready"], 1)

            def res_scaled(b):
                dve.wait_ge(s["rn_ready"], b + 1)
                if b >= 2:
                    dve.wait_ge(s["rT_psum"], b - 1)
                for m in range(b * TB, (b + 1) * TB):
                    last = V.tensor_scalar(resn[:, b % 2, m % TB, :], res[:, b % 2, m % TB, :], rn[:, m:m + 1], None,
                                           ALU.mult)
                last.then_inc(s["resn_ready"], 1)

            def r_lo(b):
                dve.wait_ge(s["rT_copied"], b + 1)
                V.tensor_tensor(rT[:, 1, :], ps[:, 2, :], rT[:, 0, :].bitcast(F32), ALU.subtract)
                V.tensor_tensor(rT[KB:P, 2, :], ps[0:KB, 3, :], rT[0:KB, 2, :].bitcast(F32), ALU.subtract
                                ).then_inc(s["rT_split"], 1)

            def second_stats(b):
                q = slice(b * TB, (b + 1) * TB)
                for m in range(b * TB, (b + 1) * TB):
                    dve.wait_ge(s["w2_psum"], m + 1)
                    last = V.tensor_tensor(row[:, m, D:2 * D], ps[:, 6 + m % 2, 0:D], h0[:, m, :], ALU.add)
                    last.then_inc(s["h1_done"], 1)
                dve.wait_ge(s["h1_done"], (b + 1) * TB)
                norm_stats(row[:, :, D:2 * D], b, mv2)
                V.tensor_scalar(var_e[:, q], mv2[:, q, 1], EPS, None, ALU.add).then_inc(s["var2_ready"], 1)

            def second_norm(b):
                dve.wait_ge(s["r2_ready"], b + 1)
                for m in range(b * TB, (b + 1) * TB):
                    V.memset(row[:, m, 2 * D + 1:ROW], 0.0)
                    V.tensor_scalar(row[:, m, 2 * D:2 * D + 1], part[:, 0:1], float(m * P), None, ALU.add)
                    last = V.tensor_scalar(row[:, m, 0:D], row[:, m, D:2 * D], mv2[:, m, 0:1], r2[:, m:m + 1],
                                           ALU.subtract, ALU.mult)
                last.then_inc(s["x2_ready"], 1)

            def logits(b):
                dve.wait_ge(s["gate_psum"], b + 1)
                for t in range(TB):
                    last = V.tensor_tensor(logit[:, b * TB + t, :], ps[:, 2, NE * t:NE * (t + 1)], bg[:], ALU.add)
                last.then_inc(s["logit_ready"], 1)

            dve.wait_ge(s["ld_gate"], 48)
            residual(0)
            res_stats(0)
            residual(1)
            res_scaled(0)
            res_stats(1)
            r_lo(0)
            for b in range(NB):
                if b + 2 < NB:
                    residual(b + 2)
                if b + 1 < NB:
                    res_scaled(b + 1)
                if b + 2 < NB:
                    res_stats(b + 2)
                if b:
                    second_norm(b - 1)
                if b + 1 < NB:
                    r_lo(b + 1)
                if b:
                    logits(b - 1)
                if b < NE // 2:
                    dve.wait_ge(s["b1_hi"], b + 1)
                    b1part = e1r[KB:KB + 2, 2 * b:2 * b + 2, 3, :]
                    V.tensor_tensor(b1part, b1raw[KB:KB + 2], b1part.bitcast(F32), ALU.subtract
                                    ).then_inc(s["b1_lo"], 1)
                second_stats(b)
            second_norm(NB - 1)
            logits(NB - 1)
            dve.wait_ge(s["logit_ready"], NB)
            link(V.tensor_reduce(top[:], logit[:], AX.X, ALU.max))
            for e in range(NE):
                link(V.tensor_tensor(tmp16[:], logit[:, :, e], top[:], ALU.is_equal))
                if e == 0:
                    V.tensor_copy(F[:, :, e], tmp16[:])
                    link(V.tensor_scalar(free[:], tmp16[:], -1.0, 1.0, ALU.mult, ALU.add))
                else:
                    link(V.tensor_tensor(F[:, :, e], tmp16[:], free[:], ALU.mult))
                    link(V.tensor_tensor(free[:], free[:], F[:, :, e], ALU.subtract))
            V.memset(tot[:, :, 0:1], 0.0).then_inc(s["f_ready"], 1)
            dve.wait_ge(s["rank_psum"], 1)
            V.tensor_copy(rank[:], ps[:, 0, 0:NT * NE].rearrange("p (t e) -> p t e", e=NE))
            for e in range(NE):
                last = V.tensor_tensor_scan(tot[:, e, 1:NT + 1],
                                            ps[:, 1, 0:NT * NE].rearrange("p (t e) -> p t e", e=NE)[:, :, e],
                                            zer64[:], 0.0, ALU.add, ALU.add)
            link(last)
            for e in range(NE):
                last = V.tensor_scalar(ntile[:, e, :], starts[:], tot[:, e, NT:NT + 1], None, ALU.is_lt)
            link(last)
            V.memset(base[:, 0:1], 0.0)
            link(V.tensor_reduce(need[:], ntile[:], AX.X, ALU.add))
            for e in range(NE):
                link(V.tensor_tensor(base[:, e + 1:e + 2], base[:, e:e + 1], need[:, e:e + 1], ALU.add))
            for e in range(NE):
                link(V.scalar_tensor_tensor(tmp16[:], rank[:, :, e], 1.0, tot[:, e, 0:NT], ALU.mult, ALU.add))
                link(V.scalar_tensor_tensor(free[:], base[:, e:e + 1].to_broadcast([P, NT]), float(P), tmp16[:],
                                            ALU.mult, ALU.add))
                if e == 0:
                    link(V.tensor_tensor(pos[:], free[:], F[:, :, e], ALU.mult))
                else:
                    link(V.tensor_tensor(free[:], free[:], F[:, :, e], ALU.mult))
                    link(V.tensor_tensor(pos[:], pos[:], free[:], ALU.add))
            V.tensor_copy(posi[:], pos[:]).then_inc(s["pos_ready"], 1)
            for e in range(1, NE):
                last = V.tensor_scalar(eidf[:, e - 1, :], slotno[:], base[:, e:e + 1], None, ALU.is_ge)
            link(last)
            link(V.tensor_tensor(eidf[:, 0, :], eidf[:, 0, :], eidf[:, 1, :], ALU.add))
            link(V.tensor_tensor(eidf[:, 0, :], eidf[:, 0, :], eidf[:, 2, :], ALU.add))
            V.tensor_copy(eid[:], eidf[:, 0, :]).then_inc(s["eid_ready"], 1)

            V.memset(xTr[KB:KB + 2, :, 3, :].bitcast(F32), 1.0)

            def lo_rows(j, par):
                dve.wait_ge(s["xT_copied"], j + 1)
                V.tensor_tensor(xTr[:, par, 1, :], ps[:, 0, 0:P], xTr[:, par, 0, :].bitcast(F32), ALU.subtract)
                V.tensor_tensor(xTr[KB:P, par, 2, :], ps[0:KB, 0, P:2 * P], xTr[0:KB, par, 2, :].bitcast(F32),
                                ALU.subtract).then_inc(s["xT_split"], 1)

            def turn_hidden(j, par, first=False):
                dve.wait_ge(s["hidT_psum"], j + 1)
                if not first:
                    dve.wait_ge(s["y2_psum"], j - 1)
                V.tensor_copy(hidT[:, par, :], ps[:, 5:7, :].rearrange("p a s -> p (a s)")[:, 0:DF]
                              ).then_inc(s["hidT_copied"], 1)

            def add_h1(h, par, first=False):
                dve.wait_ge(h1_loaded[par], (h + 1) * 16)
                if not first:
                    dve.wait_ge(stored[par], h * 16)
                V.tensor_copy(ids[:, par:par + 1], slot_h[:, par, D:D + 1]).then_inc(s["ids_ready"], 1)
                dve.wait_ge(s["y2_psum"], h * 2 + par + 1)
                V.tensor_tensor(yo[:, par, :], ps[:, 7, 0:D], slot_h[:, par, 0:D], ALU.add
                                ).then_inc(s["yo_ready"], 1)

            lo_rows(0, 0)
            lo_rows(1, 1)
            turn_hidden(0, 0, True)
            lo_rows(2, 0)
            for par in range(2):
                turn_hidden(par + 1, 1 - par, par == 0)
                lo_rows(par + 3, 1 - par)
                add_h1(0, par, True)
            with dve.Fori(1, (SLOTS - 3) // 2) as i:
                for par in range(2):
                    j = i * 2 + par
                    turn_hidden(j + 1, 1 - par)
                    lo_rows(j + 3, 1 - par)
                    add_h1(i, par)
            for j in range(SLOTS - 3, SLOTS):
                if j + 1 < SLOTS:
                    turn_hidden(j + 1, (j + 1) % 2)
                add_h1(j // 2, j % 2)

        @block.tensor
        def _(pe):
            T = nc.tensor

            def mm(o, l, r, start=True, stop=True):
                return T.matmul(o, l, r, start=start, stop=stop)

            def split_product(o, l, r):
                for n, (x, y) in enumerate(((0, 0), (0, 1), (1, 0), (2, 2), (3, 2))):
                    if len(l) < len(r):
                        x, y = y, x
                    last = mm(o, l[x], r[y], start=(n == 0), stop=(n == 4))
                return last

            pe.wait_ge(s["consts"], 1)
            pe.wait_ge(s["tokpos_ready"], 1)

            def bc_index(b):
                q = b % 2
                if b >= 2:
                    pe.wait_ge(s["bcb_ready"], b - 1)
                mm(ps[:, 2 * q, :], pick[:, b, :], rc[:, 0, :])
                mm(ps[:, 2 * q + 1, :], pick[:, b, :], rc[:, 1, :]).then_inc(s["idx_bc_ready"], 1)

            def look_up(b):
                q = b % 2
                pe.wait_ge(s["onehot_ready"], b + 1)
                for p in range(2):
                    n = 2 * b + p
                    if n >= 2:
                        pe.wait_ge(s["h0_copied"], n - 1)
                    for t in range(2):
                        w = slice((2 * p + t) * P, (2 * p + t + 1) * P)
                        o = ps[:, 4 + n % 2, t * D:(t + 1) * D]
                        for k in range(3):
                            mm(o[:, 0:DH], onehot[:, q, 0, w], tabs[:, k, 0, :], start=(k == 0), stop=(k == 2))
                        for i, (k, c) in enumerate((k, c) for k in range(3) for c in (1, 2)):
                            last = mm(o[:, DH:D], onehot[:, q, c, w], tabs[:, k, c, :], start=(i == 0), stop=(i == 5))
                    last.then_inc(s["h0_ready"], 1)

            bc_index(0)
            bc_index(1)
            pe.wait_ge(s["tabs_ready"], 1)
            for b in range(NB):
                look_up(b)
                if b + 2 < NB:
                    bc_index(b + 2)

            def turn_tiles(src, bankA, bankB):
                for t in range(TB):
                    T.transpose(ps[:, bankA, t * P:(t + 1) * P], src(t)[:, 0:KA], ident[:])
                    last = T.transpose(ps[0:KB, bankB, t * P:(t + 1) * P], src(t)[:, KA:D], ident[:])
                return last

            def turn_u(b):
                pe.wait_ge(s["u_ready"], b + 1)
                if b:
                    pe.wait_ge(s["uT_split"], b)
                turn_tiles(lambda t: u[:, b % 2, t, :], 6, 7).then_inc(s["uT_psum"], 1)

            def xtok(b):
                pe.wait_ge(s["silu_done"], b * NCT + CT_X + 1)
                for t in range(TB):
                    m = b * TB + t
                    if m:
                        pe.wait_ge(s["xtok_copied"], m)
                    for c in range(CT_X):
                        T.transpose(ps[:, 5, c * P:(c + 1) * P], xch[:, b % 2, c, t * P:(t + 1) * P], ident[:])
                    T.transpose(ps[:, 5, DI:S], BT[:, m * P:(m + 1) * P], ident[:]).then_inc(s["xtok_psum"], 1)

            def project_xbc(b, c):
                n = b * NCT + c
                if n >= 3:
                    pe.wait_ge(s["conv_done"], n - 2)
                w = slice(XBC0 + c * P, XBC0 + (c + 1) * P)
                split_product(ps[:, n % 3, :], [winr[:, k, w] for k in range(4)], [uT[:, b % 2, k, :] for k in range(3)]
                              ).then_inc(s["xbc_psum"], 1)

            def project_z(b, t):
                m = b * TB + t
                if m >= 2:
                    pe.wait_ge(s["z_copied"], m - 1)
                w = slice(t * P, (t + 1) * P)
                split_product(ps[:, 3 + m % 2, 0:XBC0], [uT[:, b % 2, k, w] for k in range(3)],
                              [winr[:, k, 0:XBC0] for k in range(4)]).then_inc(s["z_psum"], 1)

            pe.wait_ge(s["consts"], 2)
            turn_u(0)
            pe.wait_ge(s["win_split"], 1)
            pe.wait_ge(s["h0_copied"], 2 * NB)
            for b in range(NB):
                pe.wait_ge(s["uT_split"], b + 1)
                project_xbc(b, 0)
                project_xbc(b, 1)
                if b + 1 < NB:
                    turn_u(b + 1)
                for c in range(2, NCT):
                    project_xbc(b, c)
                for t in range(TB):
                    project_z(b, t)
                if b:
                    xtok(b - 1)
            pe.wait_ge(s["z_copied"], NT)
            pe.wait_ge(s["conv_done"], NB * NCT)
            pe.wait_ge(s["silu_done"], NB * NCT)

            def seg(c):
                pe.wait_ge(s["av_ready"], c + 1)
                if c:
                    pe.wait_ge(s["e_ready"], c)
                mm(ps[:, 0, :], after[:], Av)
                mm(ps[:, 1, :], ones[:], Av).then_inc(s["seg_psum"], 1)

            def bc(c):
                if c:
                    pe.wait_ge(s["mt_ready"], c)
                for b in range(NB):
                    w = slice((b * TB + c) * P, (b * TB + c + 1) * P)
                    last = mm(ps[:, 2, b * P:(b + 1) * P], BT[:, w], CT[:, w])
                last.then_inc(s["g_psum"], 1)

            bc(0)
            xtok(NB - 1)
            pe.wait_ge(s["xtok_copied"], NT)

            def turn_gated(k):
                c, b = divmod(k, NB)
                pe.wait_ge(s["ssq_done"], k + 1)
                if k:
                    pe.wait_ge(s["gT_copied"], k)
                for i in range(CT_X):
                    last = T.transpose(ps[:, 7, i * P:(i + 1) * P], zs[:, b * TB + c, i * P:(i + 1) * P], ident[:])
                last.then_inc(s["gT_psum"], 1)

            seg(0)
            for c in range(TB):
                pe.wait_ge(s["mt_ready"], c + 1)
                pe.wait_ge(s["ce_ready"], c + 1)
                if c < TB - 1:
                    bc(c + 1)
                    pe.wait_ge(s["bw_ready"], c + 1)
                    seg(c + 1)
                for b in range(NB):
                    m = b * TB + c
                    k = c * NB + b
                    if k >= 2:
                        pe.wait_ge(s["gated"], k - 1)
                    last = mm(ps[:, 3 + b % 2, 0:DI], MT[c % 2][:, b, :], xB[:, m, 0:DI], stop=(c == 0))
                    if c:
                        pe.wait_ge(s["st_done"], NB * (c - 1) + b + 1)
                        last = mm(ps[:, 3 + b % 2, 0:DI], CE[c % 2][:, b, :], state[:, b, :], start=False)
                    last.then_inc(s["y_psum"], 1)
                    if c < TB - 1:
                        if k >= 2:
                            pe.wait_ge(s["st_done"], k - 1)
                        mm(ps[:, 5 + b % 2, 0:DI], Bw[c % 2][:, b, :], xB[:, m, 0:DI]).then_inc(s["st_psum"], 1)
                    if c:
                        turn_gated(k - NB)
            for b in range(NB):
                turn_gated((TB - 1) * NB + b)

            pe.wait_ge(s["folded_out"], 1)
            pe.wait_ge(s["m1_split"], 1)
            pe.wait_ge(s["ld_gate"], 48)
            pe.wait_ge(s["ld_mlp"], 16)

            def out_proj(b):
                for m in range(b * TB, (b + 1) * TB):
                    pe.wait_ge(s["gT_copied"], (m % TB) * NB + m // TB + 1)
                    if m >= 2:
                        pe.wait_ge(s["res_ready"], m - 1)
                    for c in range(CT_X):
                        last = mm(ps[:, m % 2, 0:D], zs[:, m, c * P:(c + 1) * P], wout[:, c, :],
                                  start=(c == 0), stop=(c == CT_X - 1))
                    last.then_inc(s["out_psum"], 1)

            def turn_res(b):
                pe.wait_ge(s["resn_ready"], b + 1)
                if b:
                    pe.wait_ge(s["rT_split"], b)
                if b >= 3:
                    pe.wait_ge(s["logit_ready"], b - 2)
                turn_tiles(lambda t: resn[:, b % 2, t, :], 2, 3).then_inc(s["rT_psum"], 1)

            def mlp_up(b):
                pe.wait_ge(s["rT_split"], b + 1)
                for c in range(HT):
                    n = b * HT + c
                    if n >= 2:
                        pe.wait_ge(s["gelu_done"], n - 1)
                    w = slice(c * P, (c + 1) * P)
                    split_product(ps[:, 4 + n % 2, :], [m1r[:, k, w] for k in range(4)], [rT[:, k, :] for k in range(3)]
                                  ).then_inc(s["w1_psum"], 1)

            def mlp_down(b):
                pe.wait_ge(s["gelu_done"], (b + 1) * HT)
                for t in range(TB):
                    m = b * TB + t
                    if m >= 2:
                        pe.wait_ge(s["h1_done"], m - 1)
                    for c in range(HT):
                        last = mm(ps[:, 6 + m % 2, 0:D], hT[:, c, t * P:(t + 1) * P], m2[:, c, :],
                                  start=(c == 0), stop=(c == HT - 1))
                    last.then_inc(s["w2_psum"], 1)

            def gate(b):
                pe.wait_ge(s["x2_ready"], b + 1)
                pe.wait_ge(s["rT_split"], min(NB, b + 3))
                turn_tiles(lambda t: row[:, b * TB + t, 0:D], 2, 3).then_inc(s["x2T_psum"], 1)
                pe.wait_ge(s["x2T_copied"], b + 1)
                for t in range(TB):
                    o = ps[:, 2, NE * t:NE * (t + 1)]
                    w = slice(t * P, (t + 1) * P)
                    mm(o, x2T[:, 0, w], wgA[:], stop=False)
                    last = mm(o, x2T[0:KB, 1, w], wgB[:], start=False)
                last.then_inc(s["gate_psum"], 1)

            out_proj(0)
            out_proj(1)
            turn_res(0)
            for b in range(NB):
                mlp_up(b)
                if b + 2 < NB:
                    out_proj(b + 2)
                if b + 1 < NB:
                    turn_res(b + 1)
                if b:
                    gate(b - 1)
                mlp_down(b)
            gate(NB - 1)
            pe.wait_ge(s["f_ready"], 1)
            Ff = F[:].rearrange("p t e -> p (t e)")
            mm(ps[:, 0, 0:NT * NE], before[:], Ff)
            mm(ps[:, 1, 0:NT * NE], ones[:], Ff).then_inc(s["rank_psum"], 1)
            pe.wait_ge(s["eid_ready"], 1)
            pe.wait_ge(s["ld_e2"], 16 * (NE + 1))
            pe.wait_ge(s["b1_split"], NE // 2)
            pe.wait_ge(s["e1_split"], NE)

            def turn(h, par, first=False):
                pe.wait_ge(slot_loaded[par], (h + 1) * 16)
                if not first:
                    pe.wait_ge(s["xT_split"], h * 2 + par)
                T.transpose(ps[:, 0, 0:P], slot_x[:, par, 0:KA], ident[:])
                T.transpose(ps[0:KB, 0, P:2 * P], slot_x[:, par, KA:D], ident[:]).then_inc(s["xT_psum"], 1)

            def up(j, par, e):
                pe.wait_ge(s["xT_split"], j + 1)
                for bank, c0, w in ((1 + 2 * par, 0, 512), (2 + 2 * par, 512, DF - 512)):
                    for n, (x, y, k) in enumerate(((0, 0, P), (1, 0, P), (0, 1, P), (2, 2, P), (3, 3, KB + 2))):
                        last = mm(ps[:, bank, 0:w], xTr[0:k, par, x, :],
                                  e1f[0:k, bass.ds(e * (4 * DF) + y * DF + c0, w)], start=(n == 0), stop=(n == 4))
                last.then_inc(s["hid_psum"], 1)

            def turn_hidden(j, par, first=False):
                pe.wait_ge(s["hid_ready"], j + 1)
                if not first:
                    pe.wait_ge(s["hidT_copied"], j)
                for c in range(HT):
                    last = T.transpose(ps[:, 5 + c // 4, (c % 4) * P:(c % 4 + 1) * P],
                                       hid[:, par, c * P:(c + 1) * P], ident[:])
                last.then_inc(s["hidT_psum"], 1)

            def down(j, par, e, first=False):
                pe.wait_ge(s["hidT_copied"], j + 1)
                if not first:
                    pe.wait_ge(s["yo_ready"], j)
                for c in range(HT):
                    mm(ps[:, 7, 0:D], hidT[:, par, c * P:(c + 1) * P], e2[:, bass.ds(e * (HT * D) + c * D, D)],
                       start=(c == 0), stop=False)
                mm(ps[:, 7, 0:D], ones[0:1, :], e2b[:, bass.ds(e * D, D)], start=False).then_inc(s["y2_psum"], 1)

            def expert(j):
                return pe.value_load(eid[0:1, bass.ds(j, 1)], min_val=0, max_val=NE - 1)

            turn(0, 0, True)
            turn(0, 1)
            up(0, 0, expert(0))
            turn(1, 0)
            up(1, 1, expert(1))
            turn_hidden(0, 0, True)
            for par in range(2):
                up(par + 2, par, expert(par + 2))
                turn_hidden(par + 1, 1 - par)
                turn(1 + par, 1 - par)
                down(par, par, expert(par), par == 0)
            with pe.Fori(1, (SLOTS - 3) // 2) as i:
                for par in range(2):
                    j = i * 2 + par
                    up(j + 2, par, expert(j + 2))
                    turn_hidden(j + 1, 1 - par)
                    turn(i + 1 + par, 1 - par)
                    down(j, par, expert(j))
            j = SLOTS - 3
            up(j + 2, 0, expert(j + 2))
            turn_hidden(j + 1, 1)
            down(j, 0, expert(j))
            turn_hidden(j + 2, 0)
            down(j + 1, 1, expert(j + 1))
            down(j + 2, 0, expert(j + 2))


_INS = ["x", "L0_tok_row_emb_W", "L0_tok_col_emb_W", "L0_attn_norm1_w", "L0_attn_in_proj_W", "L0_attn_conv_w",
        "L0_attn_conv_b", "L0_attn_dt_bias", "L0_attn_A_log", "L0_attn_D", "L0_attn_ssm_norm_w",
        "L0_attn_out_proj_W", "L0_attn_norm2_w", "L0_attn_mlp_W1", "L0_attn_mlp_W2", "L0_ffn_Wg", "L0_ffn_bg",
        "L0_ffn_W1", "L0_ffn_b1", "L0_ffn_W2", "L0_ffn_b2"]


def kernel(**inputs):
    import numpy as _np
    import concourse.bacc as _bacc
    from concourse import mybir as _mybir
    from concourse.bass_utils import run_bass_kernel_spmd as _run

    nc = _bacc.Bacc("TRN2", target_bir_lowering=False, num_devices=1)
    arrays, aps = {}, {}
    for name in _INS:
        v = _np.ascontiguousarray(inputs[name])
        arrays[f"in_{name}"] = v
        aps[name] = nc.dram_tensor(f"in_{name}", v.shape, _mybir.dt.from_np(v.dtype), kind="ExternalInput").ap()
    out = nc.dram_tensor("out_h", (NB * S, D), _mybir.dt.from_np(_np.dtype("float32")), kind="ExternalOutput").ap()
    build(nc, aps, out)
    r = _run(nc, [arrays], core_ids=[0])
    return r.results[0]["out_h"].reshape(NB, S, D)
```

```python
from contextlib import ExitStack

import concourse.bass as bass
from concourse import mybir

F32 = mybir.dt.float32
BF16 = mybir.dt.bfloat16
F32R = mybir.dt.float32r
I32 = mybir.dt.int32
ALU = mybir.AluOpType
ACT = mybir.ActivationFunctionType
AX = mybir.AxisListType

P = 128
NB, S = 4, 512
TB = S // P
NT = NB * TB
D = 192
DH = D // 2
KA, KB = 128, 64
NROW, NCOL = 100, 200
NEWLINE = 7
DI = 2 * D
NS = 128
CT_X = DI // P
NCT = CT_X + 2
TAPS = 4
DF = 4 * D
HT = DF // P
NE = 4
EPS = 1e-5
REGION = NT * P + P
DUMMY = NE * REGION
SLOTS = NT + NE - 1
WAVES = (NT // 2 - (NE - 1), TB, SLOTS - NT // 2 + (NE - 1) - TB)
FIRST = (0, WAVES[0], WAVES[0] + WAVES[1])
AHEAD = 3
PEELED = 4
ROW = 2 * D + 4
NOBODY = 8192.0
DT0 = 2 * DI + 2 * NS
COUNT0 = 32
DTC, XBC0 = DI, DI + 2
NW = XBC0 + DI + 2 * NS


def build(nc, a, out):
    with ExitStack() as ctx:
        def sb(name, shape, dt=F32):
            return ctx.enter_context(nc.sbuf_tensor(name, shape, dt))

        def sem(name):
            return ctx.enter_context(nc.semaphore(name))

        sorted_rows = nc.dram_tensor("sorted_rows", [DUMMY + P, ROW], F32, kind="Internal").ap()
        ps = ctx.enter_context(nc.psum_tensor("ps", [P, 8, 512], F32))

        ident = sb("ident", [P, P])
        upto = sb("upto", [P, 1, P])
        before = sb("before", [P, P])
        after = sb("after", [P, P])
        ones = sb("ones", [P, P])
        part_i = sb("part_i", [P, 2], I32)
        part = sb("part", [P, 2])
        mhalf = sb("mhalf", [P, NT])
        spare = sb("spare", [1, 1])
        d_diag = sb("d_diag", [P, 1, P])
        starts = sb("starts", [P, 1, NT])
        slotno = sb("slotno", [P, 1, WAVES[2]])
        region = sb("region", [P, 1, NE])
        firsts = sb("firsts", [P, 1, NE])
        n1A = sb("n1A", [KA, 1])
        n1B = sb("n1B", [P, 1])
        convw = sb("convw", [P, NCT, TAPS])
        convb = sb("convb", [P, NCT])
        scal = sb("scal", [P, 4])
        wout = sb("wout", [P, CT_X, D])
        ssmn = sb("ssmn", [P, CT_X])
        m1r = sb("m1r", [P, 4, DF], F32R)
        stg0 = sb("stg0", [P, 2, DF])
        n2A = sb("n2A", [KA, 1])
        n2B = sb("n2B", [P, 1])
        m2 = sb("m2", [P, HT, D])
        wgA = sb("wgA", [KA, NE])
        wgB = sb("wgB", [KB, NE])
        bg = sb("bg", [P, 1, NE])
        e2b = sb("e2b", [P, NE * D], F32R)
        with ExitStack() as first:
            h0 = first.enter_context(nc.sbuf_tensor("h0", [P, NT, D], F32))
        hidT = sb("hidT", [P, 2, 2, DF], F32R)
        stats = sb("stats", [P, TB, 6])
        mv = sb("mv", [P, NT, 2])
        var2 = sb("var2", [P, NB, 2, TB])
        rstd2 = sb("rstd2", [P, NB, 2, TB])
        nmr = sb("nmr", [P, NT])
        with ExitStack() as first:
            u = first.enter_context(nc.sbuf_tensor("u", [P, 2, TB, D], F32))
        Av = sb("Av", [P, 2, NB, P], F32R)
        e2_even = sb("e2_even", [P, NB, P])
        afterr = sb("afterr", [P, P], F32R)
        decayr = sb("decayr", [P, 2, NT], F32R)
        eL = sb("eL", [P, 2, NB])
        acc = sb("acc", [P, 3, S])
        xch = sb("xch", [P, 2, CT_X, S])
        with ExitStack() as first:
            BCz = first.enter_context(nc.sbuf_tensor("BCz", [P, 2 * NT * P + NT * DI], F32))
        E2W = 2 * HT * D
        e2 = sb("e2", [P, NE * E2W], F32R)
        sb("e2_rest", [P, 2 * NT * P + NT * DI - NE * E2W])
        BT = BCz[:, 0:NT * P]
        CT = BCz[:, NT * P:2 * NT * P]
        zs = BCz[:, 2 * NT * P:2 * NT * P + NT * DI].rearrange("p (t d) -> p t d", d=DI)
        with ExitStack() as first:
            def early(name, shape, dt=F32):
                return first.enter_context(nc.sbuf_tensor(name, shape, dt))
            tok_i = early("tok_i", [NB, S], I32)
            count_i = early("count_i", [P, S], I32)
            count = early("count", [P, S])
            zeros = early("zeros", [NB, S])
            pick = early("pick", [NB, NB, P], BF16)
            newl = early("newl", [NB, 2, S])
            scanned = early("scanned", [NB, 2, S + 1])
            rc = early("rc", [NB, 2, S], BF16)
            bcb = early("bcb", [P, 2, 2, S], BF16)
            onehot = early("onehot", [P, 2, 3, S], BF16)
            tab = early("tab", [P, 3, DH])
            tabs = early("tabs", [P, 3, 3, DH], BF16)
        xB = sb("xB", [P, NT, S])
        with ExitStack() as first:
            winr = first.enter_context(nc.sbuf_tensor("winr", [P, 4, NW], F32R))
            uT = first.enter_context(nc.sbuf_tensor("uT", [P, 2, 3, S], F32R))
            empty = first.enter_context(nc.sbuf_tensor("empty", [P, ROW], F32))
        e1r = sb("e1r", [P, NE, 4, DF], F32R)
        e1f = e1r[:].rearrange("p e k h -> p (e k h)")
        dtr = sb("dtr", [P, NT])
        dtx = sb("dtx", [P, NT])
        dta = sb("dta", [P, NT])
        dte = sb("dte", [P, NT])
        dtl = sb("dtl", [P, NT])
        dt = sb("dt", [P, NT])
        decay = sb("decay", [P, NT])
        ssq = sb("ssq", [P, NT])
        ssq_e = sb("ssq_e", [P, NT])
        rr = sb("rr", [P, NT])
        def slot4(t, i):
            return t[:].rearrange("p a s -> p (a s)")[:, i * S:(i + 1) * S].rearrange("p (b t) -> p b t", b=NB)

        def xB_tile(m):
            b, c = divmod(m, TB)
            return xB[:, (TB - 1 - c) * NB + b, :]

        xchf = xch[:].rearrange("p a c s -> p (a c) s")
        E1, LM = slot4(acc, 1), slot4(acc, 2)
        E2 = (e2_even[:], slot4(acc, 0))
        CE = (slot4(xchf, 0), slot4(xchf, 1))
        MT = (slot4(xchf, 2), slot4(xchf, 3))
        Bw = (slot4(xchf, 4), slot4(xchf, 5))
        junk = sb("junk", [P, DI], BF16)
        b1raw = stg0
        b2raw = stg0[:, 0, :]
        rawA = xchf.rearrange("p c s -> p (c s)")[:, 0:NW]
        rawB = xchf.rearrange("p c s -> p (c s)")[:, NW:2 * NW]
        wB = sb("wB", [P, 2, NB])
        state = sb("state", [P, NB, DI])
        xBf = xB[:].rearrange("p t s -> p (t s)")
        x1_first = xBf[:, 2 * NB * S:2 * NB * S + 2 * NB * D].rearrange("p (a t d) -> p a t d", a=2, t=NB)
        x1_last = state[:].rearrange("p b c -> p (b c)").rearrange("p (a t d) -> p a t d", a=2, t=NB)
        x1 = (x1_first[:, 0], x1_first[:, 1], x1_last[:, 0], x1_last[:, 1])
        res = xBf[:, NT * ROW:NT * ROW + 2 * NB * D].rearrange("p (a t d) -> p a t d", a=2, t=NB)
        resn = u
        with ExitStack() as first:
            stg1 = first.enter_context(nc.sbuf_tensor("stg1", [P, 2, DF], F32))
        stg = (stg0, stg1)
        rT = sb("rT", [P, 3, S], F32R)
        x2T = state[:].rearrange("p b c -> p (b c)")[:, 0:2 * S].rearrange("p (a s) -> p a s", a=2)
        hT = xchf
        ssq2 = sb("ssq2", [P, NT])
        ssq2e = sb("ssq2e", [P, NT])
        rn = sb("rn", [P, NT])
        mv2 = sb("mv2", [P, NT, 2])
        var_e = sb("var_e", [P, NT])
        r2 = sb("r2", [P, NT])
        row = xBf[:, 0:NT * ROW].rearrange("p (t r) -> p t r", r=ROW)
        logit = sb("logit", [P, NT, NE])
        top = sb("top", [P, NB, 1])
        best = sb("best", [P, NB, NE])
        F = sb("F", [P, NT, NE])
        G = sb("G", [P, NT + 1, NE])
        spot = sb("spot", [P, NB, NE])
        pos = sb("pos", [P, NT])
        posi = sb("posi", [P, NT], I32)
        cnt = sb("cnt", [P, NE, 1])
        lim = sb("lim", [P, NE, 1])
        begun = sb("begun", [P, NE, NT])
        need = sb("need", [P, NE])
        done = sb("done", [P, NE])
        take = sb("take", [P, NE])
        base = sb("base", [P, NE + 1])
        off = sb("off", [P, NE])
        doff = sb("doff", [P, NE - 1, 1])
        begins = sb("begins", [P, NE, WAVES[2]])
        terms = sb("terms", [P, NE - 1, WAVES[2]])
        eidf = sb("eidf", [P, WAVES[2]])
        addrf = sb("addrf", [P, WAVES[2]])
        toward = sb("toward", [P, WAVES[2]])
        padf = sb("padf", [P, NE])
        eid = sb("eid", [P, SLOTS + 1], I32)
        addr = sb("addr", [P, SLOTS + 1], I32)
        padi = sb("padi", [P, NE], I32)
        accf = acc[:].rearrange("p a s -> p (a s)")
        slot_x = accf[:, 0:2 * D].rearrange("p (a d) -> p a d", a=2)
        slot_h = accf[:, 2 * D:2 * D + 2 * (ROW - D)].rearrange("p (a d) -> p a d", a=2)
        yo = accf[:, 3 * S - 2 * D:3 * S].rearrange("p (a d) -> p a d", a=2)
        ids = sb("ids", [P, 2], I32)
        xTr = rT[:].rearrange("p a s -> p (a s)")[:, 0:8 * P].rearrange("p (a k t) -> p a k t", a=2, k=4)
        hid = xchf.rearrange("p c s -> p (c s)")[:, 0:2 * DF].rearrange("p (a d) -> p a d", a=2)
        junk2 = sb("junk2", [P, D], BF16)

        names = """ld_x ld_tab ld_in ld_conv ld_scal ld_out ld_m1 ld_e1_odd ld_e1_even ld_b1 ld_mlp ld_gate ld_e2_even
            ld_e2_odd ld_b2 e2_split b2_hi b2_lo b2_split count_made count_copied consts pool_seq dve_seq
            act_seq tab_zero win_hi win_zero win_split folded_out m1_split e1_split e1_last_hi e1_last_split
            b1_hi b1_lo b1_split ddiag_ready dummy_ready tokpos_ready tabs_ready idx_bc_ready bcb_ready
            onehot_ready h0_ready h0_copied var_ready rstd_ready nmr_ready first_u_ready u_ready uT_psum
            uT_copied uT_split xbc_psum tap_ready conv_done silu_done z_psum z_copied xtok_psum xtok_copied
            xtok_first dt_abs dt_exp av_ready seg_psum g_psum e_ready ce_ready mt_ready bw_ready y_psum st_psum
            st_done gated ssq_done ssqe_ready rr_ready gT_psum gT_copied out_psum x1_ready res_ready ssq2_done
            ssq2e_ready rn_ready resn_ready rT_psum rT_copied rT_split w1_psum gelu_done w2_psum h1_done
            var2_ready r2_ready x2_ready x2T_psum x2T_copied gate_psum logit_ready f_ready rank_psum ranks_read
            pos_ready table_ready rows_half rows_third rows_last pads_ready loaded_even loaded_odd h1_even
            h1_odd stored_even stored_odd ids_ready xT_psum xT_copied xT_split hid_psum hid_ready hidT_psum
            hidT_hi hidT_split y_part y2_psum yo_ready""".split()
        s = {n: sem(n) for n in names}
        slot_loaded = (s["loaded_even"], s["loaded_odd"])
        h1_loaded = (s["h1_even"], s["h1_odd"])
        stored = (s["stored_even"], s["stored_odd"])
        block = ctx.enter_context(nc.Block())

        def e2_parts(e):
            return (t[:, e * E2W:(e + 1) * E2W].rearrange("p (c k d) -> p c k d", c=HT, k=2) for t in (BCz, e2))

        def gate_bank(q):
            return (0, 1) if q < TB - 1 else (7, 7)

        def bc_rows(ap1, n):
            return ap1.rearrange("(o n) -> o n", o=1).to_broadcast([P, n])

        def z_steps(b, c):
            if b < NB - 1:
                return [c] if c < TB else []
            return [2 * c, 2 * c + 1] if c < TB // 2 else []

        @block.sync
        def _(sp):
            sp.dma_start(tok_i[:], a["x"]).then_inc(s["ld_x"], 16)
            sp.wait_ge(s["tab_zero"], 1)
            sp.dma_start(tab[0:NROW, 0, :], a["L0_tok_row_emb_W"]).then_inc(s["ld_tab"], 16)
            sp.dma_start(tab[:, 1, :], a["L0_tok_col_emb_W"][0:P, :]).then_inc(s["ld_tab"], 16)
            sp.dma_start(tab[0:NCOL - P, 2, :], a["L0_tok_col_emb_W"][P:NCOL, :]).then_inc(s["ld_tab"], 16)
            win = a["L0_attn_in_proj_W"]
            n1 = a["L0_attn_norm1_w"].rearrange("(p o) -> p o", o=1)
            for dst, norm, p0, k0, k1 in ((rawA, n1A, 0, 0, KA), (rawB, n1B, 0, KA, D), (rawB, n1B, KB, KA, D)):
                d = dst[p0:p0 + k1 - k0, :]
                sp.dma_start(d[:, 0:DI], win[k0:k1, 0:DI]).then_inc(s["ld_in"], 16)
                sp.dma_start(d[:, XBC0:NW], win[k0:k1, DI:DT0]).then_inc(s["ld_in"], 16)
                sp.dma_start(d[:, DTC:DTC + 1], win[k0:k1, DT0:DT0 + 1],
                             allow_slow_non_contiguous=True).then_inc(s["ld_in"], 16)
                sp.dma_start(norm[p0:p0 + k1 - k0, :], n1[k0:k1, :]).then_inc(s["ld_in"], 16)
            sp.dma_start(convw[:], a["L0_attn_conv_w"].rearrange("(c p) k -> p c k", p=P)).then_inc(s["ld_conv"], 16)
            sp.dma_start(convb[:], a["L0_attn_conv_b"].rearrange("(c p) -> p c", p=P),
                         allow_slow_non_contiguous=True).then_inc(s["ld_conv"], 16)
            for i, n in enumerate(("L0_attn_dt_bias", "L0_attn_A_log", "L0_attn_D")):
                sp.dma_start(scal[:, i:i + 1], bc_rows(a[n], 1)).then_inc(s["ld_scal"], 16)
            sp.dma_start(wout[:], a["L0_attn_out_proj_W"].rearrange("(c p) d -> p c d", p=P)).then_inc(s["ld_out"], 16)
            sp.dma_start(ssmn[:], a["L0_attn_ssm_norm_w"].rearrange("(c p) -> p c", p=P),
                         allow_slow_non_contiguous=True).then_inc(s["ld_out"], 16)
            n2 = a["L0_attn_norm2_w"].rearrange("(p o) -> p o", o=1)

            def load_split(buf, w, signal):
                sp.dma_start(stg[buf][:, 0, :], w[0:KA, :]).then_inc(signal, 16)
                for p0 in (0, KB):
                    sp.dma_start(stg[buf][p0:p0 + KB, 1, :], w[KA:D, :]).then_inc(signal, 16)

            load_split(0, a["L0_attn_mlp_W1"], s["ld_m1"])
            sp.dma_start(n2A[:], n2[0:KA, :]).then_inc(s["ld_m1"], 16)
            for p0 in (0, KB):
                sp.dma_start(n2B[p0:p0 + KB, :], n2[KA:D, :]).then_inc(s["ld_m1"], 16)
            sp.dma_start(m2[:], a["L0_attn_mlp_W2"].rearrange("(c p) d -> p c d", p=P)).then_inc(s["ld_mlp"], 16)
            sp.dma_start(wgA[:], a["L0_ffn_Wg"][0:KA, :]).then_inc(s["ld_gate"], 16)
            sp.dma_start(wgB[:], a["L0_ffn_Wg"][KA:D, :]).then_inc(s["ld_gate"], 16)
            sp.dma_start(bg[:, 0, :], bc_rows(a["L0_ffn_bg"], NE)).then_inc(s["ld_gate"], 16)
            sp.wait_ge(s["consts"], 2)
            sp.dma_start(sorted_rows[DUMMY:DUMMY + P, :], empty[:]).then_inc(s["dummy_ready"], 16)
            load_split(1, a["L0_ffn_W1"][0], s["ld_e1_odd"])
            b1 = a["L0_ffn_b1"].rearrange("(o e) h -> o e h", o=1)
            sp.wait_ge(s["m1_split"], 1)
            load_split(0, a["L0_ffn_W1"][1], s["ld_e1_even"])
            sp.wait_ge(s["e1_split"], 1)
            load_split(1, a["L0_ffn_W1"][2], s["ld_e1_odd"])
            sp.wait_ge(s["e1_split"], 2)
            load_split(0, a["L0_ffn_W1"][3], s["ld_e1_even"])
            sp.wait_ge(s["e1_last_split"], 1)
            b2 = a["L0_ffn_b2"].rearrange("(o e) h -> o (e h)", o=1)
            for p0 in range(2):
                sp.dma_start(b2raw[p0:p0 + 1, :], b2).then_inc(s["ld_b2"], 16)
            sp.wait_ge(s["out_psum"], NT)
            for i in range(NE // 2):
                if i:
                    sp.wait_ge(s["b1_split"], i)
                for p0 in range(2):
                    sp.dma_start(b1raw[KB + p0:KB + p0 + 1], b1[:, 2 * i:2 * i + 2]).then_inc(s["ld_b1"], 16)
                if i == 0:
                    for e in range(NE):
                        if e >= 2:
                            sp.wait_ge(s["e2_split"], e - 1)
                        raw, _ = e2_parts(e)
                        sp.dma_start(raw[:, :, 1, :], a["L0_ffn_W2"][e].rearrange("(c p) d -> p c d", p=P)
                                     ).then_inc(s["ld_e2_odd" if e % 2 else "ld_e2_even"], 16)

            def first_row(j):
                return sp.value_load(addr[0:1, bass.ds(j, 1)], min_val=0, max_val=DUMMY)

            def load_x2(j, par, early=False):
                if not early:
                    sp.wait_ge(s["xT_psum"], j - 1)
                sp.dma_start(slot_x[:, par, :], sorted_rows[bass.ds(first_row(j), P), 0:D]
                             ).then_inc(slot_loaded[par], 16)

            def load_h1(j, par, early=False):
                if not early:
                    sp.wait_ge(s["yo_ready"], j - 1)
                    sp.wait_ge(s["ids_ready"], j - 1)
                sp.dma_start(slot_h[:, par, :], sorted_rows[bass.ds(first_row(j), P), D:ROW]
                             ).then_inc(h1_loaded[par], 16)

            def stage_ready(k):
                sp.wait_ge(s["table_ready"], k + 1)
                if k == 0:
                    sp.wait_ge(s["rows_half"], 16 * NT // 2)
                elif k == 1:
                    sp.wait_ge(s["rows_third"], 16 * NB)
                else:
                    sp.wait_ge(s["rows_last"], 16 * NB)
                    sp.wait_ge(s["pads_ready"], 16 * NE)

            stage_ready(0)
            for j in range(2):
                load_x2(j, j, True)
            for j in range(2):
                load_h1(j, j, True)
            for j in range(2, 2 + AHEAD):
                load_x2(j, j % 2)
            for j in range(2, FIRST[2] - 1):
                if j + AHEAD in FIRST:
                    stage_ready(FIRST.index(j + AHEAD))
                load_x2(j + AHEAD, (j + AHEAD) % 2)
                load_h1(j, j % 2)
                if j + AHEAD == FIRST[2] - 2:
                    sp.wait_ge(s["table_ready"], 3)
                    sp.wait_ge(s["dummy_ready"], 16)
                    for e in range(NE):
                        pad = sp.value_load(padi[0:1, e:e + 1], min_val=0, max_val=DUMMY - P)
                        sp.dma_start(sorted_rows[bass.ds(pad, P), :], sorted_rows[DUMMY:DUMMY + P, :]
                                     ).then_inc(s["pads_ready"], 16)
            with sp.Fori((FIRST[2] - 1) // 2, (SLOTS - 3) // 2) as i:
                for par in range(2):
                    j = i * 2 + par
                    load_x2(j + AHEAD, 1 - par)
                    load_h1(j, par)
            for j in range(SLOTS - 3, SLOTS):
                load_h1(j, j % 2)

        @block.gpsimd
        def _(pool):
            g = nc.gpsimd
            n = [0]

            def link(ins):
                n[0] += 1
                ins.then_inc(s["pool_seq"], 1)
                pool.wait_ge(s["pool_seq"], n[0])

            g.iota(count_i[:], [[1, S]], base=1, channel_multiplier=0).then_inc(s["count_made"], 1)
            g.iota(part_i[:], [[P, 2]], base=0, channel_multiplier=1)
            link(g.memset(pick[:], 1.0))
            g.tensor_copy(part[:], part_i[:])
            g.affine_select(out=pick[:], in_=pick[:], compare_op=ALU.is_equal, fill=0.0, base=0,
                            pattern=[[-1, NB], [0, P]], channel_multiplier=1).then_inc(s["consts"], 1)
            g.memset(ones[:], 1.0)
            g.memset(mhalf[:], -0.5)
            g.memset(empty[:], 0.0)
            g.memset(e2b[:].bitcast(F32), 0.0)
            for e in range(NE):
                g.memset(region[:, 0, e:e + 1], float(e * REGION))
                g.memset(firsts[:, 0, e:e + 1], float(NE - e))
            link(g.memset(upto[:], 1.0))
            pool.wait_ge(s["count_copied"], 1)
            g.affine_select(out=ident[:], in_=ones[:], compare_op=ALU.is_equal, fill=0.0, base=0,
                            pattern=[[-1, P]], channel_multiplier=1)
            g.affine_select(out=before[:], in_=ones[:], compare_op=ALU.is_ge, fill=0.0, base=-1,
                            pattern=[[1, P]], channel_multiplier=-1)
            g.affine_select(out=after[:], in_=ones[:], compare_op=ALU.is_ge, fill=0.0, base=-1,
                            pattern=[[-1, P]], channel_multiplier=1)
            link(g.tensor_scalar(slotno[:, 0, :], count[:, 0:WAVES[2]], -1.0, None, ALU.add))
            g.tensor_copy(afterr[:], after[:])
            g.tensor_scalar(starts[:, 0, :], count[:, 0:NT], float(P), -float(P), ALU.mult, ALU.add)
            g.affine_select(out=upto[:], in_=upto[:], compare_op=ALU.is_ge, fill=0.0, base=0,
                            pattern=[[0, 1], [1, P]], channel_multiplier=-1)
            g.memset(empty[:, 2 * D:2 * D + 1], NOBODY).then_inc(s["consts"], 1)
            pool.wait_ge(s["consts"], 2)
            g.memset(winr[KB:P, 3, :].bitcast(F32), 0.0).then_inc(s["win_zero"], 1)
            link(g.memset(m1r[KB:P, 3, :].bitcast(F32), 0.0))
            for b in range(NB):
                pool.wait_ge(s["var_ready"], b + 1)
                g.tensor_tensor(rstd2[:, b], var2[:, b], mhalf[:, 0:2 * TB].rearrange("p (a t) -> p a t", a=2),
                                ALU.pow).then_inc(s["rstd_ready"], 1)
                if b == 0:
                    continue
                pool.wait_ge(s["rstd_ready"], b + 1)
                if b >= 2:
                    pool.wait_ge(s["uT_psum"], b - 1)
                for t in range(TB):
                    m = b * TB + t
                    last = g.tensor_scalar(u[:, b % 2, t, :], h0[:, m, :], mv[:, m, 0:1], rstd2[:, b, 1, t:t + 1],
                                           ALU.subtract, ALU.mult)
                last.then_inc(s["u_ready"], 1)
            pool.wait_ge(s["ld_m1"], 6 * 16)
            g.tensor_scalar(stg0[:, 0, :], stg0[:, 0, :], n2A[:, 0:1], None, ALU.mult)
            link(g.tensor_scalar(stg0[:, 1, :], stg0[:, 1, :], n2B[:, 0:1], None, ALU.mult))

            def split(raw, dst):
                g.tensor_copy(dst[:, 0, :], raw[:, 0, :])
                link(g.tensor_copy(dst[:, 2, :], raw[:, 1, :]))
                g.tensor_tensor(dst[:, 1, :], raw[:, 0, :], dst[:, 0, :].bitcast(F32), ALU.subtract)
                return g.tensor_tensor(dst[0:KB, 3, :], raw[0:KB, 1, :], dst[0:KB, 2, :].bitcast(F32), ALU.subtract)

            split(stg0, m1r).then_inc(s["m1_split"], 1)
            pool.wait_ge(s["ld_out"], 32)
            for c in range(CT_X):
                last = g.tensor_scalar(wout[:, c, :], wout[:, c, :], ssmn[:, c:c + 1], None, ALU.mult)
            last.then_inc(s["folded_out"], 1)
            pool.wait_ge(s["ld_scal"], 48)
            g.tensor_scalar(d_diag[:, 0, :], ident[:], scal[:, 2:3], None, ALU.mult).then_inc(s["ddiag_ready"], 1)
            pool.wait_ge(s["dummy_ready"], 16)
            pool.wait_ge(s["xbc_psum"], NB * NCT)
            pool.wait_ge(s["z_psum"], NT)

            def split_expert(e):
                q = (e + 1) % 2
                pool.wait_ge(s[("ld_e1_even", "ld_e1_odd")[q]], 48 * (e // 2 + 1))
                split(stg[q], e1r[:, e]).then_inc(s["e1_split"], 1)

            def pow_gate(c):
                pool.wait_ge(s["ssqe_ready"], c + 1)
                v = lambda t: t[:].rearrange("p (b c) -> p b c", b=NB)[:, :, c]
                g.tensor_tensor(v(rr), v(ssq_e), mhalf[:, 0:NB], ALU.pow).then_inc(s["rr_ready"], 1)

            def pow_res(q):
                pool.wait_ge(s["ssq2e_ready"], q + 1)
                g.tensor_tensor(rn[:, q * NB:(q + 1) * NB], ssq2e[:, q * NB:(q + 1) * NB], mhalf[:, 0:NB],
                                ALU.pow).then_inc(s["rn_ready"], 1)

            def pow_second(q):
                pool.wait_ge(s["var2_ready"], q + 1)
                g.tensor_tensor(r2[:, q * NB:(q + 1) * NB], var_e[:, q * NB:(q + 1) * NB], mhalf[:, 0:NB],
                                ALU.pow).then_inc(s["r2_ready"], 1)

            def split_second(e):
                pool.wait_ge(s["ld_e2_odd" if e % 2 else "ld_e2_even"], 16 * (e // 2 + 1))
                raw, w = e2_parts(e)
                link(g.tensor_copy(w[:, :, 0, :], raw[:, :, 1, :]))
                g.tensor_tensor(w[:, :, 1, :], raw[:, :, 1, :], w[:, :, 0, :].bitcast(F32), ALU.subtract
                                ).then_inc(s["e2_split"], 1)

            def scatter(q):
                pool.wait_ge(s["pos_ready"], q + 1)
                pool.wait_ge(s["x2_ready"], q + 1)
                for r in range(q * NB, (q + 1) * NB):
                    g.indirect_dma_start(out=sorted_rows, out_offset=bass.IndirectOffsetOnAxis(posi[:, r:r + 1], 0),
                                         in_=row[:, r, :], in_offset=None
                                         ).then_inc(s[("rows_half", "rows_half", "rows_third", "rows_last")[q]], 16)

            split_expert(0)
            split_expert(1)
            pow_gate(0)
            split_expert(2)
            for c in range(1, TB):
                pow_gate(c)
                if c >= TB - 2:
                    pow_res(c - (TB - 2))
            pow_res(2)
            pow_res(3)
            for q in range(TB):
                pow_second(q)
                if q:
                    scatter(q - 1)
                if q < NE // 2:
                    for e in (2 * q, 2 * q + 1):
                        split_second(e)
            last_token = pool.to_reg(NB * S - 1)
            for j in range(SLOTS):
                pool.wait_ge(s["yo_ready"], j + 1)
                pool.wait_ge(s["ids_ready"], j + 1)
                g.indirect_dma_start(out=out, out_offset=bass.IndirectOffsetOnAxis(ids[:, j % 2:j % 2 + 1], 0),
                                     in_=yo[:, j % 2, :], in_offset=None, bounds_check=last_token,
                                     oob_is_err=False).then_inc(stored[j % 2], 16)
                if j == 1:
                    scatter(TB - 1)
            pool.wait_ge(stored[0], 16 * ((SLOTS + 1) // 2))
            pool.wait_ge(stored[1], 16 * (SLOTS // 2))

        @block.scalar
        def _(act):
            A = nc.scalar

            def fetch_table(func):
                A.activation(spare[:], mhalf[0:1, 0:1], func)

            def bc_copy(b):
                act.wait_ge(s["idx_bc_ready"], b + 1)
                if b >= 2:
                    act.wait_ge(s["onehot_ready"], b - 1)
                A.copy(bcb[:, b % 2], ps[:, 2 * (b % 2):2 * (b % 2) + 2, :]).then_inc(s["bcb_ready"], 1)

            def h0_copy(n):
                act.wait_ge(s["h0_ready"], n + 1)
                A.copy(h0[:, 2 * n:2 * n + 2, :], ps[:, 4 + n % 2, 0:2 * D].rearrange("p (a d) -> p a d", a=2)
                       ).then_inc(s["h0_copied"], 1)

            def u_hi(b):
                act.wait_ge(s["uT_psum"], b + 1)
                if b >= 2:
                    act.wait_ge(s["z_psum"], (b - 1) * TB)
                A.copy(uT[:, b % 2, 0, :], ps[:, 6, :])
                A.copy(uT[0:KB, b % 2, 2, :], ps[0:KB, 7, :]).then_inc(s["uT_copied"], 1)

            bc_copy(0)
            bc_copy(1)
            act.wait_ge(s["ld_in"], 12 * 16)
            act.wait_ge(s["tokpos_ready"], 1)
            A.activation(winr[:, 0, :], rawA, ACT.Identity, scale=n1A[:, 0:1]).then_inc(s["win_hi"], 1)
            for b in range(NB):
                if b == NB - 1:
                    u_hi(0)
                h0_copy(2 * b)
                h0_copy(2 * b + 1)
                if b == 0:
                    A.activation(winr[:, 2, :], rawB, ACT.Identity, scale=n1B[:, 0:1]).then_inc(s["win_hi"], 1)
                if b + 2 < NB:
                    bc_copy(b + 2)
            act.wait_ge(s["ld_conv"], 32)

            def tap(n):
                act.wait_ge(s["xbc_psum"], n + 1)
                if n >= 3:
                    act.wait_ge(s["silu_done"], n - 2)
                A.activation(acc[:, n % 3, :], ps[:, n % 3, :], ACT.Identity, bias=convb[:, n % NCT:n % NCT + 1],
                             scale=convw[:, n % NCT, TAPS - 1:TAPS]).then_inc(s["tap_ready"], 1)

            def silu(n):
                b, c = divmod(n, NCT)
                act.wait_ge(s["conv_done"], n + 1)
                if c == 0 and b >= 2:
                    act.wait_ge(s["xtok_psum"], (b - 1) * TB)
                if n == 0:
                    act.wait_ge(s["win_split"], 1)
                dst = xch[:, b % 2, c, :] if c < CT_X else (BT, CT)[c - CT_X][:, b * S:(b + 1) * S]
                A.activation(dst, acc[:, n % 3, :], ACT.Silu).then_inc(s["silu_done"], 1)

            def xtok(m, bank=5):
                act.wait_ge(s["xtok_psum"], m + 1)
                A.copy(xB_tile(m), ps[:, bank, :]).then_inc(s["xtok_copied"], 1)

            def z_silu(m):
                act.wait_ge(s["z_psum"], m + 1)
                A.activation(zs[:, m, :], ps[:, 3 + m % 2, 0:DI], ACT.Silu)
                A.copy(dtr[:, m:m + 1], ps[:, 3 + m % 2, DTC:DTC + 1]).then_inc(s["z_copied"], 1)

            def softplus():
                act.wait_ge(s["dt_abs"], 1)
                A.activation(dte[:], dta[:], ACT.Exp, scale=-1.0).then_inc(s["act_seq"], 1)
                A.activation(scal[:, 3:4], scal[:, 1:2], ACT.Exp).then_inc(s["act_seq"], 1)
                act.wait_ge(s["act_seq"], 2)
                A.activation(dtl[:], dte[:], ACT.Ln, bias=1.0).then_inc(s["dt_exp"], 1)

            for b in range(NB):
                for c in range(NCT):
                    n = b * NCT + c
                    tap(n)
                    if n == NB * NCT - 1:
                        softplus()
                    if n:
                        silu(n - 1)
                    for t in z_steps(b, c):
                        z_silu(b * TB + t)
                    if b and c >= NCT - TB:
                        xtok((b - 1) * TB + c - (NCT - TB))
                    if c == 1 and b + 1 < NB:
                        u_hi(b + 1)
            silu(NB * NCT - 1)
            fetch_table(ACT.Exp)
            act.wait_ge(s["silu_done"], NB * NCT)

            def decays(c):
                act.wait_ge(s["seg_psum"], 2 * c + 1)
                if c:
                    act.wait_ge(s["ce_ready"], c)
                A.activation(E1, ps[:, 0, :].rearrange("p (b t) -> p b t", b=NB), ACT.Exp)
                act.wait_ge(s["seg_psum"], 2 * c + 2)
                A.activation(E2[c % 2], ps[:, 1, :].rearrange("p (b t) -> p b t", b=NB), ACT.Exp
                             ).then_inc(s["e_ready"], 1)

            def square(k):
                c, b = divmod(k, NB)
                m = b * TB + c
                act.wait_ge(s["gated"], k + 1)
                if k:
                    act.wait_ge(s["ssq_done"], k)
                A.activation(junk[:, 0:DI], zs[:, m, :], ACT.Square, accum_out=ssq[:, m:m + 1]
                             ).then_inc(s["ssq_done"], 1)

            def keep_turned(k):
                c, b = divmod(k, NB)
                act.wait_ge(s["gT_psum"], k + 1)
                act.wait_ge(s["ssq_done"], k + 1)
                A.copy(zs[:, b * TB + c, :], ps[:, 7, 0:DI]).then_inc(s["gT_copied"], 1)

            def segments(c):
                act.wait_ge(s["seg_psum"], 2 * c)
                for b in range(NB):
                    m = b * TB + c
                    for k in range(2):
                        last = A.activation(Av[:, k, b, :], upto[:, 0, :], ACT.Identity,
                                            scale=decayr[:, k, m:m + 1].bitcast(F32))
                last.then_inc(s["av_ready"], 1)

            def first_norm_again(q):
                if q < 2:
                    act.wait_ge(s["y_psum"], 2 * NB)
                    act.wait_ge(s["st_psum"], 2 * NB)
                else:
                    act.wait_ge(s["y_psum"], NT)
                    act.wait_ge(s["st_done"], NB * (TB - 1))
                act.wait_ge(s["nmr_ready"], NB)
                for t in range(NB):
                    m = t * TB + q
                    last = A.activation(x1[q][:, t, :], h0[:, m, :], ACT.Identity, bias=nmr[:, m:m + 1],
                                        scale=rstd2[:, t, 0, q:q + 1])
                last.then_inc(s["x1_ready"], 1)

            def square_res(q, t):
                r = q * NB + t
                act.wait_ge(s["res_ready"], r + 1)
                if r:
                    act.wait_ge(s["ssq2_done"], r)
                A.activation(junk2[:], res[:, q % 2, t, :], ACT.Square, accum_out=ssq2[:, r:r + 1]
                             ).then_inc(s["ssq2_done"], 1)

            decays(0)
            for t in range(1, TB):
                xtok(NT - TB + t, 3 + t)
            for c in range(TB):
                if c == 1:
                    segments(c + 2)
                elif c == TB - 1:
                    first_norm_again(0)
                    first_norm_again(1)
                for b in range(NB):
                    square(c * NB + b)
                    if c == 0 and b == 0:
                        decays(1)
                        segments(2)
                    if c:
                        keep_turned((c - 1) * NB + b)
                    if c == TB - 1 and b:
                        square_res(0, b - 1)
                if c + 2 < TB:
                    decays(c + 2)
            square_res(0, NB - 1)

            def bias_hi(i):
                act.wait_ge(s["ld_b1"], 32 * (i + 1))
                A.copy(e1r[KB:KB + 2, 2 * i:2 * i + 2, 3, :], b1raw[KB:KB + 2]).then_inc(s["b1_hi"], 1)
                if i == 0:
                    act.wait_ge(s["ld_b2"], 32)
                    A.copy(e2b[0:2, :], b2raw[0:2, :]).then_inc(s["b2_hi"], 1)

            def bias_hi_again(i):
                if i == 0:
                    act.wait_ge(s["b2_lo"], 1)
                    A.copy(e2b[0:1, :], b2raw[0:1, :]).then_inc(s["b2_split"], 1)
                act.wait_ge(s["b1_lo"], i + 1)
                A.copy(e1r[KB:KB + 1, 2 * i:2 * i + 2, 3, :], b1raw[KB:KB + 1]).then_inc(s["b1_split"], 1)

            def r_hi(q):
                act.wait_ge(s["rT_psum"], q + 1)
                if q:
                    act.wait_ge(s["w1_psum"], q * HT)
                else:
                    act.wait_ge(s["e1_split"], NE - 1)
                A.copy(rT[:, 0, :], ps[:, 2, :])
                A.copy(rT[0:KB, 2, :], ps[0:KB, 3, :]).then_inc(s["rT_copied"], 1)

            def turn(j, par):
                act.wait_ge(s["xT_psum"], j + 1)
                A.copy(xTr[:, par, 0, :], ps[:, 0, 0:P])
                A.copy(xTr[0:KB, par, 2, :], ps[0:KB, 0, P:2 * P])
                A.copy(xTr[0:KB, par, 3, :], ps[0:KB, 0, P:2 * P]).then_inc(s["xT_copied"], 1)

            def x2_turned(q, bank=2):
                act.wait_ge(s["x2T_psum"], q + 1)
                if q:
                    act.wait_ge(s["gate_psum"], q)
                else:
                    act.wait_ge(s["res_ready"], NT)
                A.copy(x2T[:, 0, :], ps[:, bank, :])
                A.copy(x2T[0:KB, 1, :], ps[0:KB, bank + 1, :]).then_inc(s["x2T_copied"], 1)

            for b in range(NB):
                keep_turned((TB - 1) * NB + b)
                if b == 1:
                    r_hi(0)
                square_res(1, b)
                if b == 2:
                    first_norm_again(2)
            fetch_table(ACT.Gelu)
            for q in range(TB):
                for n in range(q * HT, (q + 1) * HT):
                    if q and n % HT == HT - 1:
                        x2_turned(q - 1)
                    act.wait_ge(s["w1_psum"], n + 1)
                    if q and n % HT == 0:
                        act.wait_ge(s["w2_psum"], q * NB)
                    A.activation(hT[:, n % HT, :], ps[:, 4 + n % 2, :], ACT.Gelu).then_inc(s["gelu_done"], 1)
                    if n == 3:
                        first_norm_again(3)
                if q + 1 < TB:
                    r_hi(q + 1)
                if q == 0:
                    for t in range(NB):
                        square_res(2, t)
                    for t in range(NB):
                        square_res(3, t)
                    act.wait_ge(s["ld_e1_even"], 48 * NE // 2)
                    A.copy(e1r[:, NE - 1, 0, :], stg0[:, 0, :])
                    A.copy(e1r[:, NE - 1, 2, :], stg0[:, 1, :]).then_inc(s["e1_last_hi"], 1)
                if q >= 2:
                    bias_hi_again(q - 2)
                if q and q - 1 < NE // 2:
                    bias_hi(q - 1)

            def gelu(j, par):
                act.wait_ge(s["hid_psum"], j + 1)
                A.activation(hid[:, par, :], ps[:, 1 + 2 * par:3 + 2 * par, :].rearrange("p a s -> p (a s)")[:, 0:DF],
                             ACT.Gelu).then_inc(s["hid_ready"], 1)

            def hidden_hi(j, par, first=False):
                act.wait_ge(s["hidT_psum"], j + 1)
                if not first:
                    act.wait_ge(s["y2_psum"], j - 1)
                A.copy(hidT[:, par, 0, :], ps[:, 5:7, :].rearrange("p a s -> p (a s)")[:, 0:DF]
                       ).then_inc(s["hidT_hi"], 1)

            def step(j, par, first=False):
                turn(j + 3, 1 - par)
                hidden_hi(j + 1, 1 - par, first)
                gelu(j + 2, par)

            turn(0, 0)
            turn(1, 1)
            act.wait_ge(s["h1_done"], NT)
            gelu(0, 0)
            turn(2, 0)
            gelu(1, 1)
            x2_turned(TB - 1, 5)
            hidden_hi(0, 0, True)
            for j in range(PEELED):
                step(j, j % 2, j == 0)
            with act.Fori(PEELED // 2, (SLOTS - 3) // 2) as i:
                for par in range(2):
                    step(i * 2 + par, par)
            hidden_hi(SLOTS - 2, 1)
            gelu(SLOTS - 1, 0)
            hidden_hi(SLOTS - 1, 0)

        @block.vector
        def _(dve):
            V = nc.vector
            n = [0]

            def link(ins):
                n[0] += 1
                ins.then_inc(s["dve_seq"], 1)
                dve.wait_ge(s["dve_seq"], n[0])

            V.memset(tab[:], 0.0).then_inc(s["tab_zero"], 1)
            V.memset(rawA[:, DTC + 1:DTC + 2], 0.0)
            V.memset(rawB[:, DTC + 1:DTC + 2], 0.0)
            V.memset(scanned[:, :, 0:1], 0.0)
            V.memset(zeros[:], 0.0)
            dve.wait_ge(s["count_made"], 1)
            V.tensor_copy(count[:], count_i[:]).then_inc(s["count_copied"], 1)
            dve.wait_ge(s["ld_x"], 16)
            dve.wait_ge(s["count_copied"], 1)
            link(V.tensor_copy(newl[:, 1, :], tok_i[:]))
            link(V.tensor_scalar(newl[:, 0, :], newl[:, 1, :], float(NEWLINE), None, ALU.is_equal))
            link(V.tensor_tensor(newl[:, 1, :], newl[:, 0, :], count[0:NB, :], ALU.mult))
            V.tensor_tensor_scan(scanned[:, 0, 1:S + 1], newl[:, 0, :], zeros[:], 0.0, ALU.add, ALU.add)
            link(V.tensor_tensor_scan(scanned[:, 1, 1:S + 1], newl[:, 1, :], zeros[:], 0.0, ALU.max, ALU.max))
            V.tensor_scalar(rc[:, 0, :], scanned[:, 0, 0:S], float(NROW - 1), None, ALU.min)
            link(V.scalar_tensor_tensor(newl[:, 0, :], count[0:NB, :], 1.0, scanned[:, 1, 0:S],
                                        ALU.subtract, ALU.subtract))
            V.tensor_scalar(rc[:, 1, :], newl[:, 0, :], float(NCOL - 1), None, ALU.min).then_inc(s["tokpos_ready"], 1)
            dve.wait_ge(s["ld_tab"], 48)
            link(V.tensor_copy(tabs[:, 0], tab[:]))
            link(V.tensor_tensor(tab[:], tab[:], tabs[:, 0], ALU.subtract))
            link(V.tensor_copy(tabs[:, 1], tab[:]))
            V.tensor_tensor(tabs[:, 2], tab[:], tabs[:, 1], ALU.subtract).then_inc(s["tabs_ready"], 1)
            dve.wait_ge(s["consts"], 1)

            def one_hot(b):
                q = b % 2
                dve.wait_ge(s["bcb_ready"], b + 1)
                if b >= 2:
                    dve.wait_ge(s["h0_ready"], 2 * (b - 1))
                V.tensor_scalar(onehot[:, q, 0, :], bcb[:, q, 0, :], part[:, 0:1], None, ALU.is_equal)
                V.tensor_scalar(onehot[:, q, 1, :], bcb[:, q, 1, :], part[:, 0:1], None, ALU.is_equal)
                V.tensor_scalar(onehot[:, q, 2, :], bcb[:, q, 1, :], part[:, 1:2], None, ALU.is_equal
                                ).then_inc(s["onehot_ready"], 1)

            def norm_stats(src, b, dst):
                for t in range(TB):
                    last = V.bn_stats(stats[:, t, :], src[:, b * TB + t, :])
                link(last)
                for t in range(TB):
                    last = V.bn_aggr(dst[:, b * TB + t, :], stats[:, t, :])
                link(last)

            def first_stats(b):
                dve.wait_ge(s["h0_copied"], 2 * b + 2)
                norm_stats(h0, b, mv)
                v = mv[:, b * TB:(b + 1) * TB, 1]
                V.tensor_scalar(var2[:, b, 0, :], v, EPS, None, ALU.add)
                V.tensor_scalar(var2[:, b, 1, :], v, 1.0 + EPS, EPS * EPS, ALU.mult, ALU.add
                                ).then_inc(s["var_ready"], 1)

            def first_norm():
                dve.wait_ge(s["rstd_ready"], 1)
                for t in range(TB):
                    last = V.tensor_scalar(u[:, 0, t, :], h0[:, t, :], mv[:, t, 0:1], rstd2[:, 0, 1, t:t + 1],
                                           ALU.subtract, ALU.mult)
                last.then_inc(s["first_u_ready"], 1)

            def negative_mean(b):
                dve.wait_ge(s["rstd_ready"], b + 1)
                V.scalar_tensor_tensor(nmr[:, b * TB:(b + 1) * TB], mv[:, b * TB:(b + 1) * TB, 0], -1.0,
                                       rstd2[:, b, 0, :], ALU.mult, ALU.mult).then_inc(s["nmr_ready"], 1)

            def u_lo(b):
                q = b % 2
                dve.wait_ge(s["uT_copied"], b + 1)
                V.tensor_tensor(uT[:, q, 1, :], ps[:, 6, :], uT[:, q, 0, :].bitcast(F32), ALU.subtract)
                V.tensor_tensor(uT[KB:P, q, 2, :], ps[0:KB, 7, :], uT[0:KB, q, 2, :].bitcast(F32), ALU.subtract
                                ).then_inc(s["uT_split"], 1)

            def conv(n):
                dve.wait_ge(s["tap_ready"], n + 1)
                for k in range(TAPS - 2, -1, -1):
                    d = TAPS - 1 - k
                    ins = V.scalar_tensor_tensor(acc[:, n % 3, d:S], ps[:, n % 3, 0:S - d],
                                                 convw[:, n % NCT, k:k + 1], acc[:, n % 3, d:S], ALU.mult, ALU.add)
                    if k:
                        link(ins)
                ins.then_inc(s["conv_done"], 1)

            def dt_in():
                dve.wait_ge(s["z_copied"], NT)
                dve.wait_ge(s["ld_scal"], 48)
                link(V.tensor_scalar(dtx[:], dtr[:], scal[:, 0:1], None, ALU.add))
                link(V.tensor_scalar(dta[:], dtx[:], -1.0, None, ALU.mult))
                V.tensor_tensor(dta[:], dta[:], dtx[:], ALU.max).then_inc(s["dt_abs"], 1)

            def dt_out():
                dve.wait_ge(s["dt_exp"], 1)
                link(V.scalar_tensor_tensor(dt[:], dtx[:], 0.0, dtl[:], ALU.max, ALU.add))
                link(V.tensor_scalar(decay[:], dt[:], scal[:, 3:4], -1.0, ALU.mult, ALU.mult))
                link(V.tensor_copy(decayr[:, 0, :], decay[:]))
                link(V.tensor_tensor(decayr[:, 1, :], decay[:], decayr[:, 0, :].bitcast(F32), ALU.subtract))

            def segments(c):
                if c:
                    dve.wait_ge(s["seg_psum"], 2 * c)
                else:
                    dve.wait_ge(s["uT_psum"], NB)
                for b in range(NB):
                    m = b * TB + c
                    for k in range(2):
                        last = V.tensor_scalar(Av[:, k, b, :], upto[:, 0, :], decayr[:, k, m:m + 1].bitcast(F32), None,
                                               ALU.mult)
                last.then_inc(s["av_ready"], 1)

            one_hot(0)
            one_hot(1)
            dve.wait_ge(s["win_hi"], 1)
            V.scalar_tensor_tensor(winr[:, 1, :], rawA, n1A[:, 0:1], winr[:, 0, :].bitcast(F32), ALU.mult,
                                   ALU.subtract)
            first_stats(0)
            dve.wait_ge(s["win_hi"], 2)
            V.scalar_tensor_tensor(winr[0:KB, 3, :], rawB[0:KB, :], n1B[0:KB, 0:1], winr[0:KB, 2, :].bitcast(F32),
                                   ALU.mult, ALU.subtract).then_inc(s["win_split"], 1)
            one_hot(2)
            first_norm()
            one_hot(3)
            first_stats(1)
            u_lo(0)
            first_stats(2)
            for b in range(NB):
                for c in range(NCT):
                    conv(b * NCT + c)
                    if b == 0 and c == 0:
                        first_stats(3)
                    if c == 1:
                        negative_mean(b)
                    if c == 2 and b + 1 < NB:
                        u_lo(b + 1)
                    if b == NB - 1 and c == 1:
                        dt_in()
            dt_out()
            segments(0)
            dtg = dt[:].rearrange("p (b c) -> p b c", b=NB)
            CTg = CT.rearrange("p (b c t) -> p b c t", b=NB, c=TB)
            dve.wait_ge(s["silu_done"], NB * NCT)

            def prepare_decays(c):
                q = c % 2
                dve.wait_ge(s["e_ready"], c + 1)
                if 0 < c < TB - 1:
                    V.tensor_copy(eL[:, q, :], E2[q][:, :, P - 1])
                V.tensor_tensor(wB[:, q, :], E1[:, :, P - 1], dtg[:, :, c], ALU.mult)
                mask = V.tensor_tensor(LM, E1, upto[:].to_broadcast([P, NB, P]), ALU.mult)
                if c == 0:
                    mask.then_inc(s["ce_ready"], 1)
                    dve.wait_ge(s["ce_ready"], 1)
                    return
                if c >= 2:
                    dve.wait_ge(s["y_psum"], (c - 1) * NB)
                link(mask)
                V.tensor_tensor(CE[q], CTg[:, :, c, :], E2[q], ALU.mult).then_inc(s["ce_ready"], 1)

            def prepare_mask(c):
                dve.wait_ge(s["g_psum"], c + 1)
                dve.wait_ge(s["xtok_psum"], NT)
                dve.wait_ge(s["ddiag_ready"], 1)
                if c >= 2:
                    dve.wait_ge(s["y_psum"], (c - 1) * NB)
                for b in range(NB):
                    m = b * TB + c
                    last = V.scalar_tensor_tensor(MT[c % 2][:, b, :], ps[:, 2, b * P:(b + 1) * P], dt[:, m:m + 1],
                                                  LM[:, b, :], ALU.mult, ALU.mult)
                link(last)
                V.tensor_tensor(MT[c % 2], MT[c % 2], d_diag[:].to_broadcast([P, NB, P]), ALU.add
                                ).then_inc(s["mt_ready"], 1)

            def prepare_state(c):
                q = c % 2
                if c >= TB - 1:
                    return
                if c >= 2:
                    dve.wait_ge(s["st_psum"], (c - 1) * NB)
                dve.wait_ge(s["xtok_copied"], NT - TB if c == 0 else NT - 1)
                dve.wait_ge(s["xtok_first"], 1)
                for b in range(NB):
                    last = V.tensor_scalar(Bw[q][:, b, :], xB_tile(b * TB + c)[:, DI:S], wB[:, q, b:b + 1], None, ALU.mult)
                last.then_inc(s["bw_ready"], 1)

            def gate_and_state(c, b):
                m = b * TB + c
                k = c * NB + b
                dve.wait_ge(s["y_psum"], k + 1)
                V.tensor_tensor(zs[:, m, :], ps[:, 3 + b % 2, 0:DI], zs[:, m, :], ALU.mult
                                ).then_inc(s["gated"], 1)
                if c == TB - 1:
                    return
                dve.wait_ge(s["st_psum"], k + 1)
                if c == 0:
                    V.tensor_copy(state[:, b, :], ps[:, 5 + b % 2, 0:DI]).then_inc(s["st_done"], 1)
                else:
                    V.scalar_tensor_tensor(state[:, b, :], state[:, b, :], eL[:, c % 2, b:b + 1],
                                           ps[:, 5 + b % 2, 0:DI], ALU.mult, ALU.add).then_inc(s["st_done"], 1)

            def gate_factors(c):
                dve.wait_ge(s["ssq_done"], (c + 1) * NB)
                v = lambda t: t[:].rearrange("p (b c) -> p b c", b=NB)[:, :, c]
                V.tensor_scalar(v(ssq_e), v(ssq), 1.0 / DI, EPS, ALU.mult, ALU.add).then_inc(s["ssqe_ready"], 1)

            def residual(q, t):
                r, m = q * NB + t, t * TB + q
                dve.wait_ge(s["x1_ready"], q + 1)
                dve.wait_ge(s["rr_ready"], q + 1)
                dve.wait_ge(s["out_psum"], r + 1)
                V.scalar_tensor_tensor(res[:, q % 2, t, :], ps[:, r % 2, 0:D], rr[:, m:m + 1],
                                       x1[q][:, t, :], ALU.mult, ALU.add).then_inc(s["res_ready"], 1)

            def res_stats(q):
                dve.wait_ge(s["ssq2_done"], (q + 1) * NB)
                w = slice(q * NB, (q + 1) * NB)
                V.tensor_scalar(ssq2e[:, w], ssq2[:, w], 1.0 / D, EPS, ALU.mult, ALU.add
                                ).then_inc(s["ssq2e_ready"], 1)

            def res_scaled(q):
                dve.wait_ge(s["rn_ready"], q + 1)
                if q >= 2:
                    dve.wait_ge(s["rT_psum"], q - 1)
                else:
                    dve.wait_ge(s["seg_psum"], 2 * TB)
                for t in range(NB):
                    last = V.tensor_scalar(resn[:, q % 2, t, :], res[:, q % 2, t, :],
                                           rn[:, q * NB + t:q * NB + t + 1], None, ALU.mult)
                last.then_inc(s["resn_ready"], 1)

            def r_lo(b):
                dve.wait_ge(s["rT_copied"], b + 1)
                V.tensor_tensor(rT[:, 1, :], ps[:, 2, :], rT[:, 0, :].bitcast(F32), ALU.subtract)
                V.tensor_tensor(rT[KB:P, 2, :], ps[0:KB, 3, :], rT[0:KB, 2, :].bitcast(F32), ALU.subtract
                                ).then_inc(s["rT_split"], 1)

            def add_mlp(r):
                q, t = divmod(r, NB)
                dve.wait_ge(s["w2_psum"], r + 1)
                V.tensor_tensor(row[:, r, D:2 * D], ps[:, 6 + r % 2, 0:D], h0[:, t * TB + q, :], ALU.add
                                ).then_inc(s["h1_done"], 1)

            def tile_stats(r):
                dve.wait_ge(s["h1_done"], r + 1)
                return V.bn_stats(stats[:, r % NB, :], row[:, r, D:2 * D])

            def second_stats(q):
                w = slice(q * NB, (q + 1) * NB)
                for r in range(q * NB, (q + 1) * NB):
                    last = V.bn_aggr(mv2[:, r, :], stats[:, r % NB, :])
                link(last)
                V.tensor_scalar(var_e[:, w], mv2[:, w, 1], EPS, None, ALU.add).then_inc(s["var2_ready"], 1)
                V.memset(row[:, w, 2 * D + 1:ROW], 0.0)
                for t in range(NB):
                    V.tensor_scalar(row[:, q * NB + t, 2 * D:2 * D + 1], part[:, 0:1], float((t * TB + q) * P), None,
                                    ALU.add)

            def second_norm(q):
                dve.wait_ge(s["r2_ready"], q + 1)
                for r in range(q * NB, (q + 1) * NB):
                    last = V.tensor_scalar(row[:, r, 0:D], row[:, r, D:2 * D], mv2[:, r, 0:1], r2[:, r:r + 1],
                                           ALU.subtract, ALU.mult)
                last.then_inc(s["x2_ready"], 1)

            def choose(q):
                r0 = q * NB
                w = slice(r0, r0 + NB)
                dve.wait_ge(s["gate_psum"], q + 1)
                o = ps[:, gate_bank(q)[0], 0:NB * NE].rearrange("p (t e) -> p t e", e=NE)
                V.tensor_tensor(logit[:, w, :], o, bg[:].to_broadcast([P, NB, NE]), ALU.add
                                ).then_inc(s["logit_ready"], 1)
                dve.wait_ge(s["logit_ready"], q + 1)
                link(V.tensor_reduce(top[:, :, 0], logit[:, w, :], AX.X, ALU.max))
                link(V.tensor_tensor(best[:], logit[:, w, :], top[:].to_broadcast([P, NB, NE]), ALU.is_equal))
                link(V.tensor_tensor(best[:], best[:], firsts[:].to_broadcast([P, NB, NE]), ALU.mult))
                link(V.tensor_reduce(top[:, :, 0], best[:], AX.X, ALU.max))
                link(V.tensor_tensor(F[:, w, :], best[:], top[:].to_broadcast([P, NB, NE]), ALU.is_equal))
                for r in range(r0, r0 + NB):
                    last = V.tensor_tensor(G[:, r + 1, :], G[:, r, :], F[:, r, :], ALU.add)
                    if r < r0 + NB - 1:
                        link(last)
                last.then_inc(s["f_ready"], 1)
                dve.wait_ge(s["f_ready"], q + 1)

            def read_ranks(q):
                dve.wait_ge(s["rank_psum"], q + 1)
                o = ps[:, gate_bank(q)[1], 0:NB * NE].rearrange("p (t e) -> p t e", e=NE)
                V.tensor_tensor(spot[:], o, region[:].to_broadcast([P, NB, NE]), ALU.add)
                V.tensor_copy(cnt[:, :, 0], ps[:, gate_bank(q)[1], COUNT0:COUNT0 + NE]).then_inc(s["ranks_read"], 1)

            def place(q):
                w = slice(q * NB, (q + 1) * NB)
                dve.wait_ge(s["ranks_read"], q + 1)
                link(V.tensor_tensor(spot[:], spot[:], F[:, w, :], ALU.mult))
                link(V.tensor_reduce(pos[:, w], spot[:], AX.X, ALU.add))
                V.tensor_copy(posi[:, w], pos[:, w]).then_inc(s["pos_ready"], 1)

            def first_slots(k):
                link(V.tensor_scalar(lim[:], cnt[:], float(1 - P if k < 2 else 0), None, ALU.add))
                link(V.tensor_tensor(begun[:], starts[:].to_broadcast([P, NE, NT]), lim[:].to_broadcast([P, NE, NT]),
                                     ALU.is_lt))
                link(V.tensor_reduce(need[:], begun[:], AX.X, ALU.add))
                link(V.tensor_tensor(need[:], need[:], done[:], ALU.subtract))
                for e in range(NE):
                    link(V.tensor_tensor(base[:, e + 1:e + 2], base[:, e:e + 1], need[:, e:e + 1], ALU.add))

            def slot_table(k):
                link(V.tensor_tensor(off[:], done[:], base[:, 0:NE], ALU.subtract))
                link(V.scalar_tensor_tensor(off[:], off[:], float(P), region[:, 0, :], ALU.mult, ALU.add))
                if k < 2:
                    link(V.tensor_scalar(take[:], base[:, 0:NE], -1.0, float(WAVES[k]), ALU.mult, ALU.add))
                    link(V.scalar_tensor_tensor(take[:], take[:], 0.0, need[:], ALU.max, ALU.min))
                    V.tensor_tensor(done[:], done[:], take[:], ALU.add)
                else:
                    link(V.tensor_tensor(padf[:], cnt[:, :, 0], region[:, 0, :], ALU.add))
                    V.tensor_copy(padi[:], padf[:])
                V.tensor_tensor(doff[:, :, 0], off[:, 1:NE], off[:, 0:NE - 1], ALU.subtract)
                for e in range(NE):
                    last = V.tensor_scalar(begins[:, e, :], slotno[:, 0, :], base[:, e + 1:e + 2], None, ALU.is_ge)
                link(last)
                V.tensor_reduce(eidf[:], begins[:, 0:NE - 1, :].rearrange("p e j -> p j e"), AX.X, ALU.add)
                link(V.tensor_tensor(terms[:], begins[:, 0:NE - 1, :], doff[:].to_broadcast([P, NE - 1, WAVES[2]]),
                                     ALU.mult))
                link(V.tensor_reduce(addrf[:], terms[:].rearrange("p e j -> p j e"), AX.X, ALU.add))
                link(V.scalar_tensor_tensor(addrf[:], slotno[:, 0, :], float(P), addrf[:], ALU.mult, ALU.add))
                link(V.tensor_scalar(addrf[:], addrf[:], off[:, 0:1], None, ALU.add))
                if k == 2:
                    link(V.tensor_scalar(toward[:], addrf[:], -1.0, float(DUMMY), ALU.mult, ALU.add))
                    link(V.tensor_tensor(toward[:], toward[:], begins[:, NE - 1, :], ALU.mult))
                    link(V.tensor_tensor(addrf[:], addrf[:], toward[:], ALU.add))
                V.tensor_copy(eid[:, FIRST[k]:FIRST[k] + WAVES[k]], eidf[:, 0:WAVES[k]])
                V.tensor_copy(addr[:, FIRST[k]:FIRST[k] + WAVES[k]], addrf[:, 0:WAVES[k]]
                              ).then_inc(s["table_ready"], 1)

            def lo_rows(j, par):
                dve.wait_ge(s["xT_copied"], j + 1)
                V.tensor_tensor(xTr[:, par, 1, :], ps[:, 0, 0:P], xTr[:, par, 0, :].bitcast(F32), ALU.subtract)
                V.tensor_tensor(xTr[KB:P, par, 2, :], ps[0:KB, 0, P:2 * P], xTr[0:KB, par, 2, :].bitcast(F32),
                                ALU.subtract).then_inc(s["xT_split"], 1)

            def bias_lo(i):
                dve.wait_ge(s["b1_hi"], i + 1)
                b1part = e1r[KB:KB + 2, 2 * i:2 * i + 2, 3, :]
                V.tensor_tensor(b1part, b1raw[KB:KB + 2], b1part.bitcast(F32), ALU.subtract).then_inc(s["b1_lo"], 1)
                if i == 0:
                    dve.wait_ge(s["b2_hi"], 1)
                    V.tensor_tensor(e2b[0:2, :], b2raw[0:2, :], e2b[0:2, :].bitcast(F32), ALU.subtract
                                    ).then_inc(s["b2_lo"], 1)

            prepare_decays(0)
            prepare_mask(0)
            V.tensor_copy(xB_tile(NT - TB), ps[:, 3, :]).then_inc(s["xtok_first"], 1)
            prepare_state(0)
            segments(1)
            for c in range(TB):
                gate_and_state(c, 0)
                if c + 1 < TB:
                    prepare_decays(c + 1)
                gate_and_state(c, 1)
                if c + 1 < TB:
                    prepare_mask(c + 1)
                else:
                    residual(0, 0)
                gate_and_state(c, 2)
                if c + 1 < TB:
                    prepare_state(c + 1)
                else:
                    residual(0, 1)
                if c:
                    gate_factors(c - 1)
                gate_and_state(c, 3)
            residual(0, 2)
            residual(0, 3)
            V.memset(G[:, 0, :], 0.0)
            V.memset(base[:, 0:1], 0.0)
            V.memset(done[:], 0.0)
            dve.wait_ge(s["ld_gate"], 48)
            res_stats(0)
            gate_factors(TB - 1)
            residual(1, 0)
            res_scaled(0)
            residual(1, 1)
            r_lo(0)
            residual(1, 2)
            residual(1, 3)
            res_stats(1)
            for q in range(TB):
                if q + 1 < TB:
                    res_scaled(q + 1)
                if q == 0:
                    for t in range(NB):
                        residual(2, t)
                if q:
                    second_norm(q - 1)
                    if q == TB - 1:
                        slot_table(0)
                    if q == 2:
                        bias_lo(0)
                    choose(q - 1)
                    if q == 3:
                        bias_lo(1)
                if q == 0:
                    res_stats(2)
                if q == 0:
                    for t in range(NB):
                        residual(3, t)
                if q + 1 < TB:
                    r_lo(q + 1)
                if q == 0:
                    res_stats(3)
                for t in range(NB):
                    if q and t == 1:
                        read_ranks(q - 1)
                        place(q - 1)
                    if q == 0 and t == 3:
                        dve.wait_ge(s["e1_last_hi"], 1)
                        V.tensor_tensor(e1r[:, NE - 1, 1, :], stg0[:, 0, :], e1r[:, NE - 1, 0, :].bitcast(F32),
                                        ALU.subtract)
                        V.tensor_tensor(e1r[0:KB, NE - 1, 3, :], stg0[0:KB, 1, :],
                                        e1r[0:KB, NE - 1, 2, :].bitcast(F32), ALU.subtract
                                        ).then_inc(s["e1_last_split"], 1)
                    if q == TB - 1 and t == 2:
                        dve.wait_ge(s["w1_psum"], TB * HT)
                        V.memset(xTr[KB:KB + 2, :, 3, :].bitcast(F32), 1.0)
                        lo_rows(0, 0)
                    if q == TB - 1 and t == 3:
                        lo_rows(1, 1)
                    add_mlp(q * NB + t)
                    if t:
                        tile_stats(q * NB + t - 1)
                link(tile_stats(q * NB + NB - 1))
                second_stats(q)
                if q == TB - 2:
                    first_slots(0)
            def hidden_lo(j, par):
                dve.wait_ge(s["hidT_hi"], j + 1)
                V.tensor_tensor(hidT[:, par, 1, :], ps[:, 5:7, :].rearrange("p a s -> p (a s)")[:, 0:DF],
                                hidT[:, par, 0, :].bitcast(F32), ALU.subtract).then_inc(s["hidT_split"], 1)

            def add_h1(j, h, par, first=False):
                dve.wait_ge(h1_loaded[par], (h + 1) * 16)
                if not first:
                    dve.wait_ge(stored[par], h * 16)
                V.tensor_copy(ids[:, par:par + 1], slot_h[:, par, D:D + 1]).then_inc(s["ids_ready"], 1)
                dve.wait_ge(s["y2_psum"], j + 1)
                V.tensor_tensor(yo[:, par, :], ps[:, 7, D:2 * D], slot_h[:, par, 0:D], ALU.add
                                ).then_inc(s["y_part"], 1)
                dve.wait_ge(s["y_part"], j + 1)
                V.tensor_tensor(yo[:, par, :], ps[:, 7, 0:D], yo[:, par, :], ALU.add).then_inc(s["yo_ready"], 1)

            second_norm(TB - 1)
            lo_rows(2, 0)
            first_slots(1)
            slot_table(1)
            choose(TB - 1)
            hidden_lo(0, 0)
            for j in range(PEELED):
                lo_rows(j + 3, (j + 1) % 2)
                if j == 0:
                    read_ranks(TB - 1)
                hidden_lo(j + 1, (j + 1) % 2)
                if j == 0:
                    place(TB - 1)
                add_h1(j, j // 2, j % 2, j < 2)
                if j == 0:
                    first_slots(2)
                if j == 1:
                    slot_table(2)
            with dve.Fori(PEELED // 2, (SLOTS - 3) // 2) as i:
                for par in range(2):
                    j = i * 2 + par
                    lo_rows(j + 3, 1 - par)
                    hidden_lo(j + 1, 1 - par)
                    add_h1(j, i, par)
            for j in range(SLOTS - 3, SLOTS):
                if j + 1 < SLOTS:
                    hidden_lo(j + 1, (j + 1) % 2)
                add_h1(j, j // 2, j % 2)

        @block.tensor
        def _(pe):
            T = nc.tensor

            def mm(o, l, r, start=True, stop=True):
                return T.matmul(o, l, r, start=start, stop=stop)

            def split_product(o, l, r):
                for n, (x, y) in enumerate(((0, 0), (0, 1), (1, 0), (2, 2), (3, 2))):
                    if len(l) < len(r):
                        x, y = y, x
                    last = mm(o, l[x], r[y], start=(n == 0), stop=(n == 4))
                return last

            pe.wait_ge(s["consts"], 1)
            pe.wait_ge(s["tokpos_ready"], 1)

            def bc_index(b):
                q = b % 2
                if b >= 2:
                    pe.wait_ge(s["bcb_ready"], b - 1)
                mm(ps[:, 2 * q, :], pick[:, b, :], rc[:, 0, :])
                mm(ps[:, 2 * q + 1, :], pick[:, b, :], rc[:, 1, :]).then_inc(s["idx_bc_ready"], 1)

            def look_up(b):
                q = b % 2
                pe.wait_ge(s["onehot_ready"], b + 1)
                for p in range(2):
                    n = 2 * b + p
                    if n >= 2:
                        pe.wait_ge(s["h0_copied"], n - 1)
                    for t in range(2):
                        w = slice((2 * p + t) * P, (2 * p + t + 1) * P)
                        o = ps[:, 4 + n % 2, t * D:(t + 1) * D]
                        for k in range(3):
                            mm(o[:, 0:DH], onehot[:, q, 0, w], tabs[:, k, 0, :], start=(k == 0), stop=(k == 2))
                        for i, (k, c) in enumerate((k, c) for k in range(3) for c in (1, 2)):
                            last = mm(o[:, DH:D], onehot[:, q, c, w], tabs[:, k, c, :], start=(i == 0), stop=(i == 5))
                    last.then_inc(s["h0_ready"], 1)

            bc_index(0)
            bc_index(1)
            pe.wait_ge(s["tabs_ready"], 1)
            for b in range(NB - 1):
                look_up(b)
                if b + 2 < NB:
                    bc_index(b + 2)

            def turn_tiles(src, bankA, bankB):
                for t in range(TB):
                    T.transpose(ps[:, bankA, t * P:(t + 1) * P], src(t)[:, 0:KA], ident[:])
                    last = T.transpose(ps[0:KB, bankB, t * P:(t + 1) * P], src(t)[:, KA:D], ident[:])
                return last

            def turn_u(b):
                pe.wait_ge(s["u_ready" if b else "first_u_ready"], max(b, 1))
                if b:
                    pe.wait_ge(s["uT_split"], b)
                turn_tiles(lambda t: u[:, b % 2, t, :], 6, 7).then_inc(s["uT_psum"], 1)

            def xtok(b, t):
                m = b * TB + t
                bank = 3 + t if b == NB - 1 else 5
                pe.wait_ge(s["silu_done"], b * NCT + CT_X + 1)
                if m:
                    pe.wait_ge(s["xtok_copied"], min(m, NT - TB))
                for c in range(CT_X):
                    T.transpose(ps[:, bank, c * P:(c + 1) * P], xch[:, b % 2, c, t * P:(t + 1) * P], ident[:])
                T.transpose(ps[:, bank, DI:S], BT[:, m * P:(m + 1) * P], ident[:]).then_inc(s["xtok_psum"], 1)

            def project_xbc(b, c):
                n = b * NCT + c
                if n >= 3:
                    pe.wait_ge(s["conv_done"], n - 2)
                w = slice(XBC0 + c * P, XBC0 + (c + 1) * P)
                split_product(ps[:, n % 3, :], [winr[:, k, w] for k in range(4)], [uT[:, b % 2, k, :] for k in range(3)]
                              ).then_inc(s["xbc_psum"], 1)

            def project_z(b, t):
                m = b * TB + t
                if m >= 2:
                    pe.wait_ge(s["z_copied"], m - 1)
                w = slice(t * P, (t + 1) * P)
                split_product(ps[:, 3 + m % 2, 0:XBC0], [uT[:, b % 2, k, w] for k in range(3)],
                              [winr[:, k, 0:XBC0] for k in range(4)]).then_inc(s["z_psum"], 1)

            pe.wait_ge(s["consts"], 2)
            turn_u(0)
            look_up(NB - 1)
            pe.wait_ge(s["win_split"], 1)
            pe.wait_ge(s["win_zero"], 1)
            pe.wait_ge(s["h0_copied"], 2 * NB)
            for b in range(NB):
                pe.wait_ge(s["uT_split"], b + 1)
                for c in range(NCT):
                    project_xbc(b, c)
                    for t in z_steps(b, c):
                        project_z(b, t)
                    if b and c >= NCT - TB:
                        xtok(b - 1, c - (NCT - TB))
                    if c == 1 and b + 1 < NB:
                        turn_u(b + 1)

            def seg(c):
                pe.wait_ge(s["av_ready"], c + 1)
                if c:
                    pe.wait_ge(s["e_ready"], c)
                for bank, w in ((0, afterr[:]), (1, ones[:].bitcast(F32R))):
                    mm(ps[:, bank, :], w, Av[:, 0].rearrange("p b t -> p (b t)"), stop=False)
                    mm(ps[:, bank, :], w, Av[:, 1].rearrange("p b t -> p (b t)"), start=False
                       ).then_inc(s["seg_psum"], 1)

            def bc(c):
                if c:
                    pe.wait_ge(s["mt_ready"], c)
                for b in range(NB):
                    w = slice((b * TB + c) * P, (b * TB + c + 1) * P)
                    last = mm(ps[:, 2, b * P:(b + 1) * P], BT[:, w], CT[:, w])
                last.then_inc(s["g_psum"], 1)

            def turn_gated(k):
                c, b = divmod(k, NB)
                pe.wait_ge(s["ssq_done"], k + 1)
                if k:
                    pe.wait_ge(s["gT_copied"], k)
                for i in range(CT_X):
                    last = T.transpose(ps[:, 7, i * P:(i + 1) * P], zs[:, b * TB + c, i * P:(i + 1) * P], ident[:])
                last.then_inc(s["gT_psum"], 1)

            pe.wait_ge(s["conv_done"], NB * NCT)
            seg(0)
            pe.wait_ge(s["silu_done"], NB * NCT)
            bc(0)
            pe.wait_ge(s["z_copied"], NT)
            for t in range(TB):
                xtok(NB - 1, t)
            pe.wait_ge(s["xtok_first"], 1)
            pe.wait_ge(s["xtok_copied"], NT - 1)
            pe.wait_ge(s["z_copied"], NT)

            def out_proj(q, t):
                r, m = q * NB + t, t * TB + q
                pe.wait_ge(s["gT_copied"], r + 1)
                if r >= 2:
                    pe.wait_ge(s["res_ready"], r - 1)
                for c in range(CT_X):
                    last = mm(ps[:, r % 2, 0:D], zs[:, m, c * P:(c + 1) * P], wout[:, c, :],
                              start=(c == 0), stop=(c == CT_X - 1))
                last.then_inc(s["out_psum"], 1)

            def turn_res(q):
                pe.wait_ge(s["resn_ready"], q + 1)
                if q:
                    pe.wait_ge(s["rT_split"], q)
                else:
                    pe.wait_ge(s["gated"], NT - 1)
                if q >= 2:
                    pe.wait_ge(s["x2T_copied"], q - 1)
                turn_tiles(lambda t: resn[:, q % 2, t, :], 2, 3).then_inc(s["rT_psum"], 1)

            def mlp_up(q):
                pe.wait_ge(s["rT_split"], q + 1)
                if q == 0:
                    pe.wait_ge(s["gated"], NT)
                    pe.wait_ge(s["gT_copied"], NT)
                for c in range(HT):
                    if q and c == HT - 1:
                        turn_x2(q - 1)
                    n = q * HT + c
                    if n >= 2:
                        pe.wait_ge(s["gelu_done"], n - 1)
                    w = slice(c * P, (c + 1) * P)
                    split_product(ps[:, 4 + n % 2, :], [m1r[:, k, w] for k in range(4)], [rT[:, k, :] for k in range(3)]
                                  ).then_inc(s["w1_psum"], 1)
                if q:
                    gate(q - 1)

            def turn(h, par, first=False):
                pe.wait_ge(slot_loaded[par], (h + 1) * 16)
                if not first:
                    pe.wait_ge(s["xT_split"], h * 2 + par)
                T.transpose(ps[:, 0, 0:P], slot_x[:, par, 0:KA], ident[:])
                T.transpose(ps[0:KB, 0, P:2 * P], slot_x[:, par, KA:D], ident[:]).then_inc(s["xT_psum"], 1)

            def mlp_down(q):
                pe.wait_ge(s["gelu_done"], (q + 1) * HT)
                for t in range(NB):
                    if q and t == 1:
                        ranks(q - 1)
                    if q == TB - 1 and t >= 2:
                        turn(0, t - 2, t == 2)
                    r = q * NB + t
                    if r >= 2:
                        pe.wait_ge(s["h1_done"], r - 1)
                    for c in range(HT):
                        last = mm(ps[:, 6 + r % 2, 0:D], hT[:, c, t * P:(t + 1) * P], m2[:, c, :],
                                  start=(c == 0), stop=(c == HT - 1))
                    last.then_inc(s["w2_psum"], 1)

            def turn_x2(q, bank=2):
                pe.wait_ge(s["x2_ready"], q + 1)
                pe.wait_ge(s["rT_split"], min(TB, q + 2))
                turn_tiles(lambda t: row[:, q * NB + t, 0:D], bank, bank + 1).then_inc(s["x2T_psum"], 1)

            def gate(q):
                pe.wait_ge(s["x2T_copied"], q + 1)
                if q:
                    pe.wait_ge(s["logit_ready"], q)
                else:
                    pe.wait_ge(s["res_ready"], NT)
                for t in range(NB):
                    o = ps[:, gate_bank(q)[0], NE * t:NE * (t + 1)]
                    w = slice(t * P, (t + 1) * P)
                    mm(o, x2T[:, 0, w], wgA[:], stop=False)
                    last = mm(o, x2T[0:KB, 1, w], wgB[:], start=False)
                last.then_inc(s["gate_psum"], 1)

            def ranks(q):
                pe.wait_ge(s["f_ready"], q + 1)
                w = slice(q * NB, (q + 1) * NB)
                if q:
                    pe.wait_ge(s["ranks_read"], q)
                o = ps[:, gate_bank(q)[1], 0:NB * NE]
                mm(ps[:, gate_bank(q)[1], COUNT0:COUNT0 + NE], ones[:], G[:, (q + 1) * NB, :])
                mm(o, before[:], F[:, w, :].rearrange("p t e -> p (t e)"), stop=False)
                mm(o, ones[:], G[:, w, :].rearrange("p t e -> p (t e)"), start=False).then_inc(s["rank_psum"], 1)

            for c in range(TB):
                pe.wait_ge(s["mt_ready"], c + 1)
                pe.wait_ge(s["ce_ready"], c + 1)
                if c < TB - 1:
                    bc(c + 1)
                for b in range(NB):
                    m = b * TB + c
                    k = c * NB + b
                    if k >= 2:
                        pe.wait_ge(s["gated"], k - 1)
                    last = mm(ps[:, 3 + b % 2, 0:DI], MT[c % 2][:, b, :], xB_tile(m)[:, 0:DI], stop=(c == 0))
                    if c:
                        pe.wait_ge(s["st_done"], NB * (c - 1) + b + 1)
                        last = mm(ps[:, 3 + b % 2, 0:DI], CE[c % 2][:, b, :], state[:, b, :], start=False)
                    last.then_inc(s["y_psum"], 1)
                    if c < TB - 1:
                        pe.wait_ge(s["bw_ready"], c + 1)
                        if k >= 2:
                            pe.wait_ge(s["st_done"], k - 1)
                        mm(ps[:, 5 + b % 2, 0:DI], Bw[c % 2][:, b, :], xB_tile(m)[:, 0:DI]).then_inc(s["st_psum"], 1)
                    if k == 0:
                        seg(1)
                    if b == (1 if c else 3) and c + 2 < TB:
                        seg(c + 2)
                    if c:
                        turn_gated(k - NB)
                    if c == TB - 1:
                        if b == 0:
                            pe.wait_ge(s["folded_out"], 1)
                        out_proj(0, b)
            for b in range(NB):
                turn_gated((TB - 1) * NB + b)
                if b == 1:
                    turn_res(0)
                out_proj(1, b)
            pe.wait_ge(s["m1_split"], 1)
            pe.wait_ge(s["ld_gate"], 48)
            pe.wait_ge(s["ld_mlp"], 16)
            for q in range(TB):
                mlp_up(q)
                if q + 1 < TB:
                    turn_res(q + 1)
                if q == 0:
                    for t in range(NB):
                        out_proj(2, t)
                    for t in range(NB):
                        out_proj(3, t)
                mlp_down(q)
            pe.wait_ge(s["e2_split"], NE)
            pe.wait_ge(s["b2_split"], 1)
            pe.wait_ge(s["b1_split"], NE // 2)
            pe.wait_ge(s["e1_split"], NE - 1)
            pe.wait_ge(s["e1_last_split"], 1)

            def up(j, par, e):
                pe.wait_ge(s["xT_split"], j + 1)
                for bank, c0, w in ((1 + 2 * par, 0, 512), (2 + 2 * par, 512, DF - 512)):
                    for n, (x, y, k) in enumerate(((0, 0, P), (1, 0, P), (0, 1, P), (2, 2, P), (3, 3, KB + 2))):
                        last = mm(ps[:, bank, 0:w], xTr[0:k, par, x, :],
                                  e1f[0:k, bass.ds(e * (4 * DF) + y * DF + c0, w)], start=(n == 0), stop=(n == 4))
                last.then_inc(s["hid_psum"], 1)

            def turn_hidden(j, par, first=False):
                pe.wait_ge(s["hid_ready"], j + 1)
                if not first:
                    pe.wait_ge(s["hidT_split"], j)
                for c in range(HT):
                    last = T.transpose(ps[:, 5 + c // 4, (c % 4) * P:(c % 4 + 1) * P],
                                       hid[:, par, c * P:(c + 1) * P], ident[:])
                last.then_inc(s["hidT_psum"], 1)

            def down(j, par, e, first=False):
                pe.wait_ge(s["hidT_split"], j + 1)
                if first:
                    pe.wait_ge(s["ranks_read"], TB)
                else:
                    pe.wait_ge(s["yo_ready"], j)
                for c in range(HT):
                    w = slice(c * P, (c + 1) * P)
                    mm(ps[:, 7, 0:2 * D], hidT[:, par, 0, w], e2[:, bass.ds(e * E2W + c * 2 * D, 2 * D)],
                       start=(c == 0), stop=False)
                    mm(ps[:, 7, 0:D], hidT[:, par, 1, w], e2[:, bass.ds(e * E2W + c * 2 * D, D)],
                       start=False, stop=False)
                mm(ps[:, 7, 0:D], ones[:].bitcast(F32R), e2b[:, bass.ds(e * D, D)], start=False
                   ).then_inc(s["y2_psum"], 1)

            def expert(j):
                return pe.value_load(eid[0:1, bass.ds(j, 1)], min_val=0, max_val=NE - 1)

            up(0, 0, expert(0))
            turn(1, 0)
            up(1, 1, expert(1))
            pe.wait_ge(s["h1_done"], NT)
            turn_x2(TB - 1, 5)
            pe.wait_ge(s["hid_ready"], 1)
            up(2, 0, expert(2))
            gate(TB - 1)
            turn_hidden(0, 0, True)
            for j in range(PEELED):
                par = j % 2
                if j + 2 in FIRST:
                    pe.wait_ge(s["table_ready"], FIRST.index(j + 2) + 1)
                if j:
                    up(j + 2, par, expert(j + 2))
                turn((j + 3) // 2, 1 - par)
                if j == 0:
                    ranks(TB - 1)
                turn_hidden(j + 1, 1 - par)
                down(j, par, expert(j), j == 0)
            pe.wait_ge(s["table_ready"], 3)
            with pe.Fori(PEELED // 2, (SLOTS - 3) // 2) as i:
                for par in range(2):
                    j = i * 2 + par
                    up(j + 2, par, expert(j + 2))
                    turn(i + 1 + par, 1 - par)
                    turn_hidden(j + 1, 1 - par)
                    down(j, par, expert(j))
            j = SLOTS - 3
            up(j + 2, 0, expert(j + 2))
            turn_hidden(j + 1, 1)
            down(j, 0, expert(j))
            turn_hidden(j + 2, 0)
            down(j + 1, 1, expert(j + 1))
            down(j + 2, 0, expert(j + 2))


_INS = ["x", "L0_tok_row_emb_W", "L0_tok_col_emb_W", "L0_attn_norm1_w", "L0_attn_in_proj_W", "L0_attn_conv_w",
        "L0_attn_conv_b", "L0_attn_dt_bias", "L0_attn_A_log", "L0_attn_D", "L0_attn_ssm_norm_w",
        "L0_attn_out_proj_W", "L0_attn_norm2_w", "L0_attn_mlp_W1", "L0_attn_mlp_W2", "L0_ffn_Wg", "L0_ffn_bg",
        "L0_ffn_W1", "L0_ffn_b1", "L0_ffn_W2", "L0_ffn_b2"]


def kernel(**inputs):
    import numpy as _np
    import concourse.bacc as _bacc
    from concourse import mybir as _mybir
    from concourse.bass_utils import run_bass_kernel_spmd as _run

    nc = _bacc.Bacc("TRN2", target_bir_lowering=False, num_devices=1)
    arrays, aps = {}, {}
    for name in _INS:
        v = _np.ascontiguousarray(inputs[name])
        arrays[f"in_{name}"] = v
        aps[name] = nc.dram_tensor(f"in_{name}", v.shape, _mybir.dt.from_np(v.dtype), kind="ExternalInput").ap()
    out = nc.dram_tensor("out_h", (NB * S, D), _mybir.dt.from_np(_np.dtype("float32")), kind="ExternalOutput").ap()
    build(nc, aps, out)
    r = _run(nc, [arrays], core_ids=[0])
    return r.results[0]["out_h"].reshape(NB, S, D)
```
